# Optimizing a Trainium2 kernel written in Bass

```python
import numpy as np
import jax
import jax.numpy as jnp

def _softmax(x, axis=-1):
    return jax.nn.softmax(x, axis=axis)

def _gelu(x):
    return jax.nn.gelu(x, approximate=True)

def _silu(x):
    return jax.nn.silu(x)

def _sigmoid(x):
    return jax.nn.sigmoid(x)

def _layernorm(x, axis=-1, eps=1e-05):
    m = jnp.mean(x, axis=axis, keepdims=True)
    v = jnp.var(x, axis=axis, keepdims=True)
    return (x - m) / jnp.sqrt(v + eps)

def _scatter_add(tgt, idx, src, axis=0):
    return tgt.at[idx].add(src)

def _segment_sum(src, seg, n):
    return jax.ops.segment_sum(src, seg, n)
kernel_name = 'mk_adj_ffn_d2_adj_r2_c3387b'

def setup_inputs(seed: int=0):
    np.random.seed(seed)
    _w = jnp.asarray

    def _rec_inputs():
        import jax
        import jax.numpy as jnp
        _gk = jax.random.key(seed)
        x = -0.0005207 + 1.001 * jax.random.normal(jax.random.fold_in(_gk, 1), (1354, 128), jnp.float32)
        _a = jax.random.bernoulli(jax.random.fold_in(_gk, 2), 0.0118168, (1354, 1354))
        _a = jnp.logical_or(_a, jnp.swapaxes(_a, -1, -2))
        _a = jnp.logical_or(_a, jnp.eye(1354, dtype=bool))
        _af = _a.astype(jnp.float32)
        _af = _af * jax.random.uniform(jax.random.fold_in(_gk, 3), (1354, 1354), jnp.float32, 0.05, 2.05)
        adj = _af
        return (x, adj)
    x, adj = _rec_inputs()

    def _L0_gnn_setup():
        import jax, jax.numpy as jnp
        import numpy as np
        N = 4096
        D = 128
        CUTOFF = 1.0
        MU = 1.0
        SIGMA = 0.5

        def sensitivity(r, mu, sigma):
            return jnp.exp(-(1.0 / r - 1.0 / mu) ** 2 / (2.0 * sigma * sigma))
        key = jax.random.key(seed)
        k_z, k_d, k_w = jax.random.split(key, 3)
        z = jax.random.normal(k_z, (N, D), dtype=jnp.float32)
        dist_matrix = jax.random.uniform(k_d, (N, N), dtype=jnp.float32) * 2.0 + 0.05
        W = jax.random.normal(k_w, (D, D), dtype=jnp.float32)
        B = jnp.zeros((D,), dtype=jnp.float32)
        return {'z': z, 'dist_matrix': dist_matrix, 'W': W, 'B': B}
    _L0_gnn_all = _L0_gnn_setup()
    _L0_gnn_in = {k: v for k, v in _L0_gnn_all.items() if k in ('W', 'B')}
    del _L0_gnn_all

    def _L0_ffn_setup():
        import jax, jax.numpy as jnp
        import numpy as np
        D_MODEL = 128
        EXPERT_DIM = 256
        NUM_EXPERTS = 8
        TOP_K = 2
        SEQ_LEN = 1024
        BATCH = 2
        key = jax.random.key(seed)
        ks = jax.random.split(key, 8)
        s = 0.02
        x = jax.random.normal(ks[0], (SEQ_LEN, BATCH, D_MODEL), dtype=jnp.float32)
        Wg = jax.random.normal(ks[1], (D_MODEL, NUM_EXPERTS), dtype=jnp.float32) * s
        bg = jax.random.normal(ks[2], (NUM_EXPERTS,), dtype=jnp.float32) * s
        bias = jnp.zeros((NUM_EXPERTS,), dtype=jnp.float32)
        W1 = jax.random.normal(ks[3], (NUM_EXPERTS, D_MODEL, EXPERT_DIM), dtype=jnp.float32) * s
        b1 = jax.random.normal(ks[4], (NUM_EXPERTS, EXPERT_DIM), dtype=jnp.float32) * s
        W2 = jax.random.normal(ks[5], (NUM_EXPERTS, EXPERT_DIM, D_MODEL), dtype=jnp.float32) * s
        b2 = jax.random.normal(ks[6], (NUM_EXPERTS, D_MODEL), dtype=jnp.float32) * s
        return {'x': x, 'Wg': Wg, 'bg': bg, 'bias': bias, 'W1': W1, 'b1': b1, 'W2': W2, 'b2': b2}
    _L0_ffn_all = _L0_ffn_setup()
    _L0_ffn_in = {k: v for k, v in _L0_ffn_all.items() if k in ('Wg', 'bg', 'bias', 'W1', 'b1', 'W2', 'b2')}
    del _L0_ffn_all

    def _L1_gnn_setup():
        import jax, jax.numpy as jnp
        import numpy as np
        N, H, HEADS = (2048, 128, 3)
        ALPHA = 0.2
        NEG_INF = -9000000000000000.0

        def _sign_adj(key, n, density):
            k1, k2 = jax.random.split(key)
            mask = jax.random.uniform(k1, (n, n)) < density
            sign = jnp.where(jax.random.uniform(k2, (n, n)) < 0.5, -1.0, 1.0)
            adj = jnp.where(mask, sign, 0.0).astype(jnp.float32)
            idx = jnp.arange(n)
            return adj.at[idx, idx].set(1.0)

        def _gru_cell(x, hstate, Wih, Whh, bih, bhh):
            gi = x @ Wih.T + bih
            gh = hstate @ Whh.T + bhh
            ir, iz, inn = jnp.split(gi, 3, axis=1)
            hr, hz, hn = jnp.split(gh, 3, axis=1)
            r = jax.nn.sigmoid(ir + hr)
            z = jax.nn.sigmoid(iz + hz)
            n = jnp.tanh(inn + r * hn)
            return (1.0 - z) * n + z * hstate

        def _gat_head(h, node_adj, edge_adj, W, a):
            hW = h @ W
            hp = (node_adj > 0).astype(hW.dtype) @ hW
            hm = (node_adj < 0).astype(hW.dtype) @ hW
            e_plus = jax.nn.leaky_relu(jnp.concatenate([hp, hm], axis=1) @ a, ALPHA)[:, 0]
            e_minus = jax.nn.leaky_relu(jnp.concatenate([hm, hp], axis=1) @ a, ALPHA)[:, 0]
            att = jnp.where(edge_adj > 0, e_plus[None, :], NEG_INF)
            att = jnp.where(edge_adj < 0, e_minus[None, :], att)
            att = jax.nn.softmax(att, axis=1)
            return att * edge_adj @ hW
        key = jax.random.key(seed)
        ks = jax.random.split(key, 16)
        std = 0.01
        gain = 1.414
        return {'h': jax.random.normal(ks[0], (N, H), jnp.float32), 'node_adj': _sign_adj(ks[1], N, 0.005), 'edge_adj': _sign_adj(ks[2], N, 0.005), 'gat_W': jax.random.normal(ks[3], (HEADS, H, H), jnp.float32) * (gain / np.sqrt(H, dtype=np.float32)), 'gat_a': jax.random.normal(ks[4], (HEADS, 2 * H, 1), jnp.float32) * 0.1, 'edge_Wih': jax.random.normal(ks[5], (3 * H, H), jnp.float32) * std, 'edge_Whh': jax.random.normal(ks[6], (3 * H, H), jnp.float32) * std, 'edge_bih': jnp.zeros((3 * H,), jnp.float32), 'edge_bhh': jnp.zeros((3 * H,), jnp.float32), 'node_Wih': jax.random.normal(ks[7], (3 * H, H), jnp.float32) * std, 'node_Whh': jax.random.normal(ks[8], (3 * H, H), jnp.float32) * std, 'node_bih': jnp.zeros((3 * H,), jnp.float32), 'node_bhh': jnp.zeros((3 * H,), jnp.float32)}
    _L1_gnn_all = _L1_gnn_setup()
    _L1_gnn_in = {k: v for k, v in _L1_gnn_all.items() if k in ('gat_W', 'gat_a', 'edge_Wih', 'edge_Whh', 'edge_bih', 'edge_bhh', 'node_Wih', 'node_Whh', 'node_bih', 'node_bhh')}
    del _L1_gnn_all

    def _L1_ffn_setup():
        import jax, jax.numpy as jnp
        import numpy as np
        N_EXPERTS = 8
        TOP_K = 2
        key = jax.random.key(seed)
        ks = jax.random.split(key, 5)
        B, T, C, E, H = (8, 1024, 128, 8, 341)
        scale = 1.0 / np.sqrt(C)
        return {'x': jax.random.normal(ks[0], (B, T, C), dtype=jnp.float32), 'router_w': jax.random.normal(ks[1], (E, C), dtype=jnp.float32) * scale, 'w1': jax.random.normal(ks[2], (E, H, C), dtype=jnp.float32) * scale, 'w2': jax.random.normal(ks[3], (E, C, H), dtype=jnp.float32) * (1.0 / np.sqrt(H)), 'w3': jax.random.normal(ks[4], (E, H, C), dtype=jnp.float32) * scale}
    _L1_ffn_all = _L1_ffn_setup()
    _L1_ffn_in = {k: v for k, v in _L1_ffn_all.items() if k in ('router_w', 'w1', 'w2', 'w3')}
    del _L1_ffn_all
    return {'x': x, 'adj': adj, 'L0_gnn_W': _L0_gnn_in['W'], 'L0_gnn_B': _L0_gnn_in['B'], 'L0_ffn_Wg': _L0_ffn_in['Wg'], 'L0_ffn_bg': _L0_ffn_in['bg'], 'L0_ffn_bias': _L0_ffn_in['bias'], 'L0_ffn_W1': _L0_ffn_in['W1'], 'L0_ffn_b1': _L0_ffn_in['b1'], 'L0_ffn_W2': _L0_ffn_in['W2'], 'L0_ffn_b2': _L0_ffn_in['b2'], 'L1_gnn_gat_W': _L1_gnn_in['gat_W'], 'L1_gnn_gat_a': _L1_gnn_in['gat_a'], 'L1_gnn_edge_Wih': _L1_gnn_in['edge_Wih'], 'L1_gnn_edge_Whh': _L1_gnn_in['edge_Whh'], 'L1_gnn_edge_bih': _L1_gnn_in['edge_bih'], 'L1_gnn_edge_bhh': _L1_gnn_in['edge_bhh'], 'L1_gnn_node_Wih': _L1_gnn_in['node_Wih'], 'L1_gnn_node_Whh': _L1_gnn_in['node_Whh'], 'L1_gnn_node_bih': _L1_gnn_in['node_bih'], 'L1_gnn_node_bhh': _L1_gnn_in['node_bhh'], 'L1_ffn_router_w': _L1_ffn_in['router_w'], 'L1_ffn_w1': _L1_ffn_in['w1'], 'L1_ffn_w2': _L1_ffn_in['w2'], 'L1_ffn_w3': _L1_ffn_in['w3']}

def reference(x, adj, L0_gnn_W, L0_gnn_B, L0_ffn_Wg, L0_ffn_bg, L0_ffn_bias, L0_ffn_W1, L0_ffn_b1, L0_ffn_W2, L0_ffn_b2, L1_gnn_gat_W, L1_gnn_gat_a, L1_gnn_edge_Wih, L1_gnn_edge_Whh, L1_gnn_edge_bih, L1_gnn_edge_bhh, L1_gnn_node_Wih, L1_gnn_node_Whh, L1_gnn_node_bih, L1_gnn_node_bhh, L1_ffn_router_w, L1_ffn_w1, L1_ffn_w2, L1_ffn_w3):
    import jax
    import jax.numpy as jnp

    def _L0_gnn_ref(z, dist_matrix, W, B):
        import jax, jax.numpy as jnp
        import numpy as np
        N = 4096
        D = 128
        CUTOFF = 1.0
        MU = 1.0
        SIGMA = 0.5

        def sensitivity(r, mu, sigma):
            return jnp.exp(-(1.0 / r - 1.0 / mu) ** 2 / (2.0 * sigma * sigma))
        msg = z @ W + B
        sens = sensitivity(dist_matrix, MU, SIGMA)
        weights = jnp.where(dist_matrix < CUTOFF, sens, 0.0)
        return weights @ msg

    def _L0_ffn_ref(x, Wg, bg, bias, W1, b1, W2, b2):
        import jax, jax.numpy as jnp
        import numpy as np
        D_MODEL = 128
        EXPERT_DIM = 256
        NUM_EXPERTS = 8
        TOP_K = 2
        SEQ_LEN = 1024
        BATCH = 2
        x_flat = x.reshape(-1, D_MODEL)
        gate_logits = x_flat @ Wg + bg + bias
        topk_vals, topk_idx = jax.lax.top_k(gate_logits, TOP_K)
        topk_w = jax.nn.softmax(topk_vals, axis=-1)
        combine = (jax.nn.one_hot(topk_idx, NUM_EXPERTS, dtype=x.dtype) * topk_w[..., None]).sum(axis=1)
        h = jax.nn.relu(jnp.einsum('td,edh->teh', x_flat, W1) + b1)
        y = jnp.einsum('teh,ehd->ted', h, W2) + b2
        out = jnp.einsum('ted,te->td', y, combine)
        return out.reshape(x.shape)

    def _L1_gnn_ref(h, node_adj, edge_adj, gat_W, gat_a, edge_Wih, edge_Whh, edge_bih, edge_bhh, node_Wih, node_Whh, node_bih, node_bhh):
        import jax, jax.numpy as jnp
        import numpy as np
        N, H, HEADS = (2048, 128, 3)
        ALPHA = 0.2
        NEG_INF = -9000000000000000.0

        def _sign_adj(key, n, density):
            k1, k2 = jax.random.split(key)
            mask = jax.random.uniform(k1, (n, n)) < density
            sign = jnp.where(jax.random.uniform(k2, (n, n)) < 0.5, -1.0, 1.0)
            adj = jnp.where(mask, sign, 0.0).astype(jnp.float32)
            idx = jnp.arange(n)
            return adj.at[idx, idx].set(1.0)

        def _gru_cell(x, hstate, Wih, Whh, bih, bhh):
            gi = x @ Wih.T + bih
            gh = hstate @ Whh.T + bhh
            ir, iz, inn = jnp.split(gi, 3, axis=1)
            hr, hz, hn = jnp.split(gh, 3, axis=1)
            r = jax.nn.sigmoid(ir + hr)
            z = jax.nn.sigmoid(iz + hz)
            n = jnp.tanh(inn + r * hn)
            return (1.0 - z) * n + z * hstate

        def _gat_head(h, node_adj, edge_adj, W, a):
            hW = h @ W
            hp = (node_adj > 0).astype(hW.dtype) @ hW
            hm = (node_adj < 0).astype(hW.dtype) @ hW
            e_plus = jax.nn.leaky_relu(jnp.concatenate([hp, hm], axis=1) @ a, ALPHA)[:, 0]
            e_minus = jax.nn.leaky_relu(jnp.concatenate([hm, hp], axis=1) @ a, ALPHA)[:, 0]
            att = jnp.where(edge_adj > 0, e_plus[None, :], NEG_INF)
            att = jnp.where(edge_adj < 0, e_minus[None, :], att)
            att = jax.nn.softmax(att, axis=1)
            return att * edge_adj @ hW
        dn = jnp.diag(node_adj)
        de = jnp.diag(edge_adj)
        idx = jnp.arange(node_adj.shape[0])
        node_adj_norm = node_adj.at[idx, idx].add(-dn)
        edge_adj_norm = edge_adj.at[idx, idx].add(-de)
        node_support = node_adj_norm @ h
        edge_output = _gru_cell(node_support, h, edge_Wih, edge_Whh, edge_bih, edge_bhh)
        edge_support = _gat_head(h, node_adj_norm, edge_adj_norm, gat_W[0], gat_a[0])
        for i in range(1, HEADS):
            edge_support = edge_support + _gat_head(h, node_adj_norm, edge_adj_norm, gat_W[i], gat_a[i])
        edge_support = edge_support / HEADS
        node_output = _gru_cell(edge_support, h, node_Wih, node_Whh, node_bih, node_bhh)
        return de[:, None] * edge_output + dn[:, None] * node_output

    def _L1_ffn_ref(x, router_w, w1, w2, w3):
        import jax, jax.numpy as jnp
        import numpy as np
        N_EXPERTS = 8
        TOP_K = 2
        B, T, C = x.shape
        flat = x.reshape(-1, C)
        logits = flat @ router_w.T
        probs = jax.nn.softmax(logits, axis=-1)
        topk_probs, topk_idx = jax.lax.top_k(probs, TOP_K)
        topk_probs = topk_probs / (jnp.sum(topk_probs, axis=-1, keepdims=True) + 1e-09)
        onehot = jax.nn.one_hot(topk_idx, N_EXPERTS, dtype=flat.dtype)
        gates = jnp.einsum('nk,nke->ne', topk_probs, onehot)
        h1 = jnp.einsum('nc,ehc->neh', flat, w1)
        h3 = jnp.einsum('nc,ehc->neh', flat, w3)
        h = jax.nn.silu(h1) * h3
        y = jnp.einsum('neh,ech->nec', h, w2)
        out = jnp.einsum('ne,nec->nc', gates, y)
        return out.reshape(B, T, C)
    x = x + _L0_gnn_ref(_layernorm(x, axis=-1), adj, L0_gnn_W, L0_gnn_B)
    x = x + _L0_ffn_ref(_layernorm(x, axis=-1)[None], L0_ffn_Wg, L0_ffn_bg, L0_ffn_bias, L0_ffn_W1, L0_ffn_b1, L0_ffn_W2, L0_ffn_b2)[0]
    x = x + _L1_gnn_ref(_layernorm(x, axis=-1), adj, adj, L1_gnn_gat_W, L1_gnn_gat_a, L1_gnn_edge_Wih, L1_gnn_edge_Whh, L1_gnn_edge_bih, L1_gnn_edge_bhh, L1_gnn_node_Wih, L1_gnn_node_Whh, L1_gnn_node_bih, L1_gnn_node_bhh)
    x = x + _L1_ffn_ref(_layernorm(x, axis=-1)[None], L1_ffn_router_w, L1_ffn_w1, L1_ffn_w2, L1_ffn_w3)[0]
    return x

_drawn_inputs = setup_inputs


def setup_inputs(seed=0):
    import zlib

    import numpy as np

    out = dict(_drawn_inputs(seed))
    spreads = {'L0_gnn_B': (0.0, 0.332),
     'L0_ffn_bias': (0.0, 0.8),
     'L1_gnn_edge_bih': (0.0, 0.8),
     'L1_gnn_edge_bhh': (0.0, 2.0),
     'L1_gnn_node_bih': (0.0, 2.0),
     'L1_gnn_node_bhh': (0.0, 2.0)}
    factors = {'L0_ffn_Wg': 8.0,
     'L0_ffn_bg': 8.0,
     'L0_ffn_W1': 8.0,
     'L0_ffn_b1': 8.0,
     'L0_ffn_W2': 8.0,
     'L0_ffn_b2': 8.0,
     'L1_gnn_gat_W': 8.0,
     'L1_gnn_gat_a': 8.0,
     'L1_gnn_edge_Wih': 3.354,
     'L1_gnn_edge_Whh': 8.0,
     'L1_gnn_node_Wih': 8.0,
     'L1_gnn_node_Whh': 22.306,
     'L1_ffn_router_w': 3.62,
     'L1_ffn_w1': 3.442,
     'L1_ffn_w2': 3.203,
     'L1_ffn_w3': 3.198}
    for name, (base, spread) in spreads.items():
        noise = np.random.default_rng([zlib.crc32(name.encode()), seed]).standard_normal(out[name].shape)
        drawn = base * np.exp(spread * noise) if base else spread * noise
        out[name] = jnp.asarray(drawn.astype(out[name].dtype))
    for name, factor in factors.items():
        out[name] = (out[name] * factor).astype(out[name].dtype)
    return out
```

```python
from contextlib import ExitStack

import concourse.bass as bass
from concourse import mybir

F32 = mybir.dt.float32
BF16 = mybir.dt.bfloat16
ALU = mybir.AluOpType
ACT = mybir.ActivationFunctionType
AX = mybir.AxisListType

P = 128
N = 1354
T = -(-N // P)
NP = T * P
CW = 512
C = -(-N // CW)
E = 8
H0 = 256
M0 = H0 // P
H1 = 341
M1 = -(-H1 // P)
K = 3
NEG = -1.0e30
PARTS = 3


def rows(t):
    return min(P, N - t * P)


def width(c):
    return min(CW, N - c * CW)


def cols(c):
    return slice(c * CW, c * CW + width(c))


def tiles(c):
    return range(c * CW // P, min(T, (c + 1) * CW // P))


LN_ORDER = [(0, c) for c in range(C)]
LN_ORDER += [(1, 0)]
for _c in range(C):
    LN_ORDER += ([(1, _c + 1)] if _c + 1 < C else []) + [(2, _c)]
LN_ORDER += [(3, c) for c in range(C)]
LN_AT = {key: n for n, key in enumerate(LN_ORDER)}


def build(nc, xT_d, adjT_d, adj_d, W_d, B_d, Wg_d, bg_d, bias_d, W1_d, b1_d, W2_d, b2_d,
          gW_d, gWT_d, ga_d, eWih_d, eWhh_d, ebih_d, ebhh_d, nWih_d, nWhh_d, nbih_d, nbhh_d,
          rw_d, w1_d, w3_d, w2_d, out_d):
    with ExitStack() as ctx:
        def sb(name, shape, dt=F32):
            return ctx.enter_context(nc.sbuf_tensor(name, shape, dt))

        def sem(name):
            return ctx.enter_context(nc.semaphore(name))

        regA = sb("regA", [P, T * N])
        regB = sb("regB", [P, T * N])
        regM = sb("regM", [P, T * N // 2])
        regH = sb("regH", [P, T * K * P])
        regL = sb("regL", [P, 2 * N])
        regR = sb("regR", [P, 1024])
        xT = sb("xT", [P, N])
        zT = sb("zT", [P, NP])
        gruw = sb("gruw", [P, 2, 3 * P])
        hTok = sb("hTok", [P, T, P])
        eplus = sb("eplus", [P, N])
        ident = sb("ident", [P, P])
        offdiag = sb("offdiag", [P, P])
        ones = sb("ones", [P, P])
        meanw = sb("meanw", [P, P])
        sel6 = sb("sel6", [P, 6])
        tri = sb("tri", [P, E, E])
        eps = sb("eps", [P, 1])
        neg1 = sb("neg1", [P, 1])
        rowW = sb("rowW", [1, 2 * P])
        gru_b = sb("gru_b", [P, 2, 2, 3])
        gru_c = sb("gru_c", [P, 2, 4])
        b1c = sb("b1c", [P, E * M0])
        b2r = sb("b2r", [E, P])
        ga = sb("ga", [P, 2 * K])
        u18 = sb("u18", [P, T, 2, 18], BF16)
        dcol = sb("dcol", [P, T])
        mx = sb("mx", [P, K * T])
        mx2 = sb("mx2", [P, K * T])
        negm = sb("negm", [P, K * T])
        den = sb("den", [P, K * T])
        rden = sb("rden", [P, K * T])
        rt = sb("rt", [P, 4, 4 * E])
        rs = sb("rs", [P, 2, 4])

        adjT = regA[:, :].rearrange("p (t n) -> p t n", t=T)
        adjR = regB[:, :].rearrange("p (t n) -> p t n", t=T)

        def view(reg, off, *shape):
            size = 1
            for s in shape:
                size *= s
            v = reg[:, off:off + size]
            if len(shape) == 2:
                v = v.rearrange("p (a b) -> p a b", a=shape[0])
            if len(shape) == 3:
                v = v.rearrange("p (a b c) -> p a b c", a=shape[0], b=shape[1])
            return v

        y_ring = view(regB, 0, 3, CW)
        s_ring = view(regB, 3 * CW, 2, CW)
        w_ring = view(regB, 5 * CW, 3, CW)
        hr_ring = view(regB, 8 * CW, 3, CW)
        hg_ring = view(regB, 11 * CW, 3, CW)
        msg = view(regB, 14 * CW, T, P)
        Wl0 = view(regB, 18 * CW, P)
        GT0 = view(regB, 19 * CW, CW)
        Wg = view(regB, 20 * CW, E)
        rk0 = view(regB, 21 * CW, 2, 4 * E * E)
        W1s = view(regM, 0, E, H0)
        W2s = view(regM, E * H0, E, M0, P)
        wcat = view(regM, 2 * E * H0, 3 * P + 6)
        gWT = view(regM, 2 * E * H0 + 512, K, P)
        xc_ring = view(regL, 0, 2, CW)
        sq = view(regL, 2 * CW, CW)
        yb = view(regL, 3 * CW, CW)
        tb = view(regL, 4 * CW, CW)
        e18 = regL[0:18, 0:N]
        nsT = view(regL, N, N)
        eminus = nsT
        masks = regR[:, :].bitcast(BF16).rearrange("p (r s n) -> p r s n", r=2, s=2)
        mbneg = regR[:, :].bitcast(BF16)[:, 0:N]
        mb = regM[:, :].bitcast(BF16).rearrange("p (t n) -> p t n", t=T)
        hW = regH[:, :].rearrange("p (t n) -> p t n", t=T)
        qT = view(regA, 0, 2, T, CW)
        S = view(regA, 2 * T * CW, 2, NP)
        S2 = hTok[:, :, :].rearrange("p t n -> p (t n)")[:, 0:N]
        u = view(regR, 0, T, 6)
        ur = view(regR, T * 6, T, 6)
        gt_edge = view(regA, T * CW, 6, CW)
        gt_node = view(regB, 0, 6, CW)
        w1s = view(regM, 0, E, H1)
        w3s = view(regM, E * H1, E, H1)
        w2s = view(regB, 6 * CW, E, M1, P)
        s1_ring = view(regA, 0, 3, CW)
        hg1_ring = view(regA, 3 * CW, 3, CW)
        hm_ring = view(regA, 6 * CW, 3, CW)
        GT1 = view(regA, 9 * CW, CW)
        rw = view(regA, 10 * CW, E)
        rk1 = view(regA, 11 * CW, 2, 4 * E * E)

        bk = [ctx.enter_context(nc.psum_tensor(f"bank{i}", [P, CW], F32)) for i in range(8)]
        B_LN, B_MISC, B_G, B_Y, B_GATE = bk[0], bk[1], bk[2], bk[3], bk[4]
        B_H = bk[5:8]
        B_ACC = bk[1:4]
        B_R, B_Z, B_NI, B_NH = bk[5], bk[6], bk[7], bk[4]

        names = """x_in adjT_in0 adjT_in1 adjT_in2 adjR_in wts0_in ffn0_in gat_in edge_w_in node_w_in
            ffn1a_in ffn1b_in rw_in out_done const_set zpad_set
            ln_mean ln_xc ln_sq ln_var ln_log ln_y0 ln_step ln_z
            prep r_set bgs_set msg_ps msg_set recip_done sens_sq sens_exp w_ready l0_mm
            x1_ready x2_ready x3_ready x4_ready
            logits_ps route_d route_e route_step gt_ps gt_set gate_ps h_ps h_relu h_gated y_mm
            v_ps v_set htok_ps htok_set hw_ps hw_set u_step u18_set
            offdiag_set mask_set mask_used ns_mm e18_mm ns_set e18_set
            eb_ps eb_fifth eb_set mb_set dcol_set row_diag_set spad_set
            s_step s_set p_set q_step q_set tr_ps tr_set gat_mm es_set
            gru_ps gru_t gru_a gru_n gru_step gru_src deb_ps x_edge gru_bias
            f1_gate f1_h1 f1_h3 f1_silu f1_sg f1_m f1_y f1_logits f1_gtps f1_gt""".split()
        s = {n: sem(n) for n in names}

        def at(eng, name, value):
            if value > 0:
                eng.wait_ge(s[name], value)

        block = ctx.enter_context(nc.Block())

        LN_SRC = [("x_in", 16), ("x1_ready", 1), ("x2_ready", 1), ("x3_ready", 1)]

        def ln_source_ready(eng, l, c):
            at(eng, LN_SRC[l][0], 16 if l == 0 else c + 1)

        PIECES = C * T
        SHARE = [range(e * T // E, (e + 1) * T // E) for e in range(E)]

        @block.sync
        def _(sp):
            def adjT_load(c):
                full = (T - 1) * P
                sp.dma_start(adjT[:, 0:T - 1, cols(c)],
                             adjT_d[0:full, cols(c)].rearrange("(t p) n -> p t n", p=P)).then_inc(s[f"adjT_in{c}"], 16)
                sp.dma_start(adjT[0:N - full, T - 1, cols(c)], adjT_d[full:N, cols(c)]).then_inc(s[f"adjT_in{c}"], 16)

            sp.dma_start(xT[:, :], xT_d).then_inc(s["x_in"], 16)
            sp.dma_start(Wl0, W_d).then_inc(s["wts0_in"], 16)
            sp.dma_start(rowW[0:1, 0:P], B_d).then_inc(s["wts0_in"], 16)
            sp.dma_start(rowW[0:1, P:P + E], bg_d).then_inc(s["wts0_in"], 16)
            sp.dma_start(rowW[0:1, P + E:P + 2 * E], bias_d).then_inc(s["wts0_in"], 16)
            adjT_load(0)
            sp.dma_start(Wg, Wg_d).then_inc(s["ffn0_in"], 16)
            sp.dma_start(W1s, W1_d.rearrange("e c h -> c e h")).then_inc(s["ffn0_in"], 16)
            sp.dma_start(W2s, W2_d.rearrange("e (m p) d -> p e m d", p=P)).then_inc(s["ffn0_in"], 16)
            sp.dma_start(b1c[:, :], b1_d).then_inc(s["ffn0_in"], 16)
            sp.dma_start(b2r[:, :], b2_d).then_inc(s["ffn0_in"], 16)
            adjT_load(1)
            adjT_load(2)
            sp.dma_start(wcat[:, 0:3 * P].rearrange("p (k d) -> p k d", k=K),
                         gW_d.rearrange("k c d -> c k d")).then_inc(s["gat_in"], 16)
            sp.dma_start(gWT, gWT_d).then_inc(s["gat_in"], 16)
            sp.dma_start(ga[:, :], ga_d).then_inc(s["gat_in"], 16)
            for n, (wi, wh, bi, bh) in enumerate([(eWih_d, eWhh_d, ebih_d, ebhh_d), (nWih_d, nWhh_d, nbih_d, nbhh_d)]):
                sp.dma_start(gru_b[:, n, 0, :], bi).then_inc(s["edge_w_in"], 16)
                sp.dma_start(gru_b[:, n, 1, :], bh).then_inc(s["edge_w_in"], 16)
            sp.dma_start(gruw[:, 0, :], eWih_d).then_inc(s["edge_w_in"], 16)
            sp.dma_start(gruw[:, 1, :], eWhh_d).then_inc(s["edge_w_in"], 16)
            sp.wait_ge(s["x2_ready"], C)
            sp.dma_start(adjR[:, 0:T - 1, :], adj_d[0:(T - 1) * P, :].rearrange("(t p) n -> p t n", p=P)).then_inc(s["adjR_in"], 16)
            sp.dma_start(adjR[0:rows(T - 1), T - 1, :], adj_d[(T - 1) * P:N, :]).then_inc(s["adjR_in"], 16)
            sp.wait_ge(s["x_edge"], C)
            sp.dma_start(gruw[:, 0, :], nWih_d).then_inc(s["node_w_in"], 16)
            sp.dma_start(gruw[:, 1, :], nWhh_d).then_inc(s["node_w_in"], 16)
            sp.wait_ge(s["s_set"], K * T)
            sp.dma_start(w1s, w1_d).then_inc(s["ffn1a_in"], 16)
            sp.dma_start(w3s, w3_d).then_inc(s["ffn1a_in"], 16)
            sp.wait_ge(s["q_set"], K * T)
            for m in range(M1):
                r = min(P, H1 - m * P)
                sp.dma_start(w2s[0:r, :, m, :], w2_d[m * P:m * P + r, :, :]).then_inc(s["ffn1b_in"], 16)
            sp.wait_ge(s["gat_mm"], K * C)
            sp.dma_start(rw, rw_d).then_inc(s["rw_in"], 16)
            for c in range(C):
                sp.wait_ge(s["x4_ready"], c + 1)
                sp.dma_start(out_d[:, cols(c)], xT[:, cols(c)]).then_inc(s["out_done"], 16)
            sp.wait_ge(s["out_done"], 16 * C)

        @block.gpsimd
        def _(pool):
            pool.memset(ident[:, :], 0.0).then_inc(s["prep"], 1)
            pool.memset(offdiag[:, :], 1.0).then_inc(s["prep"], 1)
            pool.memset(ones[:, :], 1.0).then_inc(s["prep"], 1)
            pool.memset(meanw[:, :], 1.0 / P).then_inc(s["prep"], 1)
            pool.memset(sel6[:, :], 0.0).then_inc(s["prep"], 1)
            pool.memset(tri[:, :, :], 1.0).then_inc(s["prep"], 1)
            pool.memset(eps[:, :], 1.0e-5).then_inc(s["prep"], 1)
            pool.memset(neg1[:, :], -1.0).then_inc(s["prep"], 1)
            pool.memset(zT[:, N:NP], 0.0).then_inc(s["zpad_set"], 1)
            pool.wait_ge(s["prep"], 8)
            pool.affine_select(out=ident[:, :], in_=ident[:, :], compare_op=ALU.not_equal, fill=1.0,
                               base=0, pattern=[[-1, P]], channel_multiplier=1).then_inc(s["const_set"], 1)
            pool.affine_select(out=offdiag[:, :], in_=offdiag[:, :], compare_op=ALU.not_equal, fill=0.0,
                               base=0, pattern=[[-1, P]], channel_multiplier=1).then_inc(s["const_set"], 1)
            pool.affine_select(out=tri[:, :, :], in_=tri[:, :, :], compare_op=ALU.is_gt, fill=0.0,
                               base=0, pattern=[[1, E], [-1, E]], channel_multiplier=0).then_inc(s["const_set"], 1)
            for part in range(PARTS):
                pool.affine_select(out=sel6[:, :], in_=sel6[:, :], compare_op=ALU.not_equal, fill=1.0,
                                   base=-6 * part, pattern=[[-1, 6]], channel_multiplier=1).then_inc(s["const_set"], 1)
                pool.wait_ge(s["const_set"], 4 + part)
            pool.wait_ge(s["w_ready"], PIECES)
            for t in range(T):
                r = rows(t)
                blk = adjT[0:r, t, t * P:t * P + r]
                pool.tensor_tensor(blk, blk, offdiag[0:r, 0:r], ALU.mult).then_inc(s["offdiag_set"], 1)
            for t in range(T):
                r = rows(t)
                blk = adjR[0:r, t, t * P:t * P + r]
                pool.wait_ge(s["dcol_set"], t + 1)
                pool.tensor_tensor(blk, blk, offdiag[0:r, 0:r], ALU.mult).then_inc(s["row_diag_set"], 1)
            pool.wait_ge(s["ns_mm"], C)
            pool.wait_ge(s["mask_set"], 2 * PIECES)
            pool.memset(S[:, :, N:NP], 0.0).then_inc(s["spad_set"], 1)

        @block.scalar
        def _(act):
            def ln_square(l, c):
                n, w = LN_AT[l, c], width(c)
                at(act, "ln_xc", n + 1)
                at(act, "ln_var", n)
                nc.scalar.activation(sq[:, 0:w], xc_ring[:, n % 2, 0:w], ACT.Square).then_inc(s["ln_sq"], 1)

            def ln_rsqrt(l, c):
                n, w = LN_AT[l, c], width(c)
                at(act, "ln_var", n + 1)
                at(act, "ln_z", n)
                nc.scalar.activation(tb[:, 0:w], B_LN[:, 0:w], ACT.Ln, bias=eps[:, 0:1]).then_inc(s["ln_log"], 1)
                at(act, "ln_log", n + 1)
                nc.scalar.activation(yb[:, 0:w], tb[:, 0:w], ACT.Exp, scale=-0.5).then_inc(s["ln_y0"], 1)

            def piece(p):
                c, j = divmod(p, T)
                r, w = rows(j), width(c)
                at(act, "recip_done", p + 1)
                at(act, "w_ready", p - 1)
                nc.scalar.activation(s_ring[0:r, p % 2, 0:w], y_ring[0:r, p % 3, 0:w], ACT.Square,
                                     bias=neg1[0:r, 0:1]).then_inc(s["sens_sq"], 1)
                at(act, "sens_sq", p + 1)
                nc.scalar.activation(s_ring[0:r, p % 2, 0:w], s_ring[0:r, p % 2, 0:w], ACT.Exp,
                                     scale=-2.0).then_inc(s["sens_exp"], 1)

            act.wait_ge(s["const_set"], 6)
            for c in range(C):
                ln_square(0, c)
                ln_rsqrt(0, c)
                at(act, "msg_ps", c + 1)
                k = len(tiles(c))
                nc.scalar.copy(msg[:, c * 4:c * 4 + k, :], B_MISC[:, 0:k * P]).then_inc(s["msg_set"], 1)
            for p in range(T):
                piece(p)
            ln_square(1, 0)
            ln_rsqrt(1, 0)
            for c in range(C):
                w = width(c)
                at(act, "route_d", c + 1)
                k = len(tiles(c)) * E
                nc.scalar.activation(rt[:, 1, 0:k], rt[:, 0, 0:k], ACT.Exp).then_inc(s["route_e"], 1)
                for e in range(E):
                    for m in range(M0):
                        q = (c * E + e) * M0 + m
                        at(act, "h_ps", q + 1)
                        at(act, "h_gated", q - 2)
                        nc.scalar.activation(hr_ring[:, q % 3, 0:w], B_H[q % 3][:, 0:w], ACT.Relu,
                                             bias=b1c[:, e * M0 + m:e * M0 + m + 1]).then_inc(s["h_relu"], 1)
                    if c + 1 < C:
                        for j in SHARE[e]:
                            piece((c + 1) * T + j)
                if c + 1 < C:
                    ln_square(1, c + 1)
                    ln_rsqrt(1, c + 1)
                ln_square(2, c)
                ln_rsqrt(2, c)
                at(act, "htok_ps", c + 1)
                k = len(tiles(c))
                nc.scalar.copy(hTok[:, c * 4:c * 4 + k, :], B_MISC[:, 0:k * P]).then_inc(s["htok_set"], 1)
                for t in tiles(c):
                    at(act, "hw_ps", t + 1)
                    nc.scalar.copy(hW[:, t, :], B_H[t % 3][:, 0:K * P]).then_inc(s["hw_set"], 1)
                    nc.scalar.copy(u[:, t, :], B_H[t % 3][:, K * P:K * P + 6]).then_inc(s["hw_set"], 1)
            for c in range(C):
                at(act, "ns_mm", c + 1)
                nc.scalar.copy(nsT[:, cols(c)], B_G[:, 0:width(c)]).then_inc(s["ns_set"], 1)

            def score_rows(k):
                for i in range(2 * C):
                    c = i // 2
                    n = 2 * C * k + i
                    at(act, "eb_ps", n + 1)
                    dst = (eplus, eminus)[i % 2]
                    if i == 1 and k == 0:
                        act.wait_ge(s["x_edge"], C)
                    if i < 2:
                        act.wait_ge(s["s_set"], T * k) if k else None
                    nc.scalar.mul(dst[:, cols(c)], B_LN[:, 0:width(c)], 0.2).then_inc(s["eb_fifth"], 1)

            def gru(n, c, tmp):
                g, w = n * C + c, width(c)
                if n == 1:
                    at(act, "gat_mm", K * C)
                    if c:
                        at(act, "gru_ps", g)
                    nc.scalar.mul(tmp[:, 5, 0:w], B_ACC[c][:, 0:w], 1.0 / K).then_inc(s["es_set"], 1)
                at(act, "gru_ps", g + 1)
                at(act, "x3_ready" if n else "x_edge", c)
                nc.scalar.activation(tmp[:, 0, 0:w], B_R[:, 0:w], ACT.Tanh, scale=0.5,
                                     bias=gru_c[:, n, 0:1]).then_inc(s["gru_t"], 1)
                nc.scalar.activation(tmp[:, 1, 0:w], B_Z[:, 0:w], ACT.Tanh, scale=0.5,
                                     bias=gru_c[:, n, 1:2]).then_inc(s["gru_t"], 1)
                at(act, "gru_a", g + 1)
                nc.scalar.activation(tmp[:, 3, 0:w], tmp[:, 2, 0:w], ACT.Tanh,
                                     bias=gru_c[:, n, 2:3]).then_inc(s["gru_n"], 1)

            at(act, "gru_bias", 1)
            for c in range(C):
                gru(0, c, gt_edge)
            for g in range(K * T + 2):
                if g < K * T and g % T == 0:
                    score_rows(g // T)
                if g < K * T:
                    r = rows(g % T)
                    at(act, "s_set", g + 1)
                    nc.scalar.activation(S[0:r, g % 2, 0:N], S[0:r, g % 2, 0:N], ACT.Exp, bias=negm[0:r, g:g + 1],
                                         accum_out=den[0:r, g:g + 1]).then_inc(s["p_set"], 1)
                if g >= 1 and g - 1 < K * T:
                    h = g - 1
                    k, t = divmod(h, T)
                    r, c = rows(t), t // 4
                    for v in range(3):
                        at(act, "tr_ps", 3 * h + v + 1)
                        if t % 4 == 0 and v == 0:
                            at(act, "gat_mm", k * C + c - 1)
                        nb = min(4, T - 4 * v)
                        nc.scalar.copy(qT[:, (k * C + c) % 2, 4 * v:4 * v + nb, (t % 4) * P:(t % 4) * P + r],
                                       B_H[v][:, 0:nb * P].rearrange("p (b i) -> p b i", b=nb)[:, :, 0:r]
                                       ).then_inc(s["tr_set"], 1)
            for c in range(C):
                gru(1, c, gt_node)
                ln_square(3, c)
                ln_rsqrt(3, c)
            for c in range(C):
                w = width(c)
                k = len(tiles(c)) * E
                at(act, "route_d", C + c + 1)
                nc.scalar.activation(rt[:, 1, 0:k], rt[:, 0, 0:k], ACT.Exp).then_inc(s["route_e"], 1)
                for e in range(E):
                    for m in range(M1):
                        q = (c * E + e) * M1 + m
                        r = min(P, H1 - m * P)
                        at(act, "f1_h1", q + 1)
                        at(act, "f1_sg", q - 2)
                        nc.scalar.activation(s1_ring[0:r, q % 3, 0:w], B_H[q % 2][0:r, 0:w], ACT.Silu).then_inc(s["f1_silu"], 1)

        @block.tensor
        def _(pe):
            def ln_mean(l, c):
                n, w = LN_AT[l, c], width(c)
                ln_source_ready(pe, l, c)
                at(pe, "ln_z", n)
                nc.tensor.matmul(B_LN[:, 0:w], meanw[:, :], xT[:, cols(c)], start=True, stop=True).then_inc(s["ln_mean"], 1)

            def ln_var(l, c):
                n, w = LN_AT[l, c], width(c)
                at(pe, "ln_sq", n + 1)
                nc.tensor.matmul(B_LN[:, 0:w], meanw[:, :], sq[:, 0:w], start=True, stop=True).then_inc(s["ln_var"], 1)

            def normed(l, c):
                at(pe, "ln_z", LN_AT[l, c] + 1)

            def piece(p):
                c, j = divmod(p, T)
                r, w = rows(j), width(c)
                at(pe, "w_ready", p + 1)
                if j == 0:
                    at(pe, "x1_ready", c)
                nc.tensor.matmul(B_G[:, 0:w], msg[0:r, j, :], w_ring[0:r, p % 3, 0:w],
                                 start=(j == 0), stop=(j == T - 1)).then_inc(s["l0_mm"], 1)

            pe.wait_ge(s["const_set"], 6)
            pe.wait_ge(s["zpad_set"], 1)
            pe.wait_ge(s["wts0_in"], 64)
            for c in range(C):
                ln_mean(0, c)
                ln_var(0, c)
                normed(0, c)
                at(pe, "msg_set", c)
                for i, t in enumerate(tiles(c)):
                    o = B_MISC[:, i * P:(i + 1) * P]
                    nc.tensor.matmul(o, zT[:, t * P:(t + 1) * P], Wl0, start=True, stop=False)
                    mm = nc.tensor.matmul(o, ones[0:1, :], rowW[0:1, 0:P], start=False, stop=True)
                mm.then_inc(s["msg_ps"], 1)
            at(pe, "msg_set", C)
            for p in range(T):
                piece(p)
            ln_mean(1, 0)
            ln_var(1, 0)
            pe.wait_ge(s["ffn0_in"], 80)
            pe.wait_ge(s["bgs_set"], 1)
            for c in range(C):
                w = width(c)
                normed(1, c)
                if c == 0:
                    pe.wait_ge(s["gat_in"], 48)
                    for k in range(K):
                        mm = nc.tensor.matmul(B_MISC[:, 2 * k:2 * k + 2], gWT[:, k, :], ga[:, 2 * k:2 * k + 2],
                                              start=True, stop=True)
                    mm.then_inc(s["v_ps"], 1)
                    at(pe, "v_set", 1)
                else:
                    at(pe, "htok_set", c)
                for i, t in enumerate(tiles(c)):
                    o = B_MISC[:, i * E:(i + 1) * E]
                    nc.tensor.matmul(o, zT[:, t * P:(t + 1) * P], Wg, start=True, stop=False)
                    mm = nc.tensor.matmul(o, ones[0:1, :], rowW[0:1, P:P + E], start=False, stop=True)
                mm.then_inc(s["logits_ps"], 1)
                at(pe, "route_step", c + 1)
                for i, t in enumerate(tiles(c)):
                    mm = nc.tensor.transpose(B_MISC[0:E, i * P:(i + 1) * P], rt[:, 3, i * E:(i + 1) * E], ident[:, :])
                mm.then_inc(s["gt_ps"], 1)
                at(pe, "gt_set", c + 1)
                at(pe, "x2_ready", c)
                nc.tensor.matmul(B_Y[:, 0:w], b2r[:, :], GT0[0:E, 0:w], start=True, stop=False)

                def down(e):
                    for m in range(M0):
                        q = (c * E + e) * M0 + m
                        at(pe, "h_gated", q + 1)
                        nc.tensor.matmul(B_Y[:, 0:w], W2s[:, e, m, :], hg_ring[:, q % 3, 0:w], start=False,
                                         stop=(e == E - 1 and m == M0 - 1)).then_inc(s["y_mm"], 1)

                for e in range(E):
                    for m in range(M0):
                        q = (c * E + e) * M0 + m
                        at(pe, "h_relu", q - 2)
                        if c and q == c * E * M0:
                            at(pe, "hw_set", 2 * 4 * c)
                        nc.tensor.matmul(B_H[q % 3][:, 0:w], W1s[:, e, m * P:(m + 1) * P], zT[:, cols(c)],
                                         start=True, stop=True).then_inc(s["h_ps"], 1)
                    at(pe, "h_gated", (c * E + e) * M0)
                    nc.tensor.matmul(B_GATE[:, 0:w], ident[0:E, e:e + 1].to_broadcast([E, P]), GT0[0:E, 0:w],
                                     start=True, stop=True).then_inc(s["gate_ps"], 1)
                    if e:
                        down(e - 1)
                    if c + 1 < C:
                        for j in SHARE[e]:
                            piece((c + 1) * T + j)
                down(E - 1)
                if c + 1 < C:
                    ln_mean(1, c + 1)
                    ln_var(1, c + 1)
                ln_mean(2, c)
                ln_var(2, c)
                normed(2, c)
                for i, t in enumerate(tiles(c)):
                    mm = nc.tensor.transpose(B_MISC[:, i * P:(i + 1) * P], zT[:, t * P:(t + 1) * P], ident[:, :])
                mm.then_inc(s["htok_ps"], 1)
                for t in tiles(c):
                    at(pe, "hw_set", 2 * (t - 2))
                    if t < 3 * (c + 1) or True:
                        at(pe, "h_relu", (c + 1) * E * M0)
                    nc.tensor.matmul(B_H[t % 3][:, 0:K * P + 6], zT[:, t * P:(t + 1) * P], wcat,
                                     start=True, stop=True).then_inc(s["hw_ps"], 1)
            at(pe, "htok_set", C)
            pe.wait_ge(s["u18_set"], 2)
            pe.wait_ge(s["offdiag_set"], T)
            for p in range(PIECES):
                c, j = divmod(p, T)
                r, w = rows(j), width(c)
                if j == 0:
                    at(pe, "ns_set", c)
                    at(pe, "e18_set", c)
                ns = nc.tensor.matmul(B_G[:, 0:w], hTok[0:r, j, :], adjT[0:r, j, cols(c)], start=(j == 0), stop=(j == T - 1))
                if j == T - 1:
                    ns.then_inc(s["ns_mm"], 1)
                for sign in range(2):
                    at(pe, "mask_set", 2 * p + sign + 1)
                    mm = nc.tensor.matmul(B_Y[0:18, 0:w], u18[0:r, j, sign, :], masks[0:r, p % 2, sign, 0:w],
                                          start=(j == 0 and sign == 0), stop=(j == T - 1 and sign == 1))
                mm.then_inc(s["mask_used"], 1)

            def gru(n, c, src, deb_after):
                g, w = n * C + c, width(c)
                at(pe, "gru_n", g)
                if g == 0:
                    at(pe, "hw_set", 2 * T)
                hz = zT[:, cols(c)]
                for b, i in ((B_R, 0), (B_Z, 1)):
                    nc.tensor.matmul(b[:, 0:w], gruw[:, 0, i * P:(i + 1) * P], src, start=True, stop=False)
                    nc.tensor.matmul(b[:, 0:w], gruw[:, 1, i * P:(i + 1) * P], hz, start=False, stop=True)
                nc.tensor.matmul(B_NI[:, 0:w], gruw[:, 0, 2 * P:3 * P], src, start=True, stop=True)
                nc.tensor.matmul(B_NH[:, 0:w], gruw[:, 1, 2 * P:3 * P], hz, start=True, stop=True).then_inc(s["gru_ps"], 1)
                deb_after()
                for i, t in enumerate(tiles(c)):
                    r = rows(t)
                    mm = nc.tensor.matmul(B_LN[:, i * P:i * P + r], dcol[0:r, t:t + 1].to_broadcast([r, P]), ident[0:r, 0:r],
                                          start=True, stop=True)
                mm.then_inc(s["deb_ps"], 1)

            pe.wait_ge(s["edge_w_in"], 96)
            pe.wait_ge(s["dcol_set"], T)
            for c in range(C):
                at(pe, "ns_set", c + 1)
                gru(0, c, nsT[:, cols(c)], lambda c=c: at(pe, "x_edge", c))
            at(pe, "e18_set", C)
            pe.wait_ge(s["x_edge"], C)
            for g in range(K * T + 2):
                if g < K * T and g % T == 0:
                    k = g // T
                    for i in range(2 * C):
                        c = i // 2
                        n = 2 * C * k + i
                        at(pe, "eb_set", n)
                        nc.tensor.matmul(B_LN[:, 0:width(c)], sel6[0:18, (i % 2) * K + k:(i % 2) * K + k + 1].to_broadcast([18, P]),
                                         e18[:, cols(c)], start=True, stop=True).then_inc(s["eb_ps"], 1)
                if 1 <= g <= K * T:
                    h = g - 1
                    r = rows(h % T)
                    at(pe, "q_set", h + 1)
                    for v in range(3):
                        at(pe, "tr_set", 3 * (h - 1) + v + 1)
                        for i in range(min(4, T - 4 * v)):
                            j = 4 * v + i
                            mm = nc.tensor.transpose(B_H[v][:, i * P:i * P + r], S[0:r, h % 2, j * P:(j + 1) * P], ident[0:r, 0:r])
                        mm.then_inc(s["tr_ps"], 1)
                if g >= 2:
                    h = g - 2
                    k, t = divmod(h, T)
                    if t % 4 == 3 or t == T - 1:
                        c = t // 4
                        w = width(c)
                        at(pe, "tr_set", 3 * (h + 1))
                        for j in range(T):
                            r = rows(j)
                            mm = nc.tensor.matmul(B_ACC[c][:, 0:w], hW[0:r, j, k * P:(k + 1) * P], qT[0:r, (k * C + c) % 2, j, 0:w],
                                                  start=(k == 0 and j == 0), stop=(k == K - 1 and j == T - 1))
                        mm.then_inc(s["gat_mm"], 1)
            pe.wait_ge(s["node_w_in"], 32)
            for c in range(C):
                at(pe, "es_set", c + 1)
                gru(1, c, gt_node[:, 5, 0:width(c)], lambda c=c: at(pe, "ln_z", LN_AT[3, c]))
                ln_mean(3, c)
                ln_var(3, c)
            pe.wait_ge(s["ffn1a_in"], 32)
            pe.wait_ge(s["ffn1b_in"], 16 * M1)
            pe.wait_ge(s["rw_in"], 16)
            for c in range(C):
                w = width(c)
                at(pe, "f1_gt", c)
                normed(3, c)
                for i, t in enumerate(tiles(c)):
                    mm = nc.tensor.matmul(B_MISC[:, i * E:(i + 1) * E], zT[:, t * P:(t + 1) * P], rw, start=True, stop=True)
                mm.then_inc(s["f1_logits"], 1)
                at(pe, "route_step", C + c + 1)
                for i, t in enumerate(tiles(c)):
                    mm = nc.tensor.transpose(B_MISC[0:E, i * P:(i + 1) * P], rt[:, 3, i * E:(i + 1) * E], ident[:, :])
                mm.then_inc(s["f1_gtps"], 1)
                at(pe, "f1_gt", c + 1)
                at(pe, "x4_ready", c)

                def down1(q):
                    e, m = divmod(q - c * E * M1, M1)
                    r = min(P, H1 - m * P)
                    at(pe, "f1_m", q + 1)
                    nc.tensor.matmul(B_G[:, 0:w], w2s[0:r, e, m, :], hm_ring[0:r, q % 3, 0:w], start=(e == 0 and m == 0),
                                     stop=(e == E - 1 and m == M1 - 1)).then_inc(s["f1_y"], 1)

                for e in range(E):
                    for m in range(M1):
                        q = (c * E + e) * M1 + m
                        r = min(P, H1 - m * P)
                        if m == 0:
                            at(pe, "f1_sg", q)
                            nc.tensor.matmul(B_GATE[:, 0:w], ident[0:E, e:e + 1].to_broadcast([E, P]), GT1[0:E, 0:w],
                                             start=True, stop=True).then_inc(s["f1_gate"], 1)
                        at(pe, "f1_silu", q - 1)
                        nc.tensor.matmul(B_H[q % 2][0:r, 0:w], w1s[:, e, m * P:m * P + r], zT[:, cols(c)],
                                         start=True, stop=True).then_inc(s["f1_h1"], 1)
                        at(pe, "f1_m", q - 1)
                        b3 = (B_H[2], B_Y)[q % 2]
                        nc.tensor.matmul(b3[0:r, 0:w], w3s[:, e, m * P:m * P + r], zT[:, cols(c)],
                                         start=True, stop=True).then_inc(s["f1_h3"], 1)
                        if q - 1 >= c * E * M1:
                            down1(q - 1)
                down1((c + 1) * E * M1 - 1)

        @block.vector
        def _(dve):
            def ln_center(l, c):
                n, w = LN_AT[l, c], width(c)
                at(dve, "ln_mean", n + 1)
                at(dve, "ln_z", n)
                nc.vector.tensor_tensor(xc_ring[:, n % 2, 0:w], xT[:, cols(c)], B_LN[:, 0:w], ALU.subtract).then_inc(s["ln_xc"], 1)

            def ln_scale(l, c):
                n, w = LN_AT[l, c], width(c)
                y, t = yb[:, 0:w], tb[:, 0:w]
                at(dve, "ln_y0", n + 1)
                nc.vector.tensor_tensor(t, y, y, ALU.mult).then_inc(s["ln_step"], 1)
                at(dve, "ln_step", 4 * n + 1)
                nc.vector.scalar_tensor_tensor(out=t, in0=B_LN[:, 0:w], scalar=1.0e-5, in1=t, op0=ALU.add,
                                               op1=ALU.mult).then_inc(s["ln_step"], 1)
                at(dve, "ln_step", 4 * n + 2)
                nc.vector.tensor_scalar(t, t, -0.5, 1.5, ALU.mult, ALU.add).then_inc(s["ln_step"], 1)
                at(dve, "ln_step", 4 * n + 3)
                nc.vector.tensor_tensor(t, t, y, ALU.mult).then_inc(s["ln_step"], 1)
                at(dve, "ln_step", 4 * n + 4)
                nc.vector.tensor_tensor(zT[:, cols(c)], xc_ring[:, n % 2, 0:w], t, ALU.mult).then_inc(s["ln_z"], 1)

            def recip(p):
                c, j = divmod(p, T)
                r, w = rows(j), width(c)
                at(dve, f"adjT_in{c}", 32)
                at(dve, "sens_sq", p - 2)
                y = y_ring[0:r, p % 3, 0:w]
                nc.vector.tensor_scalar(y, adjT[0:r, j, cols(c)], 1.0e-18, None, ALU.add).then_inc(s["r_set"], 1)
                at(dve, "r_set", p + 1)
                nc.vector.reciprocal(y, y).then_inc(s["recip_done"], 1)

            def piece(p):
                if p + 1 < PIECES:
                    recip(p + 1)
                c, j = divmod(p, T)
                r, w = rows(j), width(c)
                at(dve, "sens_exp", p + 1)
                at(dve, "l0_mm", p - 2)
                nc.vector.scalar_tensor_tensor(out=w_ring[0:r, p % 3, 0:w], in0=adjT[0:r, j, cols(c)], scalar=1.0,
                                               in1=s_ring[0:r, p % 2, 0:w], op0=ALU.is_lt, op1=ALU.mult).then_inc(s["w_ready"], 1)

            step = [0]

            def link(ins):
                step[0] += 1
                ins.then_inc(s["q_step"], 1)
                dve.wait_ge(s["q_step"], step[0])

            def route(c, rk, on_probs, n, gt, logits, gtps, gtset):
                k = len(tiles(c))
                L, D, X, G = (rt[:, i, 0:k * E].rearrange("p (t e) -> p t e", t=k) for i in (2, 0, 1, 3))
                m1, m2 = rs[:, 0, 0:k], rs[:, 1, 0:k]
                at(dve, logits, c + 1)
                link(nc.vector.tensor_copy(L, B_MISC[:, 0:k * E].rearrange("p (t e) -> p t e", t=k)))
                link(nc.vector.tensor_reduce(m1, L, AX.X, ALU.max))
                nc.vector.tensor_tensor(D, L, m1.unsqueeze(2).to_broadcast([P, k, E]), ALU.subtract).then_inc(s["route_d"], 1)
                if on_probs:
                    at(dve, "route_e", n + 1)
                    link(nc.vector.tensor_reduce(m1, X, AX.X, ALU.add))
                    link(nc.vector.reciprocal(m2, m1))
                    link(nc.vector.tensor_tensor(L, X, m2.unsqueeze(2).to_broadcast([P, k, E]), ALU.mult))
                g4 = [rk[:, i, 0:k * E * E].rearrange("p (t e f) -> p t e f", t=k, e=E) for i in range(2)]
                other = L.unsqueeze(2).to_broadcast([P, k, E, E])
                own = L.unsqueeze(3).to_broadcast([P, k, E, E])
                link(nc.vector.tensor_tensor(g4[0], other, own, ALU.is_gt))
                link(nc.vector.tensor_tensor(g4[1], other, own, ALU.is_ge))
                link(nc.vector.tensor_tensor(g4[1], g4[1], tri[:, :, :].unsqueeze(1).to_broadcast([P, k, E, E]), ALU.mult))
                link(nc.vector.tensor_tensor(g4[0], g4[0], g4[1], ALU.max))
                link(nc.vector.tensor_reduce(D if on_probs else G, g4[0], AX.X, ALU.add))
                if on_probs:
                    link(nc.vector.scalar_tensor_tensor(out=G, in0=D, scalar=2.0, in1=L, op0=ALU.is_lt, op1=ALU.mult))
                    link(nc.vector.tensor_reduce(m1, G, AX.X, ALU.add))
                    link(nc.vector.tensor_scalar(m1, m1, 1.0e-9, None, ALU.add))
                else:
                    at(dve, "route_e", n + 1)
                    link(nc.vector.scalar_tensor_tensor(out=G, in0=G, scalar=2.0, in1=X, op0=ALU.is_lt, op1=ALU.mult))
                    link(nc.vector.tensor_reduce(m1, G, AX.X, ALU.add))
                link(nc.vector.reciprocal(m2, m1))
                nc.vector.tensor_tensor(G, G, m2.unsqueeze(2).to_broadcast([P, k, E]), ALU.mult).then_inc(s["route_step"], 1)
                at(dve, gtps, c + 1)
                nc.vector.tensor_copy(gt[0:E, 0:k * P], B_MISC[0:E, 0:k * P]).then_inc(s[gtset], 1)

            dve.wait_ge(s["x_in"], 16)
            ln_center(0, 0)
            recip(0)
            dve.wait_ge(s["wts0_in"], 64)
            nc.vector.tensor_tensor(rowW[0:1, P:P + E], rowW[0:1, P:P + E], rowW[0:1, P + E:P + 2 * E],
                                    ALU.add).then_inc(s["bgs_set"], 1)
            ln_scale(0, 0)
            for c in range(1, C):
                ln_center(0, c)
                ln_scale(0, c)
            for p in range(T):
                piece(p)

            def x1(c):
                at(dve, "l0_mm", T * (c + 1))
                nc.vector.tensor_tensor(xT[:, cols(c)], xT[:, cols(c)], B_G[:, 0:width(c)], ALU.add).then_inc(s["x1_ready"], 1)

            x1(0)
            ln_center(1, 0)
            ln_scale(1, 0)
            for c in range(C):
                w = width(c)
                if c == 0:
                    dve.wait_ge(s["v_ps"], 1)
                    nc.vector.tensor_copy(wcat[:, 3 * P:3 * P + 6].rearrange("p (h k) -> p k h", h=2),
                                          B_MISC[:, 0:6].rearrange("p (k h) -> p k h", h=2)).then_inc(s["v_set"], 1)
                    dve.wait_ge(s["const_set"], 6)
                route(c, rk0, False, c, GT0, "logits_ps", "gt_ps", "gt_set")
                for e in range(E):
                    at(dve, "gate_ps", c * E + e + 1)
                    for m in range(M0):
                        q = (c * E + e) * M0 + m
                        at(dve, "h_relu", q + 1)
                        at(dve, "y_mm", q - 2)
                        nc.vector.tensor_tensor(hg_ring[:, q % 3, 0:w], hr_ring[:, q % 3, 0:w], B_GATE[:, 0:w],
                                                ALU.mult).then_inc(s["h_gated"], 1)
                    if c + 1 < C:
                        for j in SHARE[e]:
                            piece((c + 1) * T + j)
                at(dve, "y_mm", (c + 1) * E * M0)
                nc.vector.tensor_tensor(xT[:, cols(c)], xT[:, cols(c)], B_Y[:, 0:w], ALU.add).then_inc(s["x2_ready"], 1)
                if c + 1 < C:
                    x1(c + 1)
                    ln_center(1, c + 1)
                    ln_scale(1, c + 1)
                ln_center(2, c)
                ln_scale(2, c)
            at(dve, "hw_set", 2 * T)
            usw = [u18[:, :, sg, :].rearrange("p t (r j) -> p t r j", r=PARTS) for sg in range(2)]
            for part in range(PARTS):
                src = u if part == 0 else ur
                link(nc.vector.tensor_copy(usw[0][:, :, part, :], src[:, :, :]))
                if part + 1 < PARTS:
                    link(nc.vector.tensor_tensor(ur[:, :, :], src[:, :, :], usw[0][:, :, part, :], ALU.subtract))
            for half in range(2):
                nc.vector.tensor_copy(usw[1][:, :, :, half * K:(half + 1) * K],
                                      usw[0][:, :, :, (1 - half) * K:(2 - half) * K]).then_inc(s["u18_set"], 1)
            dve.wait_ge(s["offdiag_set"], T)
            for p in range(PIECES):
                c, j = divmod(p, T)
                r, w = rows(j), width(c)
                at(dve, "mask_used", p - 1)
                for sign, op in ((0, ALU.is_gt), (1, ALU.is_lt)):
                    nc.vector.tensor_scalar(masks[0:r, p % 2, sign, 0:w], adjT[0:r, j, cols(c)], 0.0, None, op
                                            ).then_inc(s["mask_set"], 1)
                if j == T - 1:
                    at(dve, "mask_used", p + 1)
                    nc.vector.tensor_copy(e18[:, cols(c)], B_Y[0:18, 0:w]).then_inc(s["e18_set"], 1)
            dve.wait_ge(s["adjR_in"], 32)
            for t in range(T):
                r = rows(t)
                link(nc.vector.tensor_tensor_reduce(S[0:r, 0, 0:r], adjR[0:r, t, t * P:t * P + r], ident[0:r, 0:r], 1.0, 0.0,
                                                    ALU.mult, ALU.add, dcol[0:r, t:t + 1]))
                dve.sem_inc(s["dcol_set"], 1)
            dve.wait_ge(s["edge_w_in"], 96)
            for n in range(2):
                link(nc.vector.tensor_tensor(gru_c[:, n, 0:2], gru_b[:, n, 0, 0:2], gru_b[:, n, 1, 0:2], ALU.add))
                link(nc.vector.tensor_scalar(gru_c[:, n, 0:2], gru_c[:, n, 0:2], 0.5, None, ALU.mult))
                link(nc.vector.tensor_copy(gru_c[:, n, 2:3], gru_b[:, n, 0, 2:3]))
                link(nc.vector.tensor_copy(gru_c[:, n, 3:4], gru_b[:, n, 1, 2:3]))
            dve.sem_inc(s["gru_bias"], 1)
            dve.wait_ge(s["row_diag_set"], T)
            for t in range(T):
                r = rows(t)
                nc.vector.tensor_scalar(mb[0:r, t, :], adjR[0:r, t, :], 0.0, NEG, ALU.is_le, ALU.mult).then_inc(s["mb_set"], 1)

            def gru(n, c, tmp):
                g, w = n * C + c, width(c)
                tr, tz, a, nn, d, _ = (tmp[:, i, 0:w] for i in range(6))
                at(dve, "gru_t", 2 * (g + 1))
                link(nc.vector.tensor_scalar(tr, tr, 0.5, 0.5, ALU.mult, ALU.add))
                link(nc.vector.tensor_scalar(tz, tz, 0.5, 0.5, ALU.mult, ALU.add))
                link(nc.vector.scalar_tensor_tensor(out=a, in0=B_NH[:, 0:w], scalar=gru_c[:, n, 3:4], in1=tr, op0=ALU.add, op1=ALU.mult))
                nc.vector.tensor_tensor(a, a, B_NI[:, 0:w], ALU.add).then_inc(s["gru_a"], 1)
                at(dve, "gru_n", g + 1)
                link(nc.vector.tensor_tensor(d, zT[:, cols(c)], nn, ALU.subtract))
                link(nc.vector.tensor_tensor(d, d, tz, ALU.mult))
                link(nc.vector.tensor_tensor(d, d, nn, ALU.add))
                at(dve, "deb_ps", g + 1)
                link(nc.vector.tensor_tensor(d, d, B_LN[:, 0:w], ALU.mult))
                nc.vector.tensor_tensor(xT[:, cols(c)], xT[:, cols(c)], d, ALU.add).then_inc(s["x_edge" if n == 0 else "x3_ready"], 1)

            for c in range(C):
                gru(0, c, gt_edge)

            def attend(g):
                t = g % T
                r = rows(t)
                at(dve, "p_set", g + 1)
                link(nc.vector.reciprocal(rden[0:r, g:g + 1], den[0:r, g:g + 1]))
                row = S[0:r, g % 2, 0:N]
                nc.vector.scalar_tensor_tensor(out=row, in0=row, scalar=rden[0:r, g:g + 1], in1=adjR[0:r, t, :],
                                               op0=ALU.mult, op1=ALU.mult).then_inc(s["q_set"], 1)

            dve.wait_ge(s["spad_set"], 1)
            dve.wait_ge(s["mb_set"], T)
            for g in range(K * T + 1):
                if g < K * T:
                    k, t = divmod(g, T)
                    r = rows(t)
                    if t == 0:
                        for i in range(2 * C):
                            c = i // 2
                            n = 2 * C * k + i
                            at(dve, "eb_fifth", n + 1)
                            dst = (eplus, eminus)[i % 2][:, cols(c)]
                            nc.vector.tensor_tensor(dst, dst, B_LN[:, 0:width(c)], ALU.max).then_inc(s["eb_set"], 1)
                        at(dve, "eb_set", 2 * C * (k + 1))
                    at(dve, "tr_ps", 3 * (g - 1))
                    row = S[0:r, g % 2, 0:N]
                    nc.vector.tensor_tensor_reduce(row, eplus[0:r, :], mb[0:r, t, :], 1.0, -3.0e38,
                                                   ALU.add, ALU.max, mx[0:r, g:g + 1]).then_inc(s["s_step"], 1)
                    link(nc.vector.tensor_scalar(mbneg[0:r, :], adjR[0:r, t, :], 0.0, NEG, ALU.is_ge, ALU.mult))
                    link(nc.vector.tensor_tensor_reduce(S2[0:r, :], eminus[0:r, :], mbneg[0:r, :], 1.0, -3.0e38,
                                                        ALU.add, ALU.max, mx2[0:r, g:g + 1]))
                    at(dve, "s_step", g + 1)
                    link(nc.vector.tensor_tensor(row, row, S2[0:r, :], ALU.max))
                    link(nc.vector.tensor_tensor(mx[0:r, g:g + 1], mx[0:r, g:g + 1], mx2[0:r, g:g + 1], ALU.max))
                    nc.vector.tensor_scalar(negm[0:r, g:g + 1], mx[0:r, g:g + 1], -1.0, None, ALU.mult).then_inc(s["s_set"], 1)
                if g:
                    attend(g - 1)
            for c in range(C):
                gru(1, c, gt_node)
                ln_center(3, c)
                ln_scale(3, c)
            for c in range(C):
                w = width(c)
                route(c, rk1, True, C + c, GT1, "f1_logits", "f1_gtps", "f1_gt")
                for e in range(E):
                    for m in range(M1):
                        q = (c * E + e) * M1 + m
                        r = min(P, H1 - m * P)
                        at(dve, "f1_gate", c * E + e + 1)
                        at(dve, "f1_silu", q + 1)
                        at(dve, "f1_m", q - 2)
                        nc.vector.tensor_tensor(hg1_ring[0:r, q % 3, 0:w], s1_ring[0:r, q % 3, 0:w], B_GATE[0:r, 0:w],
                                                ALU.mult).then_inc(s["f1_sg"], 1)
                        at(dve, "f1_sg", q + 1)
                        at(dve, "f1_h3", q + 1)
                        at(dve, "f1_y", q - 2)
                        b3 = (B_H[2], B_Y)[q % 2]
                        nc.vector.tensor_tensor(hm_ring[0:r, q % 3, 0:w], hg1_ring[0:r, q % 3, 0:w], b3[0:r, 0:w],
                                                ALU.mult).then_inc(s["f1_m"], 1)
                at(dve, "f1_y", (c + 1) * E * M1)
                nc.vector.tensor_tensor(xT[:, cols(c)], xT[:, cols(c)], B_G[:, 0:w], ALU.add).then_inc(s["x4_ready"], 1)


def kernel(**inputs):
    import numpy as _np
    import concourse.bacc as _bacc
    from concourse import mybir as _mybir
    from concourse.bass_utils import run_bass_kernel_spmd as _run

    g = {k: _np.asarray(v) for k, v in inputs.items()}

    def cols3(b):
        return b.reshape(3, 128).transpose(1, 0)

    laid = {
        "xT": g["x"].transpose(1, 0),
        "adjT": g["adj"].transpose(1, 0),
        "adj": g["adj"],
        "W": g["L0_gnn_W"],
        "B": g["L0_gnn_B"].reshape(1, -1),
        "Wg": g["L0_ffn_Wg"],
        "bg": g["L0_ffn_bg"].reshape(1, -1),
        "bias": g["L0_ffn_bias"].reshape(1, -1),
        "W1": g["L0_ffn_W1"],
        "b1": g["L0_ffn_b1"].reshape(16, 128).transpose(1, 0),
        "W2": g["L0_ffn_W2"],
        "b2": g["L0_ffn_b2"],
        "gW": g["L1_gnn_gat_W"],
        "gWT": g["L1_gnn_gat_W"].transpose(2, 0, 1),
        "ga": g["L1_gnn_gat_a"].reshape(6, 128).transpose(1, 0),
        "eWih": g["L1_gnn_edge_Wih"].transpose(1, 0),
        "eWhh": g["L1_gnn_edge_Whh"].transpose(1, 0),
        "ebih": cols3(g["L1_gnn_edge_bih"]),
        "ebhh": cols3(g["L1_gnn_edge_bhh"]),
        "nWih": g["L1_gnn_node_Wih"].transpose(1, 0),
        "nWhh": g["L1_gnn_node_Whh"].transpose(1, 0),
        "nbih": cols3(g["L1_gnn_node_bih"]),
        "nbhh": cols3(g["L1_gnn_node_bhh"]),
        "rw": g["L1_ffn_router_w"].transpose(1, 0),
        "w1": g["L1_ffn_w1"].transpose(2, 0, 1),
        "w3": g["L1_ffn_w3"].transpose(2, 0, 1),
        "w2": g["L1_ffn_w2"].transpose(2, 0, 1),
    }
    nc = _bacc.Bacc("TRN2", target_bir_lowering=False, num_devices=1)
    arrays, args = {}, []
    for name, a in laid.items():
        a = _np.ascontiguousarray(a)
        arrays[f"in_{name}"] = a
        args.append(nc.dram_tensor(f"in_{name}", a.shape, _mybir.dt.from_np(a.dtype), kind="ExternalInput").ap())
    args.append(nc.dram_tensor("outT", (128, 1354), _mybir.dt.float32, kind="ExternalOutput").ap())
    build(nc, *args)
    r = _run(nc, [arrays], core_ids=[0])
    return _np.ascontiguousarray(r.results[0]["outT"].transpose(1, 0))
```

```python
from contextlib import ExitStack

import concourse.bass as bass
from concourse import mybir

F32 = mybir.dt.float32
F32R = mybir.dt.float32r
BF16 = mybir.dt.bfloat16
I32 = mybir.dt.int32
ALU = mybir.AluOpType
ACT = mybir.ActivationFunctionType
AX = mybir.AxisListType

P = 128
N = 1354
T = -(-N // P)
NP = T * P
CW = 512
C = -(-N // CW)
E = 8
H0 = 256
M0 = H0 // P
H1 = 341
M1 = -(-H1 // P)
K = 3
NONE = 1.0e30
SIGN = -(1 << 31)
PARTS = 3


def rows(t):
    return min(P, N - t * P)


def width(c):
    return min(CW, N - c * CW)


def cols(c):
    return slice(c * CW, c * CW + width(c))


def tiles(c):
    return range(c * CW // P, min(T, (c + 1) * CW // P))



TILES0 = C * E * M0
LAG0 = 3
RING0 = 6
TILES1 = C * E * M1
LAG1 = 3
RING1 = 5
PIECES = C * T


def beside(c, e):
    out = []
    if c >= 1:
        if e == 2:
            out += [("center", 2, c - 1)]
        if e == 3:
            out += [("scale", 2, c - 1)]
        if e == 4:
            out += [("htok", c - 1)]
        if e in (5, 6):
            out += [("hw", t) for t in tiles(c - 1)[2 * (e - 5):2 * (e - 5) + 2]]
    if c + 1 < C:
        if e < 6:
            out += [("piece", (c + 1) * T + j) for j in range(2 * e, min(2 * e + 2, T))]
        if e == 5:
            out += [("x1", c + 1), ("center", 1, c + 1)]
        if e == 6:
            out += [("scale", 1, c + 1)]
        if e == 7:
            out += [("route", c + 1)]
    return out


LN_ORDER = [(0, c) for c in range(C)] + [(1, 0)]
LN_ORDER += [x[1:] for c in range(C) for e in range(E) for x in beside(c, e) if x[0] == "center"]
LN_ORDER += [(2, C - 1)] + [(3, c) for c in range(C)]
LN_AT = {key: n for n, key in enumerate(LN_ORDER)}
assert [x[1:] for c in range(C) for e in range(E) for x in beside(c, e) if x[0] == "scale"] == LN_ORDER[C + 1:-1 - C]


def build(nc, xT_d, adjT_d, adj_d, W_d, B_d, Wg_d, bg_d, bias_d, W1_d, b1_d, W2_d, b2_d,
          gW_d, gWT_d, ga_d, eWih_d, eWhh_d, ebih_d, ebhh_d, nWih_d, nWhh_d, nbih_d, nbhh_d,
          rw_d, w1_d, w3_d, w2_d, out_d):
    with ExitStack() as ctx:
        def sb(name, shape, dt=F32):
            return ctx.enter_context(nc.sbuf_tensor(name, shape, dt))

        def sem(name):
            return ctx.enter_context(nc.semaphore(name))

        def place(slot, bytes_, variants):
            out = []
            for variant in variants:
                used = 0
                with ExitStack() as inner:
                    for name, shape, dt in variant:
                        out.append(inner.enter_context(nc.sbuf_tensor(name, shape, dt)))
                        n = 2 if dt == BF16 else 4
                        for d in shape[1:]:
                            n *= d
                        used += n
                assert used <= bytes_, (slot, used, bytes_)
            sb(slot, [P, bytes_ // 4])
            return out

        xT = sb("xT", [P, N])
        zT = sb("zT", [P, NP])
        gruw = sb("gruw", [P, 2, 3 * P])
        hTok = sb("hTok", [P, T, P])
        regL = sb("regL", [P, 6 * CW])
        regR = sb("regR", [P, 1030])
        ident = sb("ident", [P, P])
        sel6 = sb("sel6", [P, 6])
        sel16f = sb("sel16f", [16, E])
        sel16 = sb("sel16", [16, E], F32R)
        tri = sb("tri", [P, E, E])
        one = sb("one", [P, 1])
        meanw = sb("meanw", [P, 1])
        eps = sb("eps", [P, 1])
        tiny = sb("tiny", [P, 1])
        rowW = sb("rowW", [1, P + 2 * E])
        gru_b = sb("gru_b", [P, 2, 2, 3])
        gru_c = sb("gru_c", [P, 2, 4])
        b1c = sb("b1c", [P, E * M0])
        ga = sb("ga", [P, 2 * K])
        u18 = sb("u18", [P, T, 2, 18], BF16)
        dcol = sb("dcol", [P, T])
        lowest = sb("lowest", [P, K * T])
        low2 = sb("low2", [P, 2])
        den = sb("den", [P, K * T])
        rden = sb("rden", [P, K * T])
        rt = sb("rt", [P, 4, 4 * E])
        g16 = sb("g16", [P, 4, 16], F32R)
        rs = sb("rs", [P, 2, 4])
        negsum = sb("negsum", [P, T])
        negtot = sb("negtot", [P, 1])
        flag = sb("flag", [1, 1], I32)

        (adjT, qT, S_a, gt_edge, gt_node, z3hi, z3lo, s1_ring, m1_ring, GT1, rw) = place("slotA", T * N * 4, [
            [("adjT", [P, T, N], F32)],
            [("qT", [P, 2, T, CW], F32), ("S_a", [P, 2, NP], F32)],
            [("gt_edge", [P, 6, CW], F32)],
            [("gt_node", [P, 6, CW], F32), ("z3hi", [P, N], F32R), ("z3lo", [P, N], F32R),
             ("s1_ring", [P, 4, CW], F32), ("m1_ring", [P, RING1, CW], F32), ("GT1", [16, C, CW], F32R),
             ("rw", [P, E], F32)],
        ])
        (W1hi, W1lo, W2s, zhi, zlo, a_ring, t_ring, hr_ring, msg, GT0, Wl0, Wg, wcat, gWT, b2x, b2hi, b2lo,
         adjR, mb, w13hi, w13lo, w2s, padX, w13) = place("slotB", T * N * 6, [
            [("W1hi", [P, E, H0], F32R), ("W1lo", [P, E, H0], F32R), ("W2s", [P, E, M0, P], F32),
             ("zhi", [P, 2, CW], F32R), ("zlo", [P, 2, CW], F32R), ("a_ring", [P, 3, CW], F32),
             ("t_ring", [P, 3, CW], F32), ("hr_ring", [P, RING0, CW], F32), ("msg", [P, T, P], F32),
             ("GT0", [16, CW], F32R), ("Wl0", [P, P], F32), ("Wg", [P, E], F32), ("wcat", [P, 3 * P + 6], F32),
             ("gWT", [P, K, P], F32), ("b2x", [16, P], F32), ("b2hi", [16, P], F32R), ("b2lo", [16, P], F32R)],
            [("adjR", [P, T, N], F32), ("mb", [P, T, N], BF16)],
            [("w13hi", [P, E, 2, H1], F32R), ("w13lo", [P, E, 2, H1], F32R), ("w2s", [P, E, M1, P], F32),
             ("padX", [P, T * N - 4 * E * H1 - E * M1 * P], F32), ("w13", [P, E, 2, H1], F32)],
        ])
        (W1f, hW) = place("slotH", T * K * P * 4, [
            [("W1f", [P, E, H0], F32)],
            [("hW", [P, T, K * P], F32)],
        ])
        (w_ring, masks, eplus) = place("slotE", N * 4, [
            [("w_ring", [P, 2, CW], F32)],
            [("masks", [P, 2, N], BF16)],
            [("eplus", [P, N], F32)],
        ])
        xc_ring = regL[:, 0:2 * CW].rearrange("p (r n) -> p r n", r=2)
        y_ring = regL[:, 2 * CW:4 * CW].rearrange("p (r n) -> p r n", r=2)
        v_ring = regL[:, 4 * CW:6 * CW].rearrange("p (r n) -> p r n", r=2)
        e18 = regL[0:18, 0:N]
        nsT = regL[:, N:2 * N]
        eminus = nsT
        HALF = N // 2
        neg_row = regR[:, 0:HALF]
        neg_mask = regR[:, HALF:HALF + (HALF + 1) // 2].bitcast(BF16)
        rank = regR[:, 0:2 * 4 * E * E].rearrange("p (i n) -> p i n", i=2)
        u = regR[:, 512:512 + T * 6].rearrange("p (t j) -> p t j", t=T)
        ur = regR[:, 580:580 + T * 6].rearrange("p (t j) -> p t j", t=T)
        S = [S_a[:, 0, :], S_a[:, 1, :], hTok[:, :, :].rearrange("p t n -> p (t n)")]

        bk = [ctx.enter_context(nc.psum_tensor(f"bank{i}", [P, CW], F32)) for i in range(8)]
        B_SIDE = bk[0]
        B_GNN, B_Y0 = bk[2], bk[3]
        B_GATE = [bk[4], bk[1]]
        B_H = bk[5:8]
        B_MSG = [bk[1], bk[3], bk[4]]
        B_NS = bk[2:5]
        B_E18 = bk[5:8]
        B_ACC = bk[1:4]
        B_R, B_Z, B_NI, B_NH = bk[5], bk[6], bk[7], bk[4]
        B_H1, B_H3, B_Y1 = [bk[5], bk[6]], [bk[7], bk[3]], bk[2]

        def ln_bank(l, c):
            return B_H[c] if l == 0 else B_SIDE

        names = """x_in adjT_in0 adjT_in1 adjT_in2 adjR_in0 adjR_in1 adjR_in2 wts0_in W1_in ffn0_in gat_in gru_in node_in
            w13_in w2_in rw_in out_done const_raw const_set zpad_set sel16_set
            ln_mean ln_xc ln_sq ln_var ln_log ln_y0 ln_step ln_z z_hi z_split
            bgs_set W1_split b2_split msg_ps msg_set
            r2_log y0_set y0_sign newton_t newton_y sens_arg sens_exp w_ready gnn_mm
            x1_ready x2_ready x3_ready x4_ready
            logits_ps logits_read route_d route_e route_step gates_set gt_ps gt_set
            gate_ps h_ps h_relu h_gated y_mm v_ps v_set htok_ps htok_set hw_ps hw_set u_step u18_set
            offdiag_set mask_set mask_used ns_mm ns_set e18_set neg_acc neg_max neg_ps flag_set
            nmask_set nmask_used ne18_mm ne18_set
            eb_ps eb_fifth eb_set nb_ps nb_fifth nb_set mb_set dcol_set row_diag_set spad_set
            s_set neg_step p_set rden_set q_set tr_ps tr_set gat_mm es_set
            gru_ps gru_t gru_a gru_n gru_step deb_ps x_edge gru_bias
            w13_hi w13_lo gate1_ps h1_ps h3_ps s_silu s_gated m_set y1_mm""".split()
        s = {n: sem(n) for n in names}

        def at(eng, name, value):
            if value > 0:
                eng.wait_ge(s[name], value)

        block = ctx.enter_context(nc.Block())

        @block.sync
        def _(sp):
            def adjT_load(c):
                full = (T - 1) * P
                sp.dma_start(adjT[:, 0:T - 1, cols(c)],
                             adjT_d[0:full, cols(c)].rearrange("(t p) n -> p t n", p=P)).then_inc(s[f"adjT_in{c}"], 16)
                sp.dma_start(adjT[0:N - full, T - 1, cols(c)], adjT_d[full:N, cols(c)]).then_inc(s[f"adjT_in{c}"], 16)

            sp.dma_start(xT[:, :], xT_d).then_inc(s["x_in"], 16)
            sp.dma_start(Wl0[:, :], W_d).then_inc(s["wts0_in"], 16)
            sp.dma_start(rowW[0:1, 0:P], B_d).then_inc(s["wts0_in"], 16)
            sp.dma_start(rowW[0:1, P:P + E], bg_d).then_inc(s["wts0_in"], 16)
            sp.dma_start(rowW[0:1, P + E:P + 2 * E], bias_d).then_inc(s["wts0_in"], 16)
            adjT_load(0)
            sp.dma_start(W1f[:, :, :], W1_d.rearrange("e c h -> c e h")).then_inc(s["W1_in"], 16)
            sp.dma_start(Wg[:, :], Wg_d).then_inc(s["ffn0_in"], 16)
            sp.dma_start(W2s[:, :, :, :], W2_d.rearrange("e (m p) d -> p e m d", p=P)).then_inc(s["ffn0_in"], 16)
            sp.dma_start(b1c[:, :], b1_d).then_inc(s["ffn0_in"], 16)
            sp.dma_start(b2x[0:E, :], b2_d).then_inc(s["ffn0_in"], 16)
            sp.dma_start(b2x[E:2 * E, :], b2_d).then_inc(s["ffn0_in"], 16)
            adjT_load(1)
            adjT_load(2)
            sp.dma_start(wcat[:, 0:3 * P].rearrange("p (k d) -> p k d", k=K),
                         gW_d.rearrange("k c d -> c k d")).then_inc(s["gat_in"], 16)
            sp.dma_start(gWT[:, :, :], gWT_d).then_inc(s["gat_in"], 16)
            sp.dma_start(ga[:, :], ga_d).then_inc(s["gat_in"], 16)
            for n, (bi, bh) in enumerate([(ebih_d, ebhh_d), (nbih_d, nbhh_d)]):
                sp.dma_start(gru_b[:, n, 0, :], bi).then_inc(s["gru_in"], 16)
                sp.dma_start(gru_b[:, n, 1, :], bh).then_inc(s["gru_in"], 16)
            sp.dma_start(gruw[:, 0, :], eWih_d).then_inc(s["gru_in"], 16)
            sp.dma_start(gruw[:, 1, :], eWhh_d).then_inc(s["gru_in"], 16)
            sp.wait_ge(s["x2_ready"], C)
            sp.wait_ge(s["hw_ps"], T)
            for t in range(T):
                sp.dma_start(adjR[0:rows(t), t, :], adj_d[t * P:t * P + rows(t), :]).then_inc(s[f"adjR_in{t // 4}"], 16)
            sp.wait_ge(s["x_edge"], C)
            sp.dma_start(gruw[:, 0, :], nWih_d).then_inc(s["node_in"], 16)
            sp.dma_start(gruw[:, 1, :], nWhh_d).then_inc(s["node_in"], 16)
            sp.wait_ge(s["s_set"], K * T)
            sp.dma_start(w13[:, :, 0, :], w1_d).then_inc(s["w13_in"], 16)
            sp.dma_start(w13[:, :, 1, :], w3_d).then_inc(s["w13_in"], 16)
            sp.wait_ge(s["q_set"], K * T)
            for m in range(M1):
                r = min(P, H1 - m * P)
                sp.dma_start(w2s[0:r, :, m, :], w2_d[m * P:m * P + r, :, :]).then_inc(s["w2_in"], 16)
            sp.wait_ge(s["gat_mm"], K * C)
            sp.dma_start(rw[:, :], rw_d).then_inc(s["rw_in"], 16)
            for c in range(C):
                sp.wait_ge(s["x4_ready"], c + 1)
                sp.dma_start(out_d[:, cols(c)], xT[:, cols(c)]).then_inc(s["out_done"], 16)
            sp.wait_ge(s["out_done"], 16 * C)

        @block.gpsimd
        def _(pool):
            raw = [(ident[:, :], 0.0), (sel6[:, :], 0.0), (sel16f[:, :], 0.0), (tri[:, :, :], 1.0), (one[:, :], 1.0),
                   (meanw[:, :], 1.0 / P), (eps[:, :], 1.0e-5), (tiny[:, :], 1.0e-19)]
            for ap, value in raw:
                pool.memset(ap, value).then_inc(s["const_raw"], 1)
            pool.memset(zT[:, N:NP], 0.0).then_inc(s["zpad_set"], 1)
            pool.wait_ge(s["const_raw"], len(raw))
            pool.affine_select(out=ident[:, :], in_=ident[:, :], compare_op=ALU.not_equal, fill=1.0,
                               base=0, pattern=[[-1, P]], channel_multiplier=1).then_inc(s["const_set"], 1)
            pool.affine_select(out=tri[:, :, :], in_=tri[:, :, :], compare_op=ALU.is_gt, fill=0.0,
                               base=0, pattern=[[1, E], [-1, E]], channel_multiplier=0).then_inc(s["const_set"], 1)
            n = 2
            for ap, k, parts in ((sel16f, E, 2), (sel6, 6, PARTS)):
                for part in range(parts):
                    pool.affine_select(out=ap[:, :], in_=ap[:, :], compare_op=ALU.not_equal, fill=1.0, base=-k * part,
                                       pattern=[[-1, k]], channel_multiplier=1).then_inc(s["const_set"], 1)
                    n += 1
                    pool.wait_ge(s["const_set"], n)
            pool.wait_ge(s["w_ready"], PIECES)
            for t in range(T):
                r = rows(t)
                blk = adjT[0:r, t, t * P:t * P + r]
                pool.affine_select(out=blk, in_=blk, compare_op=ALU.not_equal, fill=0.0, base=0, pattern=[[-1, r]],
                                   channel_multiplier=1).then_inc(s["offdiag_set"], 1)
            for t in range(T):
                r = rows(t)
                blk = adjR[0:r, t, t * P:t * P + r]
                pool.wait_ge(s["dcol_set"], t + 1)
                pool.wait_ge(s["neg_acc"], t + 1)
                pool.affine_select(out=blk, in_=blk, compare_op=ALU.not_equal, fill=0.0, base=0, pattern=[[-1, r]],
                                   channel_multiplier=1).then_inc(s["row_diag_set"], 1)
            pool.wait_ge(s["x_edge"], 1)
            for i in range(2):
                pool.memset(S[i][:, N:NP], 0.0).then_inc(s["spad_set"], 1)
            pool.memset(S[2][:, N:NP], 0.0).then_inc(s["spad_set"], 1)

        CONSTS = 2 + 2 + PARTS

        @block.scalar
        def _(act):
            def ln_square(l, c):
                n, w = LN_AT[l, c], width(c)
                at(act, "ln_xc", n + 1)
                at(act, "ln_z", n - 1)
                nc.scalar.activation(y_ring[:, n % 2, 0:w], xc_ring[:, n % 2, 0:w], ACT.Square).then_inc(s["ln_sq"], 1)

            def ln_rsqrt(l, c):
                n, w = LN_AT[l, c], width(c)
                at(act, "ln_var", n + 1)
                nc.scalar.activation(v_ring[:, n % 2, 0:w], ln_bank(l, c)[:, 0:w], ACT.Ln, bias=eps[:, 0:1]).then_inc(s["ln_log"], 1)
                at(act, "ln_log", n + 1)
                nc.scalar.activation(y_ring[:, n % 2, 0:w], v_ring[:, n % 2, 0:w], ACT.Exp, scale=-0.5).then_inc(s["ln_y0"], 1)

            def first_reciprocal(p):
                if p >= PIECES:
                    return
                c, j = divmod(p, T)
                r, w = rows(j), width(c)
                a = a_ring[0:r, p % 3, 0:w]
                if j == 0:
                    at(act, f"adjT_in{c}", 32)
                at(act, "newton_y", p - 2)
                nc.scalar.activation(a, adjT[0:r, j, cols(c)], ACT.Square).then_inc(s["r2_log"], 1)
                at(act, "r2_log", 2 * p + 1)
                nc.scalar.activation(a, a, ACT.Ln, bias=tiny[0:r, 0:1]).then_inc(s["r2_log"], 1)
                at(act, "r2_log", 2 * p + 2)
                nc.scalar.activation(a, a, ACT.Exp, scale=-0.5).then_inc(s["y0_set"], 1)

            def sensitivity(p):
                if p >= PIECES:
                    return
                c, j = divmod(p, T)
                t = t_ring[0:rows(j), p % 3, 0:width(c)]
                at(act, "newton_y", p + 1)
                nc.scalar.activation(t, t, ACT.Square, bias=one[0:rows(j), 0:1]).then_inc(s["sens_arg"], 1)
                at(act, "sens_arg", p + 1)
                nc.scalar.activation(t, t, ACT.Exp, scale=-2.0).then_inc(s["sens_exp"], 1)

            def h_tokens(c):
                at(act, "htok_ps", c + 1)
                k = len(tiles(c))
                nc.scalar.copy(hTok[:, c * 4:c * 4 + k, :], B_SIDE[:, 0:k * P]).then_inc(s["htok_set"], 1)

            def head_products(t):
                at(act, "hw_ps", t + 1)
                if t == 0:
                    at(act, "W1_split", 2)
                nc.scalar.copy(hW[:, t, :], B_SIDE[:, 0:K * P]).then_inc(s["hw_set"], 1)
                nc.scalar.copy(u[:, t, :], B_SIDE[:, K * P:K * P + 6]).then_inc(s["hw_set"], 1)

            def router_exp(n):
                at(act, "route_d", n + 1)
                k = len(tiles(n % C)) * E
                nc.scalar.activation(rt[:, 1, 0:k], rt[:, 0, 0:k], ACT.Exp).then_inc(s["route_e"], 1)

            def side(task):
                kind = task[0]
                if kind == "piece":
                    first_reciprocal(task[1] + 2)
                    sensitivity(task[1] + 1)
                elif kind == "center":
                    ln_square(*task[1:])
                elif kind == "scale":
                    ln_rsqrt(*task[1:])
                elif kind == "route":
                    router_exp(task[1])
                elif kind == "htok":
                    h_tokens(task[1])
                elif kind == "hw":
                    head_products(task[1])

            act.preload_act_table_set("natural_log_exp_and_others")
            act.wait_ge(s["const_set"], CONSTS)
            ln_square(0, 0)
            ln_square(0, 1)
            ln_rsqrt(0, 0)
            first_reciprocal(0)
            ln_square(0, 2)
            ln_rsqrt(0, 1)
            first_reciprocal(1)
            ln_rsqrt(0, 2)
            sensitivity(0)
            for c in range(C):
                at(act, "msg_ps", c + 1)
                k = len(tiles(c))
                nc.scalar.copy(msg[:, c * 4:c * 4 + k, :], B_MSG[c][:, 0:k * P]).then_inc(s["msg_set"], 1)
            for p in range(T):
                side(("piece", p))
            side(("center", 1, 0))
            side(("scale", 1, 0))
            side(("route", 0))
            for q in range(TILES0):
                c, e, m = q // (E * M0), q // M0 % E, q % M0
                w = width(c)
                at(act, "h_ps", q + 1)
                at(act, "y_mm", q - RING0 + 1)
                nc.scalar.activation(hr_ring[:, q % RING0, 0:w], B_H[q % 3][:, 0:w], ACT.Relu,
                                     bias=b1c[:, e * M0 + m:e * M0 + m + 1]).then_inc(s["h_relu"], 1)
                if m == M0 - 1:
                    for task in beside(c, e):
                        side(task)
            side(("center", 2, C - 1))
            side(("scale", 2, C - 1))
            side(("htok", C - 1))
            for t in tiles(C - 1):
                side(("hw", t))
            act.preload_act_table_set("exp_and_others")
            for c in range(C):
                at(act, "ns_mm", c + 1)
                nc.scalar.copy(nsT[:, cols(c)], B_NS[c][:, 0:width(c)]).then_inc(s["ns_set"], 1)
            for t in range(T):
                r = rows(t)
                at(act, f"adjR_in{t // 4}", 16 * len(tiles(t // 4)))
                at(act, "neg_acc", t)
                nc.scalar.activation(mb[0:r, t, :], adjR[0:r, t, :], ACT.Relu, scale=-1.0,
                                     accum_out=negsum[0:r, t:t + 1]).then_inc(s["neg_acc"], 1)

            def gru(n, c, tmp, src):
                g, w = n * C + c, width(c)
                if n == 1:
                    at(act, "gat_mm", (K - 1) * C + c + 1)
                    at(act, "gru_ps", g if c else 0)
                    nc.scalar.mul(src, B_ACC[c][:, 0:w], 1.0 / K).then_inc(s["es_set"], 1)
                at(act, "gru_ps", g + 1)
                at(act, "x3_ready" if n else "x_edge", c)
                nc.scalar.activation(tmp[:, 0, 0:w], B_R[:, 0:w], ACT.Tanh, scale=0.5,
                                     bias=gru_c[:, n, 0:1]).then_inc(s["gru_t"], 1)
                nc.scalar.activation(tmp[:, 1, 0:w], B_Z[:, 0:w], ACT.Tanh, scale=0.5,
                                     bias=gru_c[:, n, 1:2]).then_inc(s["gru_t"], 1)
                at(act, "gru_a", g + 1)
                nc.scalar.activation(tmp[:, 3, 0:w], tmp[:, 2, 0:w], ACT.Tanh,
                                     bias=gru_c[:, n, 2:3]).then_inc(s["gru_n"], 1)

            at(act, "flag_set", 1)
            any_negative = act.value_load(flag[0:1, 0:1], min_val=0, max_val=1)

            def score_rows(k):
                for c in range(C):
                    at(act, "eb_ps", C * k + c + 1)
                    if c == 0:
                        at(act, "s_set", T * k)
                        at(act, "mask_used", T)
                    nc.scalar.mul(eplus[:, cols(c)], B_SIDE[:, 0:width(c)], -0.2).then_inc(s["eb_fifth"], 1)
                with act.If(any_negative == 1):
                    for c in range(C):
                        at(act, "nb_ps", C * k + c + 1)
                        nc.scalar.mul(eminus[:, cols(c)], B_SIDE[:, 0:width(c)], -0.2).then_inc(s["nb_fifth"], 1)

            at(act, "gru_bias", 1)
            for c in range(C):
                gru(0, c, gt_edge, None)
            for g in range(K * T + 1):
                if g < K * T and g % T == 0:
                    score_rows(g // T)
                if g < K * T:
                    r = rows(g % T)
                    at(act, "s_set", g + 1)
                    row = S[g % 3][0:r, 0:N]
                    nc.scalar.activation(row, row, ACT.Exp, bias=lowest[0:r, g:g + 1], scale=-1.0,
                                         accum_out=den[0:r, g:g + 1]).then_inc(s["p_set"], 1)
                if g >= 1:
                    h = g - 1
                    k, t = divmod(h, T)
                    r, c = rows(t), t // 4
                    if h == 0:
                        at(act, "x_edge", C)
                    for v in range(3):
                        at(act, "tr_ps", 3 * h + v + 1)
                        if t % 4 == 0 and v == 0:
                            at(act, "gat_mm", k * C + c - 1)
                        nb = min(4, T - 4 * v)
                        nc.scalar.copy(qT[:, (k * C + c) % 2, 4 * v:4 * v + nb, (t % 4) * P:(t % 4) * P + r],
                                       B_H[v][:, 0:nb * P].rearrange("p (b i) -> p b i", b=nb)[:, :, 0:r]
                                       ).then_inc(s["tr_set"], 1)
            at(act, "gat_mm", K * C)
            for c in range(C):
                gru(1, c, gt_node, gt_node[:, 5, 0:width(c)])
                if c:
                    ln_square(3, c - 1)
                for e in range(c * E // C, (c + 1) * E // C):
                    at(act, "w13_in", 32)
                    at(act, "q_set", K * T)
                    nc.scalar.copy(w13hi[:, e, :, :], w13[:, e, :, :]).then_inc(s["w13_hi"], 1)
            act.preload_act_table_set("natural_log_exp_and_others")
            ln_rsqrt(3, 0)
            ln_square(3, C - 1)
            for c in range(1, C):
                ln_rsqrt(3, c)
            for c in range(C):
                router_exp(C + c)
            for q in range(TILES1):
                c, m = q // (E * M1), q % M1
                r, w = min(P, H1 - m * P), width(c)
                at(act, "h1_ps", q + 1)
                at(act, "m_set", q - 3)
                nc.scalar.activation(s1_ring[0:r, q % 4, 0:w], B_H1[q % 2][0:r, 0:w], ACT.Silu).then_inc(s["s_silu"], 1)

        @block.tensor
        def _(pe):
            side_free = [("ln_z", 0)]

            def take_side(name, count):
                at(pe, *side_free[0])
                side_free[0] = (name, count)

            def exact(out, w, x, start, stop):
                (whi, wlo), (xhi, xlo) = w, x
                nc.tensor.matmul(out, whi, xhi, start=start, stop=False)
                nc.tensor.matmul(out, whi, xlo, start=False, stop=False)
                return nc.tensor.matmul(out, wlo, xhi, start=False, stop=stop)

            def ln_mean(l, c):
                n, w = LN_AT[l, c], width(c)
                at(pe, ["x_in", "x1_ready", "x2_ready", "x3_ready"][l], c + 1 if l else 16)
                if l:
                    take_side("ln_xc", n + 1)
                nc.tensor.matmul(ln_bank(l, c)[:, 0:w], meanw[:, 0:1].to_broadcast([P, P]), xT[:, cols(c)],
                                 start=True, stop=True).then_inc(s["ln_mean"], 1)

            def ln_var(l, c):
                n, w = LN_AT[l, c], width(c)
                if l:
                    take_side("ln_z", n + 1)
                at(pe, "ln_sq", n + 1)
                nc.tensor.matmul(ln_bank(l, c)[:, 0:w], meanw[:, 0:1].to_broadcast([P, P]), y_ring[:, n % 2, 0:w],
                                 start=True, stop=True).then_inc(s["ln_var"], 1)

            def piece(p):
                c, j = divmod(p, T)
                r, w = rows(j), width(c)
                at(pe, "w_ready", p + 1)
                if j == 0:
                    at(pe, "x1_ready", c)
                    at(pe, "msg_set", C)
                nc.tensor.matmul(B_GNN[:, 0:w], msg[0:r, j, :], w_ring[0:r, p % 2, 0:w],
                                 start=(j == 0), stop=(j == T - 1)).then_inc(s["gnn_mm"], 1)

            def route(n):
                l, c = divmod(n, C)
                at(pe, "ln_z", LN_AT[2 * l + 1, c] + 1)
                take_side("logits_read", n + 1)
                for i, t in enumerate(tiles(c)):
                    o = B_SIDE[:, i * E:(i + 1) * E]
                    mm = nc.tensor.matmul(o, zT[:, t * P:(t + 1) * P], (Wg, rw)[l][:, :], start=True, stop=(l == 1))
                    if l == 0:
                        mm = nc.tensor.matmul(o, one[0:1, 0:1].to_broadcast([1, P]), rowW[0:1, P:P + E], start=False, stop=True)
                mm.then_inc(s["logits_ps"], 1)
                at(pe, "gates_set", n + 1)
                take_side("gt_set", n + 1)
                for i, t in enumerate(tiles(c)):
                    mm = nc.tensor.transpose(B_SIDE[0:16, i * P:(i + 1) * P], g16[:, i, :].bitcast(F32), ident[:, :])
                mm.then_inc(s["gt_ps"], 1)

            def h_tokens(c):
                at(pe, "ln_z", LN_AT[2, c] + 1)
                take_side("htok_set", c + 1)
                for i, t in enumerate(tiles(c)):
                    mm = nc.tensor.transpose(B_SIDE[:, i * P:(i + 1) * P], zT[:, t * P:(t + 1) * P], ident[:, :])
                mm.then_inc(s["htok_ps"], 1)

            def head_products(t):
                take_side("hw_set", 2 * (t + 1))
                nc.tensor.matmul(B_SIDE[:, 0:K * P + 6], zT[:, t * P:(t + 1) * P], wcat[:, :],
                                 start=True, stop=True).then_inc(s["hw_ps"], 1)

            def side(task):
                kind = task[0]
                if kind == "piece":
                    piece(task[1])
                elif kind == "center":
                    ln_mean(*task[1:])
                elif kind == "scale":
                    ln_var(*task[1:])
                elif kind == "route":
                    route(task[1])
                elif kind == "htok":
                    h_tokens(task[1])
                elif kind == "hw":
                    head_products(task[1])

            pe.wait_ge(s["const_set"], CONSTS)
            pe.wait_ge(s["zpad_set"], 1)
            ln_mean(0, 0)
            ln_mean(0, 1)
            ln_var(0, 0)
            ln_mean(0, 2)
            ln_var(0, 1)
            ln_var(0, 2)
            pe.wait_ge(s["wts0_in"], 64)
            for c in range(C):
                at(pe, "ln_z", c + 1)
                for i, t in enumerate(tiles(c)):
                    o = B_MSG[c][:, i * P:(i + 1) * P]
                    nc.tensor.matmul(o, zT[:, t * P:(t + 1) * P], Wl0[:, :], start=True, stop=False)
                    mm = nc.tensor.matmul(o, one[0:1, 0:1].to_broadcast([1, P]), rowW[0:1, 0:P], start=False, stop=True)
                mm.then_inc(s["msg_ps"], 1)
            pe.wait_ge(s["gat_in"], 48)
            for k in range(K):
                mm = nc.tensor.matmul(B_SIDE[:, 2 * k:2 * k + 2], gWT[:, k, :], ga[:, 2 * k:2 * k + 2], start=True, stop=True)
            mm.then_inc(s["v_ps"], 1)
            side_free[0] = ("v_set", 1)
            for p in range(T):
                piece(p)
            side(("center", 1, 0))
            side(("scale", 1, 0))
            pe.wait_ge(s["ffn0_in"], 80)
            pe.wait_ge(s["bgs_set"], 1)
            side(("route", 0))
            at(pe, "W1_split", 2)
            at(pe, "b2_split", 2)
            at(pe, "sel16_set", 1)

            def down(q):
                c, e, m = q // (E * M0), q // M0 % E, q % M0
                w = width(c)
                if e == 0 and m == 0:
                    at(pe, "x2_ready", c)
                    nc.tensor.matmul(B_Y0[:, 0:w], b2hi[:, :], GT0[:, 0:w], start=True, stop=False)
                    nc.tensor.matmul(B_Y0[:, 0:w], b2lo[:, :], GT0[:, 0:w], start=False, stop=False)
                at(pe, "h_gated", q + 1)
                nc.tensor.matmul(B_Y0[:, 0:w], W2s[:, e, m, :], hr_ring[:, q % RING0, 0:w], start=False,
                                 stop=(e == E - 1 and m == M0 - 1)).then_inc(s["y_mm"], 1)

            for q in range(TILES0):
                c, e, m = q // (E * M0), q // M0 % E, q % M0
                w = width(c)
                if e == 0 and m == 0:
                    at(pe, "gt_set", c + 1)
                    at(pe, "z_split", c + 1)
                    if q == 0:
                        at(pe, "msg_set", C)
                if m == 0:
                    at(pe, "h_gated", (q // M0 - 1) * M0)
                    nc.tensor.matmul(B_GATE[q // M0 % 2][:, 0:w], sel16[:, e:e + 1].to_broadcast([16, P]), GT0[:, 0:w],
                                     start=True, stop=True).then_inc(s["gate_ps"], 1)
                at(pe, "h_relu", q - 2)
                exact(B_H[q % 3][:, 0:w], (W1hi[:, e, m * P:(m + 1) * P], W1lo[:, e, m * P:(m + 1) * P]),
                      (zhi[:, c % 2, 0:w], zlo[:, c % 2, 0:w]), True, True).then_inc(s["h_ps"], 1)
                if q >= LAG0:
                    down(q - LAG0)
                if m == M0 - 1:
                    for task in beside(c, e):
                        side(task)
            for q in range(TILES0 - LAG0, TILES0):
                down(q)

            def neighbours(j):
                r = rows(j)
                at(pe, "offdiag_set", j + 1)
                at(pe, "htok_set", j // 4 + 1)
                if j == 0:
                    at(pe, "x2_ready", C)
                for c in range(C):
                    ns = nc.tensor.matmul(B_NS[c][:, 0:width(c)], hTok[0:r, j, :], adjT[0:r, j, cols(c)],
                                          start=(j == 0), stop=(j == T - 1))
                    if j == T - 1:
                        ns.then_inc(s["ns_mm"], 1)
                at(pe, "u18_set", 2 * (j // 4 + 1))
                at(pe, "mask_set", j + 1)
                for c in range(C):
                    mm = nc.tensor.matmul(B_E18[c][0:18, 0:width(c)], u18[0:r, j, 0, :], masks[0:r, j % 2, cols(c)],
                                          start=(j == 0), stop=(j == T - 1))
                mm.then_inc(s["mask_used"], 1)

            side(("center", 2, C - 1))
            neighbours(0)
            side(("scale", 2, C - 1))
            for j in range(1, 4):
                neighbours(j)
            side(("htok", C - 1))
            for i, t in enumerate(tiles(C - 1)):
                side(("hw", t))
                neighbours(4 + i)
            for j in range(4 + len(tiles(C - 1)), T):
                neighbours(j)
            at(pe, "neg_max", 1)
            take_side("flag_set", 1)
            nc.tensor.matmul(B_SIDE[0:1, 0:1], negtot[:, 0:1], one[:, 0:1], start=True, stop=True).then_inc(s["neg_ps"], 1)
            at(pe, "flag_set", 1)
            any_negative = pe.value_load(flag[0:1, 0:1], min_val=0, max_val=1)
            at(pe, "e18_set", C)
            with pe.If(any_negative == 1):
                for j in range(T):
                    r = rows(j)
                    at(pe, "nmask_set", j + 1)
                    for c in range(C):
                        mm = nc.tensor.matmul(B_E18[c][0:18, 0:width(c)], u18[0:r, j, 1, :], masks[0:r, j % 2, cols(c)],
                                              start=(j == 0), stop=(j == T - 1))
                    mm.then_inc(s["nmask_used"], 1)
                at(pe, "ne18_set", C)

            def score_rows(k):
                for c in range(C):
                    take_side("eb_set", C * k + c + 1)
                    nc.tensor.matmul(B_SIDE[:, 0:width(c)], sel6[0:18, k:k + 1].to_broadcast([18, P]),
                                     e18[:, cols(c)], start=True, stop=True).then_inc(s["eb_ps"], 1)
                with pe.If(any_negative == 1):
                    for c in range(C):
                        at(pe, "eb_set", C * (k + 1))
                        at(pe, "nb_set", C * k + c)
                        nc.tensor.matmul(B_SIDE[:, 0:width(c)], sel6[0:18, K + k:K + k + 1].to_broadcast([18, P]),
                                         e18[:, cols(c)], start=True, stop=True).then_inc(s["nb_ps"], 1)
                    at(pe, "nb_set", C * (k + 1))

            def gru(n, c, src):
                g, w = n * C + c, width(c)
                at(pe, "gru_n", g)
                at(pe, "gru_a", g)
                hz = zT[:, cols(c)]
                for b, i in ((B_R, 0), (B_Z, 1)):
                    nc.tensor.matmul(b[:, 0:w], gruw[:, 0, i * P:(i + 1) * P], src, start=True, stop=False)
                    nc.tensor.matmul(b[:, 0:w], gruw[:, 1, i * P:(i + 1) * P], hz, start=False, stop=True)
                nc.tensor.matmul(B_NI[:, 0:w], gruw[:, 0, 2 * P:3 * P], src, start=True, stop=True)
                nc.tensor.matmul(B_NH[:, 0:w], gruw[:, 1, 2 * P:3 * P], hz, start=True, stop=True).then_inc(s["gru_ps"], 1)
                take_side("x3_ready" if n else "x_edge", c + 1)
                for i, t in enumerate(tiles(c)):
                    r = rows(t)
                    mm = nc.tensor.matmul(B_SIDE[:, i * P:i * P + r], dcol[0:r, t:t + 1].to_broadcast([r, P]),
                                          ident[0:r, 0:r], start=True, stop=True)
                mm.then_inc(s["deb_ps"], 1)

            pe.wait_ge(s["gru_in"], 96)
            at(pe, "dcol_set", T)
            at(pe, "ns_set", C)
            for c in range(C):
                gru(0, c, nsT[:, cols(c)])
            at(pe, "x_edge", C)
            at(pe, "gru_n", C)
            pe.wait_ge(s["spad_set"], 3)
            for g in range(K * T + 2):
                if g < K * T and g % T == 0:
                    score_rows(g // T)
                if 1 <= g <= K * T:
                    h = g - 1
                    r = rows(h % T)
                    at(pe, "q_set", h + 1)
                    for v in range(3):
                        at(pe, "tr_set", 3 * (h - 1) + v + 1)
                        for i in range(min(4, T - 4 * v)):
                            j = 4 * v + i
                            mm = nc.tensor.transpose(B_H[v][:, i * P:i * P + r], S[h % 3][0:r, j * P:(j + 1) * P], ident[0:r, 0:r])
                        mm.then_inc(s["tr_ps"], 1)
                if g >= 2:
                    h = g - 2
                    k, t = divmod(h, T)
                    if t % 4 == 3 or t == T - 1:
                        c = t // 4
                        w = width(c)
                        at(pe, "tr_set", 3 * (h + 1))
                        for j in range(T):
                            r = rows(j)
                            mm = nc.tensor.matmul(B_ACC[c][:, 0:w], hW[0:r, j, k * P:(k + 1) * P], qT[0:r, (k * C + c) % 2, j, 0:w],
                                                  start=(k == 0 and j == 0), stop=(k == K - 1 and j == T - 1))
                        mm.then_inc(s["gat_mm"], 1)
            pe.wait_ge(s["node_in"], 32)
            for c in range(C):
                at(pe, "es_set", c + 1)
                gru(1, c, gt_node[:, 5, 0:width(c)])
                if c:
                    side(("center", 3, c - 1))
            side(("scale", 3, 0))
            side(("center", 3, C - 1))
            for c in range(1, C):
                side(("scale", 3, c))
            pe.wait_ge(s["rw_in"], 16)
            for c in range(C):
                route(C + c)
            pe.wait_ge(s["w2_in"], 16 * M1)

            def down1(q):
                c, e, m = q // (E * M1), q // M1 % E, q % M1
                r, w = min(P, H1 - m * P), width(c)
                first = e == 0 and m == 0
                if first:
                    at(pe, "x4_ready", c)
                at(pe, "m_set", q + 1)
                nc.tensor.matmul(B_Y1[:, 0:w], w2s[0:r, e, m, :], m1_ring[0:r, q % RING1, 0:w], start=first,
                                 stop=(e == E - 1 and m == M1 - 1)).then_inc(s["y1_mm"], 1)

            for q in range(TILES1):
                c, e, m = q // (E * M1), q // M1 % E, q % M1
                r, w = min(P, H1 - m * P), width(c)
                if m == 0:
                    at(pe, "s_gated", (q // M1 - 1) * M1)
                    nc.tensor.matmul(B_GATE[q // M1 % 2][:, 0:w], sel16[:, e:e + 1].to_broadcast([16, P]), GT1[:, c, 0:w],
                                     start=True, stop=True).then_inc(s["gate1_ps"], 1)
                    if c == 0:
                        at(pe, "w13_lo", e + 1)
                    if e == 0:
                        at(pe, "z_split", C + c + 1)
                at(pe, "s_silu", q - 1)
                x = (z3hi[:, cols(c)], z3lo[:, cols(c)])
                f = slice(m * P, m * P + r)
                exact(B_H1[q % 2][0:r, 0:w], (w13hi[:, e, 0, f], w13lo[:, e, 0, f]), x, True, True).then_inc(s["h1_ps"], 1)
                at(pe, "m_set", q - 1)
                exact(B_H3[q % 2][0:r, 0:w], (w13hi[:, e, 1, f], w13lo[:, e, 1, f]), x, True, True).then_inc(s["h3_ps"], 1)
                if q >= LAG1:
                    down1(q - LAG1)
            for q in range(TILES1 - LAG1, TILES1):
                down1(q)

        @block.vector
        def _(dve):
            def ln_center(l, c):
                n, w = LN_AT[l, c], width(c)
                at(dve, "ln_mean", n + 1)
                at(dve, "ln_z", n - 1)
                nc.vector.tensor_tensor(xc_ring[:, n % 2, 0:w], xT[:, cols(c)], ln_bank(l, c)[:, 0:w], ALU.subtract).then_inc(s["ln_xc"], 1)

            def ln_scale(l, c):
                n, w = LN_AT[l, c], width(c)
                y, t = y_ring[:, n % 2, 0:w], v_ring[:, n % 2, 0:w]
                at(dve, "ln_y0", n + 1)
                nc.vector.tensor_tensor(t, y, y, ALU.mult).then_inc(s["ln_step"], 1)
                at(dve, "ln_step", 4 * n + 1)
                nc.vector.scalar_tensor_tensor(out=t, in0=ln_bank(l, c)[:, 0:w], scalar=1.0e-5, in1=t, op0=ALU.add,
                                               op1=ALU.mult).then_inc(s["ln_step"], 1)
                at(dve, "ln_step", 4 * n + 2)
                nc.vector.tensor_scalar(t, t, -0.5, 1.5, ALU.mult, ALU.add).then_inc(s["ln_step"], 1)
                at(dve, "ln_step", 4 * n + 3)
                nc.vector.tensor_tensor(t, t, y, ALU.mult).then_inc(s["ln_step"], 1)
                at(dve, "ln_step", 4 * n + 4)
                if l == 1:
                    at(dve, "msg_ps", C)
                nc.vector.tensor_tensor(zT[:, cols(c)], xc_ring[:, n % 2, 0:w], t, ALU.mult).then_inc(s["ln_z"], 1)
                if l in (1, 3):
                    hi, lo = (zhi[:, c % 2, 0:w], zlo[:, c % 2, 0:w]) if l == 1 else (z3hi[:, cols(c)], z3lo[:, cols(c)])
                    k = c + (C if l == 3 else 0)
                    if l == 1:
                        at(dve, "h_ps", (c - 1) * E * M0)
                    at(dve, "ln_z", n + 1)
                    nc.vector.tensor_copy(hi, zT[:, cols(c)]).then_inc(s["z_hi"], 1)
                    at(dve, "z_hi", k + 1)
                    nc.vector.tensor_tensor(lo, zT[:, cols(c)], hi.bitcast(F32), ALU.subtract).then_inc(s["z_split"], 1)

            def newton(p):
                if p >= PIECES:
                    return
                c, j = divmod(p, T)
                r, w = rows(j), width(c)
                x, y, t = adjT[0:r, j, cols(c)], a_ring[0:r, p % 3, 0:w], t_ring[0:r, p % 3, 0:w]
                at(dve, "y0_set", p + 1)
                nc.vector.scalar_tensor_tensor(out=y.bitcast(I32), in0=x.bitcast(I32), scalar=SIGN, in1=y.bitcast(I32),
                                               op0=ALU.bitwise_and, op1=ALU.bitwise_or).then_inc(s["y0_sign"], 1)
                at(dve, "y0_sign", p + 1)
                at(dve, "w_ready", p - 2)
                nc.vector.tensor_tensor(t, x, y, ALU.mult).then_inc(s["newton_t"], 1)
                at(dve, "newton_t", p + 1)
                nc.vector.scalar_tensor_tensor(out=t, in0=t, scalar=2.0, in1=y, op0=ALU.subtract, op1=ALU.mult
                                               ).then_inc(s["newton_y"], 1)

            def cutoff(p):
                c, j = divmod(p, T)
                r, w = rows(j), width(c)
                at(dve, "sens_exp", p + 1)
                at(dve, "gnn_mm", p - 1)
                nc.vector.scalar_tensor_tensor(out=w_ring[0:r, p % 2, 0:w], in0=adjT[0:r, j, cols(c)], scalar=1.0,
                                               in1=t_ring[0:r, p % 3, 0:w], op0=ALU.is_lt, op1=ALU.mult).then_inc(s["w_ready"], 1)

            step = [0]

            def link(ins):
                step[0] += 1
                ins.then_inc(s["route_step"], 1)
                dve.wait_ge(s["route_step"], step[0])

            def x1(c):
                at(dve, "gnn_mm", T * (c + 1))
                nc.vector.tensor_tensor(xT[:, cols(c)], xT[:, cols(c)], B_GNN[:, 0:width(c)], ALU.add).then_inc(s["x1_ready"], 1)

            def route(n):
                l, c = divmod(n, C)
                k = len(tiles(c))
                L, D, X, G = (rt[:, i, 0:k * E].rearrange("p (t e) -> p t e", t=k) for i in (2, 0, 1, 3))
                m1, m2 = rs[:, 0, 0:k], rs[:, 1, 0:k]
                at(dve, "logits_ps", n + 1)
                nc.vector.tensor_copy(L, B_SIDE[:, 0:k * E].rearrange("p (t e) -> p t e", t=k)).then_inc(s["logits_read"], 1)
                at(dve, "logits_read", n + 1)
                link(nc.vector.tensor_reduce(m1, L, AX.X, ALU.max))
                at(dve, "route_e", n)
                nc.vector.tensor_tensor(D, L, m1.unsqueeze(2).to_broadcast([P, k, E]), ALU.subtract).then_inc(s["route_d"], 1)
                if l:
                    at(dve, "route_e", n + 1)
                    link(nc.vector.tensor_reduce(m1, X, AX.X, ALU.add))
                    link(nc.vector.reciprocal(m2, m1))
                    link(nc.vector.tensor_tensor(L, X, m2.unsqueeze(2).to_broadcast([P, k, E]), ALU.mult))
                g4 = [rank[:, i, 0:k * E * E].rearrange("p (t e f) -> p t e f", t=k, e=E) for i in range(2)]
                other = L.unsqueeze(2).to_broadcast([P, k, E, E])
                own = L.unsqueeze(3).to_broadcast([P, k, E, E])
                link(nc.vector.tensor_tensor(g4[0], other, own, ALU.is_gt))
                link(nc.vector.tensor_tensor(g4[1], other, own, ALU.is_ge))
                link(nc.vector.tensor_tensor(g4[1], g4[1], tri[:, :, :].unsqueeze(1).to_broadcast([P, k, E, E]), ALU.mult))
                link(nc.vector.tensor_tensor(g4[0], g4[0], g4[1], ALU.max))
                link(nc.vector.tensor_reduce(G, g4[0], AX.X, ALU.add))
                if l:
                    link(nc.vector.scalar_tensor_tensor(out=G, in0=G, scalar=2.0, in1=L, op0=ALU.is_lt, op1=ALU.mult))
                    link(nc.vector.tensor_reduce(m1, G, AX.X, ALU.add))
                    link(nc.vector.tensor_scalar(m1, m1, 1.0e-9, None, ALU.add))
                else:
                    at(dve, "route_e", n + 1)
                    link(nc.vector.scalar_tensor_tensor(out=G, in0=G, scalar=2.0, in1=X, op0=ALU.is_lt, op1=ALU.mult))
                    link(nc.vector.tensor_reduce(m1, G, AX.X, ALU.add))
                link(nc.vector.reciprocal(m2, m1))
                link(nc.vector.tensor_tensor(G, G, m2.unsqueeze(2).to_broadcast([P, k, E]), ALU.mult))
                at(dve, "gt_ps", n)
                link(nc.vector.tensor_copy(g16[:, 0:k, 0:E], G))
                nc.vector.tensor_tensor(g16[:, 0:k, E:2 * E], G, g16[:, 0:k, 0:E].bitcast(F32), ALU.subtract).then_inc(s["gates_set"], 1)
                at(dve, "gt_ps", n + 1)
                gt = GT1[:, c, 0:k * P] if l else GT0[:, 0:k * P]
                if l == 0:
                    at(dve, "gate_ps", c * E)
                    at(dve, "y_mm", (c - 1) * E * M0 + 1)
                nc.vector.tensor_copy(gt, B_SIDE[0:16, 0:k * P]).then_inc(s["gt_set"], 1)

            usw = [u18[:, :, sg, :].rearrange("p t (r j) -> p t r j", r=PARTS) for sg in range(2)]

            def split_u(c):
                a, b = c * 4, c * 4 + len(tiles(c))
                at(dve, "hw_set", 2 * b)
                for part in range(PARTS):
                    src = (u if part == 0 else ur)[:, a:b, :]
                    link(nc.vector.tensor_copy(usw[0][:, a:b, part, :], src))
                    if part + 1 < PARTS:
                        link(nc.vector.tensor_tensor(ur[:, a:b, :], src, usw[0][:, a:b, part, :], ALU.subtract))
                for half in range(2):
                    nc.vector.tensor_copy(usw[1][:, a:b, :, half * K:(half + 1) * K],
                                          usw[0][:, a:b, :, (1 - half) * K:(2 - half) * K]).then_inc(s["u18_set"], 1)

            def side(task):
                kind = task[0]
                if kind == "piece":
                    newton(task[1] + 1)
                    cutoff(task[1])
                elif kind == "x1":
                    x1(task[1])
                elif kind == "center":
                    ln_center(*task[1:])
                elif kind == "scale":
                    ln_scale(*task[1:])
                elif kind == "route":
                    route(task[1])

            dve.wait_ge(s["x_in"], 16)
            ln_center(0, 0)
            ln_center(0, 1)
            dve.wait_ge(s["const_set"], CONSTS)
            nc.vector.tensor_copy(sel16[:, :], sel16f[:, :]).then_inc(s["sel16_set"], 1)
            ln_scale(0, 0)
            ln_center(0, 2)
            ln_scale(0, 1)
            newton(0)
            ln_scale(0, 2)
            dve.wait_ge(s["wts0_in"], 64)
            nc.vector.tensor_tensor(rowW[0:1, P:P + E], rowW[0:1, P:P + E], rowW[0:1, P + E:P + 2 * E],
                                    ALU.add).then_inc(s["bgs_set"], 1)
            for p in range(T):
                side(("piece", p))
                if p == 3:
                    dve.wait_ge(s["W1_in"], 16)
                    nc.vector.tensor_copy(W1hi[:, :, :], W1f[:, :, :]).then_inc(s["W1_split"], 1)
                if p == 5:
                    at(dve, "W1_split", 1)
                    nc.vector.tensor_tensor(W1lo[:, :, :], W1f[:, :, :], W1hi[:, :, :].bitcast(F32), ALU.subtract).then_inc(s["W1_split"], 1)
                if p == 7:
                    dve.wait_ge(s["ffn0_in"], 80)
                    nc.vector.tensor_copy(b2hi[:, :], b2x[:, :]).then_inc(s["b2_split"], 1)
                    at(dve, "b2_split", 1)
                    nc.vector.tensor_tensor(b2lo[:, :], b2x[:, :], b2hi[:, :].bitcast(F32), ALU.subtract).then_inc(s["b2_split"], 1)
                if p == 8:
                    dve.wait_ge(s["v_ps"], 1)
                    nc.vector.tensor_copy(wcat[:, 3 * P:3 * P + 6].rearrange("p (h k) -> p k h", h=2),
                                          B_SIDE[:, 0:6].rearrange("p (k h) -> p k h", h=2)).then_inc(s["v_set"], 1)
            x1(0)
            side(("center", 1, 0))
            side(("scale", 1, 0))
            side(("route", 0))

            def x2(c):
                at(dve, "y_mm", (c + 1) * E * M0)
                nc.vector.tensor_tensor(xT[:, cols(c)], xT[:, cols(c)], B_Y0[:, 0:width(c)], ALU.add).then_inc(s["x2_ready"], 1)

            for q in range(TILES0):
                c, e, m = q // (E * M0), q // M0 % E, q % M0
                w = width(c)
                at(dve, "gate_ps", q // M0 + 1)
                at(dve, "h_relu", q + 1)
                hr = hr_ring[:, q % RING0, 0:w]
                nc.vector.tensor_tensor(hr, hr, B_GATE[q // M0 % 2][:, 0:w], ALU.mult).then_inc(s["h_gated"], 1)
                if c and q % (E * M0) == LAG0:
                    x2(c - 1)
                if m == M0 - 1:
                    for task in beside(c, e):
                        side(task)
            x2(C - 1)

            def positive(j):
                r = rows(j)
                at(dve, "mask_used", j - 1)
                at(dve, "offdiag_set", j + 1)
                if j == 0:
                    at(dve, "gnn_mm", PIECES)
                nc.vector.tensor_scalar(masks[0:r, j % 2, :], adjT[0:r, j, :], 0.0, None, ALU.is_gt).then_inc(s["mask_set"], 1)

            side(("center", 2, C - 1))
            split_u(0)
            split_u(1)
            positive(0)
            side(("scale", 2, C - 1))
            for j in range(1, 4 + len(tiles(C - 1))):
                positive(j)
            split_u(C - 1)
            for j in range(4 + len(tiles(C - 1)), T):
                positive(j)
            for t in range(T):
                r = rows(t)
                at(dve, f"adjR_in{t // 4}", 16 * len(tiles(t // 4)))
                if t == 0:
                    at(dve, "ns_mm", C)
                if t:
                    at(dve, "dcol_set", t)
                nc.vector.tensor_tensor_reduce(rank[0:r, 0, 0:r], adjR[0:r, t, t * P:t * P + r], ident[0:r, 0:r], 1.0, 0.0,
                                               ALU.mult, ALU.add, dcol[0:r, t:t + 1]).then_inc(s["dcol_set"], 1)
            for c in range(C):
                at(dve, "mask_used", T)
                nc.vector.tensor_copy(e18[:, cols(c)], B_E18[c][0:18, 0:width(c)]).then_inc(s["e18_set"], 1)
            dve.wait_ge(s["gru_in"], 96)
            for n in range(2):
                link(nc.vector.tensor_tensor(gru_c[:, n, 0:2], gru_b[:, n, 0, 0:2], gru_b[:, n, 1, 0:2], ALU.add))
                link(nc.vector.tensor_scalar(gru_c[:, n, 0:2], gru_c[:, n, 0:2], 0.5, None, ALU.mult))
                link(nc.vector.tensor_copy(gru_c[:, n, 2:3], gru_b[:, n, 0, 2:3]))
                nc.vector.tensor_copy(gru_c[:, n, 3:4], gru_b[:, n, 1, 2:3]).then_inc(s["gru_bias"], 1)
            for t in range(T):
                r = rows(t)
                at(dve, "row_diag_set", t + 1)
                at(dve, "neg_acc", t + 1)
                nc.vector.tensor_scalar(mb[0:r, t, :], adjR[0:r, t, :], 0.0, NONE, ALU.is_le, ALU.mult).then_inc(s["mb_set"], 1)
            at(dve, "neg_acc", T)
            link(nc.vector.memset(negtot[:, :], 0.0))
            link(nc.vector.tensor_reduce(negtot[:, :], negsum[:, 0:T - 1], AX.X, ALU.max))
            nc.vector.tensor_tensor(negtot[0:rows(T - 1), :], negtot[0:rows(T - 1), :], negsum[0:rows(T - 1), T - 1:T],
                                    ALU.max).then_inc(s["neg_max"], 1)
            at(dve, "neg_ps", 1)
            nc.vector.tensor_scalar(flag[0:1, 0:1], B_SIDE[0:1, 0:1], 0.0, None, ALU.is_gt).then_inc(s["flag_set"], 1)
            at(dve, "flag_set", 1)
            any_negative = dve.value_load(flag[0:1, 0:1], min_val=0, max_val=1)
            with dve.If(any_negative == 1):
                for j in range(T):
                    r = rows(j)
                    at(dve, "nmask_used", j - 1)
                    nc.vector.tensor_scalar(masks[0:r, j % 2, :], adjT[0:r, j, :], 0.0, None, ALU.is_lt).then_inc(s["nmask_set"], 1)
                for c in range(C):
                    at(dve, "nmask_used", T)
                    at(dve, "e18_set", C)
                    nc.vector.tensor_tensor(e18[:, cols(c)], e18[:, cols(c)], B_E18[c][0:18, 0:width(c)], ALU.add).then_inc(s["ne18_set"], 1)

            def gru(n, c, tmp):
                g, w = n * C + c, width(c)
                tr, tz, a, nn, d, _ = (tmp[:, i, 0:w] for i in range(6))
                at(dve, "gru_t", 2 * (g + 1))
                link(nc.vector.tensor_scalar(tr, tr, 0.5, 0.5, ALU.mult, ALU.add))
                link(nc.vector.tensor_scalar(tz, tz, 0.5, 0.5, ALU.mult, ALU.add))
                link(nc.vector.scalar_tensor_tensor(out=a, in0=B_NH[:, 0:w], scalar=gru_c[:, n, 3:4], in1=tr, op0=ALU.add, op1=ALU.mult))
                nc.vector.tensor_tensor(a, a, B_NI[:, 0:w], ALU.add).then_inc(s["gru_a"], 1)
                at(dve, "gru_n", g + 1)
                link(nc.vector.tensor_tensor(d, zT[:, cols(c)], nn, ALU.subtract))
                link(nc.vector.tensor_tensor(d, d, tz, ALU.mult))
                link(nc.vector.tensor_tensor(d, d, nn, ALU.add))
                at(dve, "deb_ps", g + 1)
                link(nc.vector.tensor_tensor(d, d, B_SIDE[:, 0:w], ALU.mult))
                nc.vector.tensor_tensor(xT[:, cols(c)], xT[:, cols(c)], d, ALU.add).then_inc(s["x_edge" if n == 0 else "x3_ready"], 1)

            for c in range(C):
                gru(0, c, gt_edge)

            def leaky(dst, c, done, k):
                nc.vector.scalar_tensor_tensor(out=dst[:, cols(c)], in0=B_SIDE[:, 0:width(c)], scalar=-1.0, in1=dst[:, cols(c)],
                                               op0=ALU.mult, op1=ALU.min).then_inc(s[done], 1)

            def score_rows(k):
                for c in range(C):
                    at(dve, "eb_fifth", C * k + c + 1)
                    leaky(eplus, c, "eb_set", k)
                at(dve, "eb_set", C * (k + 1))
                with dve.If(any_negative == 1):
                    for c in range(C):
                        at(dve, "nb_fifth", C * k + c + 1)
                        leaky(eminus, c, "nb_set", k)
                    at(dve, "nb_set", C * (k + 1))

            def scores(g):
                t = g % T
                r = rows(t)
                row, low = S[g % 3][0:r, 0:N], lowest[0:r, g:g + 1]
                at(dve, "tr_ps", 3 * (g - 2))
                nc.vector.tensor_tensor_reduce(row, eplus[0:r, :], mb[0:r, t, :], 1.0, 3.0e38,
                                               ALU.add, ALU.min, low).then_inc(s["neg_step"], 1)
                at(dve, "neg_step", g + 1)
                with dve.If(any_negative == 1):
                    n = 8 * g
                    for i in range(2):
                        part = slice(i * HALF, (i + 1) * HALF)
                        for j, ins in enumerate([
                            lambda: nc.vector.tensor_scalar(neg_mask[0:r, 0:HALF], adjR[0:r, t, part], 0.0, NONE, ALU.is_ge, ALU.mult),
                            lambda: nc.vector.tensor_tensor_reduce(neg_row[0:r, :], eminus[0:r, part], neg_mask[0:r, 0:HALF], 1.0, 3.0e38,
                                                                   ALU.add, ALU.min, low2[0:r, i:i + 1]),
                            lambda: nc.vector.tensor_tensor(row[:, part], row[:, part], neg_row[0:r, :], ALU.min),
                            lambda: nc.vector.tensor_tensor(low, low, low2[0:r, i:i + 1], ALU.min),
                        ]):
                            ins().then_inc(s["u_step"], 1)
                            n += 1
                            at(dve, "u_step", n)
                dve.sem_inc(s["s_set"], 1)

            def attend(g):
                t = g % T
                r = rows(t)
                at(dve, "p_set", g + 1)
                nc.vector.reciprocal(rden[0:r, g:g + 1], den[0:r, g:g + 1]).then_inc(s["rden_set"], 1)
                at(dve, "rden_set", g + 1)
                row = S[g % 3][0:r, 0:N]
                nc.vector.scalar_tensor_tensor(out=row, in0=row, scalar=rden[0:r, g:g + 1], in1=adjR[0:r, t, :],
                                               op0=ALU.mult, op1=ALU.mult).then_inc(s["q_set"], 1)

            dve.wait_ge(s["mb_set"], T)
            for g in range(K * T + 1):
                if g < K * T:
                    if g % T == 0:
                        score_rows(g // T)
                    scores(g)
                if g:
                    attend(g - 1)
            for c in range(C):
                gru(1, c, gt_node)
                if c:
                    side(("center", 3, c - 1))
                for e in range(c * E // C, (c + 1) * E // C):
                    at(dve, "w13_hi", e + 1)
                    nc.vector.tensor_tensor(w13lo[:, e, :, :], w13[:, e, :, :], w13hi[:, e, :, :].bitcast(F32),
                                            ALU.subtract).then_inc(s["w13_lo"], 1)
            side(("scale", 3, 0))
            side(("center", 3, C - 1))
            for c in range(1, C):
                side(("scale", 3, c))
            for c in range(C):
                route(C + c)
            for q in range(TILES1):
                c, e, m = q // (E * M1), q // M1 % E, q % M1
                r, w = min(P, H1 - m * P), width(c)
                sg = s1_ring[0:r, q % 4, 0:w]
                at(dve, "gate1_ps", q // M1 + 1)
                at(dve, "s_silu", q + 1)
                nc.vector.tensor_tensor(sg, sg, B_GATE[q // M1 % 2][0:r, 0:w], ALU.mult).then_inc(s["s_gated"], 1)
                at(dve, "s_gated", q + 1)
                at(dve, "h3_ps", q + 1)
                at(dve, "y1_mm", q - RING1 + 1)
                nc.vector.tensor_tensor(m1_ring[0:r, q % RING1, 0:w], sg, B_H3[q % 2][0:r, 0:w], ALU.mult).then_inc(s["m_set"], 1)
                if c and q % (E * M1) == LAG1 - 1:
                    at(dve, "y1_mm", c * E * M1)
                    nc.vector.tensor_tensor(xT[:, cols(c - 1)], xT[:, cols(c - 1)], B_Y1[:, 0:width(c - 1)], ALU.add).then_inc(s["x4_ready"], 1)
            at(dve, "y1_mm", TILES1)
            nc.vector.tensor_tensor(xT[:, cols(C - 1)], xT[:, cols(C - 1)], B_Y1[:, 0:width(C - 1)], ALU.add).then_inc(s["x4_ready"], 1)


def kernel(**inputs):
    import numpy as _np
    import concourse.bacc as _bacc
    from concourse import mybir as _mybir
    from concourse.bass_utils import run_bass_kernel_spmd as _run

    g = {k: _np.asarray(v) for k, v in inputs.items()}

    def cols3(b):
        return b.reshape(3, 128).transpose(1, 0)

    laid = {
        "xT": g["x"].transpose(1, 0),
        "adjT": g["adj"].transpose(1, 0),
        "adj": g["adj"],
        "W": g["L0_gnn_W"],
        "B": g["L0_gnn_B"].reshape(1, -1),
        "Wg": g["L0_ffn_Wg"],
        "bg": g["L0_ffn_bg"].reshape(1, -1),
        "bias": g["L0_ffn_bias"].reshape(1, -1),
        "W1": g["L0_ffn_W1"],
        "b1": g["L0_ffn_b1"].reshape(16, 128).transpose(1, 0),
        "W2": g["L0_ffn_W2"],
        "b2": g["L0_ffn_b2"],
        "gW": g["L1_gnn_gat_W"],
        "gWT": g["L1_gnn_gat_W"].transpose(2, 0, 1),
        "ga": g["L1_gnn_gat_a"].reshape(6, 128).transpose(1, 0),
        "eWih": g["L1_gnn_edge_Wih"].transpose(1, 0),
        "eWhh": g["L1_gnn_edge_Whh"].transpose(1, 0),
        "ebih": cols3(g["L1_gnn_edge_bih"]),
        "ebhh": cols3(g["L1_gnn_edge_bhh"]),
        "nWih": g["L1_gnn_node_Wih"].transpose(1, 0),
        "nWhh": g["L1_gnn_node_Whh"].transpose(1, 0),
        "nbih": cols3(g["L1_gnn_node_bih"]),
        "nbhh": cols3(g["L1_gnn_node_bhh"]),
        "rw": g["L1_ffn_router_w"].transpose(1, 0),
        "w1": g["L1_ffn_w1"].transpose(2, 0, 1),
        "w3": g["L1_ffn_w3"].transpose(2, 0, 1),
        "w2": g["L1_ffn_w2"].transpose(2, 0, 1),
    }
    nc = _bacc.Bacc("TRN2", target_bir_lowering=False, num_devices=1)
    arrays, args = {}, []
    for name, a in laid.items():
        a = _np.ascontiguousarray(a)
        arrays[f"in_{name}"] = a
        args.append(nc.dram_tensor(f"in_{name}", a.shape, _mybir.dt.from_np(a.dtype), kind="ExternalInput").ap())
    args.append(nc.dram_tensor("outT", (128, 1354), _mybir.dt.float32, kind="ExternalOutput").ap())
    build(nc, *args)
    r = _run(nc, [arrays], core_ids=[0])
    return _np.ascontiguousarray(r.results[0]["outT"].transpose(1, 0))
```

```python
from contextlib import ExitStack

import concourse.bass as bass
from concourse import mybir

F32 = mybir.dt.float32
F32R = mybir.dt.float32r
BF16 = mybir.dt.bfloat16
I32 = mybir.dt.int32
ALU = mybir.AluOpType
ACT = mybir.ActivationFunctionType
AX = mybir.AxisListType

P = 128
N = 1354
T = -(-N // P)
NP = T * P
CW = 512
C = -(-N // CW)
E = 8
H0 = 256
M0 = H0 // P
H1 = 341
M1 = -(-H1 // P)
K = 3
NONE = 1.0e30
SIGN = -(1 << 31)
PARTS = 3


def rows(t):
    return min(P, N - t * P)


def width(c):
    return min(CW, N - c * CW)


def cols(c):
    return slice(c * CW, c * CW + width(c))


def tiles(c):
    return range(c * CW // P, min(T, (c + 1) * CW // P))



TILES0 = C * E * M0
LAG0 = 3
RING0 = 6
RINGW = 4
RINGS = 4
TILES1 = C * E * M1
LAG1 = 3
RING1 = 5
PIECES = C * T


TILES_C = E * M0
EARLY = 3
SENS_AT = [-1] * (T + EARLY) + list(range(T - EARLY)) + [x for x in range(10, PIECES) if x - 10 < T]
PIECE_AT = [-1] * T + [x + 2 for x in range(-EARLY, 0)] + [x + 2 for x in range(T - EARLY)] + [x + 2 for x in SENS_AT[2 * T:]]
PIECE_AT[T:T + EARLY] = [0, 0, 1]


def beside(c, i):
    plan = {}

    def put(i, *task):
        plan.setdefault(i, []).append(task)

    if c >= 1:
        put(1, "mean", 2, c - 1)
        put(1, "center", 2, c - 1)
        put(4, "var", 2, c - 1)
        put(4, "scale", 2, c - 1)
    for p in range(PIECES):
        if SENS_AT[p] // TILES_C == c and SENS_AT[p] >= 0:
            put(SENS_AT[p] % TILES_C, "sens", p)
        if PIECE_AT[p] // TILES_C == c and PIECE_AT[p] >= 0:
            put(PIECE_AT[p] % TILES_C, "piece", p)
    if c + 1 < C:
        last = PIECE_AT[(c + 2) * T - 1] % TILES_C
        n = max(last, 6)
        put(n, "x1", c + 1)
        put(n, "center", 1, c + 1)
        put(n + 1, "mean", 1, c + 1)
        put(n + 2, "var", 1, c + 1)
        put(n + 2, "scale", 1, c + 1)
        put(n + 4, "logits", c + 1)
        put(n + 4, "rank", c + 1)
        put(min(n + 6, TILES_C - 1), "turn", c + 1)
    else:
        put(11, "split", 0)
        put(12, "split", 1)
        put(13, "mask", 0)
        put(14, "mask", 1)
    if c >= 1:
        n = 12 if c + 1 < C else 7
        put(n - 1, "htok", c - 1)
        for k, t in enumerate(tiles(c - 1)):
            put(n + k, "hw", t)
    return plan.get(i, [])


LN_ORDER = [(0, c) for c in range(C)] + [(1, 0)]
LN_ORDER += [x[1:] for c in range(C) for i in range(E * M0) for x in beside(c, i) if x[0] == "mean"]
LN_ORDER += [(2, C - 1)] + [(3, c) for c in range(C)]
LN_AT = {key: n for n, key in enumerate(LN_ORDER)}


def attention_sums():
    steps, waiting = [[] for _ in range(K * T + 3)], []
    for g in range(K * T + 3):
        if g >= 3:
            k, t = divmod(g - 3, T)
            if t % 4 == 3 or t == T - 1:
                waiting += [(k, t // 4, j) for j in range(T)]
        n = 3 if g < (K - 1) * T + 9 else 6 if g < K * T + 2 else len(waiting)
        steps[g], waiting = waiting[:n], waiting[n:]
    assert not waiting
    return steps


SUMS = attention_sums()


GRU_STEPS = [["gates"], ["mid", "new"], ["finish"]]


def at_step(g):
    out = []
    for c in range(C):
        for i, tasks in enumerate(GRU_STEPS):
            if g == 2 * c + i:
                out += [(x, 0, c) for x in tasks]
    at = g - ((K - 1) * T + 9)
    out += [[("mean_heads", 1, 0)], [("gates", 1, 0)], [("mid", 1, 0), ("new", 1, 0)], [("finish", 1, 0)]][at] if 0 <= at < 4 else []
    return out


AFTER = [("mean_heads", 1, 1), ("gates", 1, 1), ("mean_heads", 1, 2), ("mean", 3, 0), ("center", 3, 0), ("mid", 1, 1), ("new", 1, 1),
         ("gates", 1, 2), ("finish", 1, 1), ("mid", 1, 2), ("new", 1, 2), ("mean", 3, 1), ("center", 3, 1), ("finish", 1, 2),
         ("table",), ("var", 3, 0), ("scale", 3, 0), ("logits", C), ("rank", C), ("turn", C)]
BESIDE1 = {2: [("table",), ("var", 3, 1)], 3: [("scale", 3, 1)], 5: [("mean", 3, 2), ("center", 3, 2)],
           8: [("table",), ("var", 3, 2)], 9: [("scale", 3, 2)],
           13: [("logits", C + 1)], 14: [("table",), ("rank", C + 1)], 16: [("turn", C + 1)],
           17: [("logits", C + 2)], 18: [("table",), ("rank", C + 2)], 20: [("turn", C + 2)]}


def build(nc, xT_d, adjT_d, adj_d, W_d, B_d, Wg_d, bg_d, bias_d, W1_d, b1_d, W2_d, b2_d,
          gW_d, gWT_d, ga_d, eWih_d, eWhh_d, ebih_d, ebhh_d, nWih_d, nWhh_d, nbih_d, nbhh_d,
          rw_d, w1_d, w3_d, w2_d, out_d):
    with ExitStack() as ctx:
        def sb(name, shape, dt=F32):
            return ctx.enter_context(nc.sbuf_tensor(name, shape, dt))

        def sem(name):
            return ctx.enter_context(nc.semaphore(name))

        W13_AT = T * N * 6 // 4 - E * 2 * H1

        def place(slot, bytes_, variants):
            out = []
            for variant in variants:
                used = 0
                with ExitStack() as inner:
                    for name, shape, dt in variant:
                        tensor = inner.enter_context(nc.sbuf_tensor(name, shape, dt))
                        if not name.startswith("pad"):
                            out.append(tensor)
                        n = 2 if dt == BF16 else 4
                        for d in shape[1:]:
                            n *= d
                        used += n
                assert used <= bytes_, (slot, used, bytes_)
            sb(slot, [P, bytes_ // 4])
            return out

        xT = sb("xT", [P, N])
        zT = sb("zT", [P, NP])
        gruw = sb("gruw", [P, 2, 3 * P])
        hTok = sb("hTok", [P, T, P])
        regL = sb("regL", [P, 6 * CW])
        regR = sb("regR", [P, 1030])
        ident = sb("ident", [P, P])
        sel6 = sb("sel6", [P, 6])
        sel16f = sb("sel16f", [16, E])
        sel16 = sb("sel16", [16, E], F32R)
        tri = sb("tri", [P, E, E])
        one = sb("one", [P, 1])
        meanw = sb("meanw", [P, 1])
        eps = sb("eps", [P, 1])
        tiny = sb("tiny", [P, 1])
        rowW = sb("rowW", [1, P + 2 * E])
        gru_b = sb("gru_b", [P, 2, 2, 3])
        gru_c = sb("gru_c", [P, 2, 4])
        b1c = sb("b1c", [P, E * M0])
        ga = sb("ga", [P, 2 * K])
        u18 = sb("u18", [P, T, 2, 18], BF16)
        dcol = sb("dcol", [P, T])
        lowest = sb("lowest", [P, K * T])
        low2 = sb("low2", [P, 2])
        den = sb("den", [P, K * T])
        rden = sb("rden", [P, K * T])
        rt = sb("rt", [P, 4, 4 * E])
        g16 = sb("g16", [P, 4, 16], F32R)
        rs = sb("rs", [P, 2, 4])
        negsum = sb("negsum", [P, T])
        negtot = sb("negtot", [P, 1])
        flag = sb("flag", [1, 1], I32)

        RINGQ = T * CW
        (adjT, qT, S_a, gn_d, nsT, ge, z3hi, z3lo, GT1, rw, s1_ring, m1_ring) = place("slotA", T * N * 4, [
            [("adjT", [P, T, N], F32)],
            [("qT", [P, 2, T, CW], F32), ("S_a", [P, 2, NP], F32), ("gn_d", [P, CW], F32)],
            [("pad1", [P, RINGQ], F32), ("nsT", [P, N], F32), ("ge", [P, 4, CW], F32)],
            [("pad2", [P, RINGQ], F32), ("z3hi", [P, N], F32R), ("z3lo", [P, N], F32R), ("GT1", [16, C, CW], F32R),
             ("rw", [P, E], F32)],
            [("s1_ring", [P, 4, CW], F32), ("m1_ring", [P, RING1, CW], F32)],
        ])
        (a_ring, t_ring, w_ring, msg, W1hi, W1lo, W2s, zhi, zlo, hr_ring, GT0, Wl0, Wg, wcat, gWT, b2x, b2hi, b2lo,
         adjR, mb, gn, w13hi, w13lo, w2s, w13) = place("slotB", T * N * 6, [
            [("a_ring", [P, RINGS, CW], F32), ("t_ring", [P, RINGS, CW], F32), ("w_ring", [P, RINGW, CW], F32),
             ("msg", [P, T, P], F32), ("W1hi", [P, E, H0], F32R), ("W1lo", [P, E, H0], F32R), ("W2s", [P, E, M0, P], F32),
             ("zhi", [P, 2, CW], F32R), ("zlo", [P, 2, CW], F32R), ("hr_ring", [P, RING0, CW], F32),
             ("GT0", [16, 2, CW], F32R), ("Wl0", [P, P], F32), ("Wg", [P, E], F32), ("wcat", [P, 3 * P + 6], F32),
             ("gWT", [P, K, P], F32), ("b2x", [16, P], F32), ("b2hi", [16, P], F32R), ("b2lo", [16, P], F32R)],
            [("adjR", [P, T, N], F32), ("mb", [P, T, N], BF16)],
            [("pad3", [P, T * N], F32), ("gn", [P, 3, CW], F32)],
            [("w13hi", [P, E, 2, H1], F32R), ("w13lo", [P, E, 2, H1], F32R), ("w2s", [P, E, M1, P], F32)],
            [("pad4", [P, W13_AT], F32), ("w13", [P, E, 2, H1], F32)],
        ])
        (W1f, hW) = place("slotH", T * K * P * 4, [
            [("W1f", [P, E, H0], F32)],
            [("hW", [P, T, K * P], F32)],
        ])
        (masks, eplus) = place("slotE", N * 4, [
            [("masks", [P, 2, N], BF16)],
            [("eplus", [P, N], F32)],
        ])
        xc_ring = regL[:, 0:2 * CW].rearrange("p (r n) -> p r n", r=2)
        y_ring = regL[:, 2 * CW:4 * CW].rearrange("p (r n) -> p r n", r=2)
        v_ring = regL[:, 4 * CW:6 * CW].rearrange("p (r n) -> p r n", r=2)
        e18 = regL[0:18, 0:N]
        e6 = regL[0:6, 0:N]
        eminus = regL[:, N:2 * N]
        GRU_BUF = [[[ge[:, i, :] for i in range(4)]] * C,
                   [[gn[:, 0, :], gn[:, 1, :], gn[:, 2, :], gn_d[:, :]],
                    [eplus[:, 0:CW], eplus[:, CW:2 * CW], regL[:, 0:CW], regL[:, 2 * CW:3 * CW]],
                    [s1_ring[:, i, :] for i in range(4)]]]
        HALF = N // 2
        neg_row = regR[:, 0:HALF]
        neg_mask = regR[:, HALF:HALF + (HALF + 1) // 2].bitcast(BF16)
        rank = regR[:, 0:2 * 4 * E * E].rearrange("p (i n) -> p i n", i=2)
        u = regR[:, 512:512 + T * 6].rearrange("p (t j) -> p t j", t=T)
        ur = regR[:, 580:580 + T * 6].rearrange("p (t j) -> p t j", t=T)
        S = [S_a[:, 0, :], S_a[:, 1, :], hTok[:, :, :].rearrange("p t n -> p (t n)")]

        bk = [ctx.enter_context(nc.psum_tensor(f"bank{i}", [P, CW], F32)) for i in range(8)]
        B_SIDE = bk[0]
        B_GNN, B_Y0 = bk[2], bk[3]
        B_GATE = [bk[4], bk[1]]
        B_H = bk[5:8]
        B_MSG = [bk[1], bk[3], bk[4]]
        B_NS = bk[2:5]
        B_E18 = bk[5:8]
        B_ACC = bk[1:4]
        GRU_BANK = [[[bk[4], bk[1], bk[0], bk[2], bk[3]]] * C,
                    [[bk[4], bk[1], bk[0], bk[4], bk[1]],
                     [bk[5], bk[6], bk[7], bk[2], bk[5]],
                     [bk[4], bk[1], bk[3], bk[2], bk[4]]]]
        B_EB = [bk[0], bk[4]]
        B_H1, B_H3, B_Y1 = [bk[5], bk[6]], [bk[7], bk[3]], bk[2]

        def ln_bank(l, c):
            return B_H[c] if l == 0 else B_SIDE

        names = """x_in adjT_in0 adjT_in1 adjT_in2 adjR_in0 adjR_in1 adjR_in2 wts0_in W1_in ffn0_in gat_in gru_in
            node_in w13_in0 w13_in1 w13_in2 w13_in3 w13_in4 w13_in5 w13_in6 w13_in7 w2_in rw_in out_done
            const_raw const_set zpad_set sel16_set ln_mean ln_xc ln_sq ln_var ln_log ln_y0 ln_step ln_z z_hi
            z_split bgs_set W1_split b2_split msg_ps msg_set r2_log y0_set y0_sign newton_t newton_y sens_arg
            sens_exp w_ready gnn_mm x1_ready x2_ready x3_ready x4_ready logits_ps logits_read route_d route_e
            route_step gates_set gt_ps gt_set gate_ps h_ps h_relu h_gated y_mm v_ps v_set htok_ps htok_set hw_ps
            hw_set u_step u18_set offdiag_set mask_set mask_used ns_mm ns_set e18_set neg_acc neg_max neg_ps
            flag_set nmask_set nmask_used ne18_set e6_ps e6_fifth e6_set eb_ps eb_set nb_ps nb_set mb_set
            dcol_set row_diag_set spad_set s_set neg_step p_set rden_set q_set tr_ps tr_set gat_mm es_set gru_ps
            gru_nh gru_t gru_a gru_n diag_ps x_edge gru_bias w13_hi w13_lo gate1_ps h1_ps h3_ps s_silu s_gated
            m_set y1_mm""".split()
        s = {n: sem(n) for n in names}

        def at(eng, name, value):
            if value > 0:
                eng.wait_ge(s[name], value)

        block = ctx.enter_context(nc.Block())

        EARLY_ROWS = (T * P + (2 * RINGS + RINGW) * CW) // N

        def mask_tiles(e):
            return -(-(W13_AT - T * N + (e + 1) * 2 * H1) * 2 // N)

        def hi_tiles(e):
            return -(-(e + 1) * 2 * H1 // N)

        def lo_tiles(e):
            return -(-(E + e + 1) * 2 * H1 // N)

        @block.sync
        def _(sp):
            def adjT_load(c):
                full = (T - 1) * P
                sp.dma_start(adjT[:, 0:T - 1, cols(c)],
                             adjT_d[0:full, cols(c)].rearrange("(t p) n -> p t n", p=P)).then_inc(s[f"adjT_in{c}"], 16)
                sp.dma_start(adjT[0:N - full, T - 1, cols(c)], adjT_d[full:N, cols(c)]).then_inc(s[f"adjT_in{c}"], 16)

            sp.dma_start(xT[:, :], xT_d).then_inc(s["x_in"], 16)
            sp.dma_start(Wl0[:, :], W_d).then_inc(s["wts0_in"], 16)
            sp.dma_start(rowW[0:1, 0:P], B_d).then_inc(s["wts0_in"], 16)
            sp.dma_start(rowW[0:1, P:P + E], bg_d).then_inc(s["wts0_in"], 16)
            sp.dma_start(rowW[0:1, P + E:P + 2 * E], bias_d).then_inc(s["wts0_in"], 16)
            adjT_load(0)
            sp.dma_start(W1f[:, :, :], W1_d.rearrange("e c h -> c e h")).then_inc(s["W1_in"], 16)
            sp.dma_start(Wg[:, :], Wg_d).then_inc(s["ffn0_in"], 16)
            sp.dma_start(W2s[:, :, :, :], W2_d.rearrange("e (m p) d -> p e m d", p=P)).then_inc(s["ffn0_in"], 16)
            sp.dma_start(b1c[:, :], b1_d).then_inc(s["ffn0_in"], 16)
            sp.dma_start(b2x[0:E, :], b2_d).then_inc(s["ffn0_in"], 16)
            sp.dma_start(b2x[E:2 * E, :], b2_d).then_inc(s["ffn0_in"], 16)
            adjT_load(1)
            adjT_load(2)
            sp.dma_start(wcat[:, 0:3 * P].rearrange("p (k d) -> p k d", k=K),
                         gW_d.rearrange("k c d -> c k d")).then_inc(s["gat_in"], 16)
            sp.dma_start(gWT[:, :, :], gWT_d).then_inc(s["gat_in"], 16)
            sp.dma_start(ga[:, :], ga_d).then_inc(s["gat_in"], 16)
            for n, (bi, bh) in enumerate([(ebih_d, ebhh_d), (nbih_d, nbhh_d)]):
                sp.dma_start(gru_b[:, n, 0, :], bi).then_inc(s["gru_in"], 16)
                sp.dma_start(gru_b[:, n, 1, :], bh).then_inc(s["gru_in"], 16)
            sp.dma_start(gruw[:, 0, :], eWih_d).then_inc(s["gru_in"], 16)
            sp.dma_start(gruw[:, 1, :], eWhh_d).then_inc(s["gru_in"], 16)
            sp.wait_ge(s["gnn_mm"], PIECES)
            for t in range(T):
                if t == EARLY_ROWS:
                    sp.wait_ge(s["x2_ready"], C)
                    sp.wait_ge(s["hw_ps"], T)
                sp.dma_start(adjR[0:rows(t), t, :], adj_d[t * P:t * P + rows(t), :]).then_inc(s[f"adjR_in{t // 4}"], 16)
            sp.wait_ge(s["x_edge"], C)
            sp.dma_start(gruw[:, 0, :], nWih_d).then_inc(s["node_in"], 16)
            sp.dma_start(gruw[:, 1, :], nWhh_d).then_inc(s["node_in"], 16)
            for e in range(E):
                sp.wait_ge(s["s_set"], (K - 1) * T + mask_tiles(e))
                sp.dma_start(w13[:, e, 0, :], w1_d[:, e, :]).then_inc(s[f"w13_in{e}"], 16)
                sp.dma_start(w13[:, e, 1, :], w3_d[:, e, :]).then_inc(s[f"w13_in{e}"], 16)
            sp.wait_ge(s["q_set"], K * T)
            for m in range(M1):
                r = min(P, H1 - m * P)
                sp.dma_start(w2s[0:r, :, m, :], w2_d[m * P:m * P + r, :, :]).then_inc(s["w2_in"], 16)
            sp.wait_ge(s["gat_mm"], K * C)
            sp.dma_start(rw[:, :], rw_d).then_inc(s["rw_in"], 16)
            for c in range(C):
                sp.wait_ge(s["x4_ready"], c + 1)
                sp.dma_start(out_d[:, cols(c)], xT[:, cols(c)]).then_inc(s["out_done"], 16)
            sp.wait_ge(s["out_done"], 16 * C)

        @block.gpsimd
        def _(pool):
            raw = [(ident[:, :], 0.0), (sel6[:, :], 0.0), (sel16f[:, :], 0.0), (tri[:, :, :], 1.0), (one[:, :], 1.0),
                   (meanw[:, :], 1.0 / P), (eps[:, :], 1.0e-5), (tiny[:, :], 1.0e-19)]
            for ap, value in raw:
                pool.memset(ap, value).then_inc(s["const_raw"], 1)
            pool.memset(zT[:, N:NP], 0.0).then_inc(s["zpad_set"], 1)
            pool.wait_ge(s["const_raw"], len(raw))
            pool.affine_select(out=ident[:, :], in_=ident[:, :], compare_op=ALU.not_equal, fill=1.0,
                               base=0, pattern=[[-1, P]], channel_multiplier=1).then_inc(s["const_set"], 1)
            pool.affine_select(out=tri[:, :, :], in_=tri[:, :, :], compare_op=ALU.is_gt, fill=0.0,
                               base=0, pattern=[[1, E], [-1, E]], channel_multiplier=0).then_inc(s["const_set"], 1)
            n = 2
            for ap, k, parts in ((sel16f, E, 2), (sel6, 6, PARTS)):
                for part in range(parts):
                    pool.affine_select(out=ap[:, :], in_=ap[:, :], compare_op=ALU.not_equal, fill=1.0, base=-k * part,
                                       pattern=[[-1, k]], channel_multiplier=1).then_inc(s["const_set"], 1)
                    n += 1
                    pool.wait_ge(s["const_set"], n)
            pool.wait_ge(s["w_ready"], PIECES)
            for t in range(T):
                r = rows(t)
                blk = adjT[0:r, t, t * P:t * P + r]
                pool.affine_select(out=blk, in_=blk, compare_op=ALU.not_equal, fill=0.0, base=0, pattern=[[-1, r]],
                                   channel_multiplier=1).then_inc(s["offdiag_set"], 1)
            for t in range(T):
                r = rows(t)
                blk = adjR[0:r, t, t * P:t * P + r]
                pool.wait_ge(s["dcol_set"], t + 1)
                pool.wait_ge(s["neg_acc"], t + 1)
                pool.affine_select(out=blk, in_=blk, compare_op=ALU.not_equal, fill=0.0, base=0, pattern=[[-1, r]],
                                   channel_multiplier=1).then_inc(s["row_diag_set"], 1)
            pool.wait_ge(s["ns_set"], 1)
            for i in range(2):
                pool.memset(S[i][:, N:NP], 0.0).then_inc(s["spad_set"], 1)
            pool.memset(S[2][:, N:NP], 0.0).then_inc(s["spad_set"], 1)

        CONSTS = 2 + 2 + PARTS

        @block.scalar
        def _(act):
            def ln_square(l, c):
                n, w = LN_AT[l, c], width(c)
                at(act, "ln_xc", n + 1)
                at(act, "ln_z", n - 1)
                nc.scalar.activation(y_ring[:, n % 2, 0:w], xc_ring[:, n % 2, 0:w], ACT.Square).then_inc(s["ln_sq"], 1)

            def ln_rsqrt(l, c):
                n, w = LN_AT[l, c], width(c)
                at(act, "ln_var", n + 1)
                nc.scalar.activation(v_ring[:, n % 2, 0:w], ln_bank(l, c)[:, 0:w], ACT.Ln, bias=eps[:, 0:1]).then_inc(s["ln_log"], 1)
                at(act, "ln_log", n + 1)
                nc.scalar.activation(y_ring[:, n % 2, 0:w], v_ring[:, n % 2, 0:w], ACT.Exp, scale=-0.5).then_inc(s["ln_y0"], 1)

            def first_reciprocal(p, between):
                if p >= PIECES:
                    for step in between:
                        step()
                    return
                c, j = divmod(p, T)
                r, w = rows(j), width(c)
                a = a_ring[0:r, p % RINGS, 0:w]
                if j == 0:
                    at(act, f"adjT_in{c}", 32)
                at(act, "newton_y", p - RINGS + 1)
                nc.scalar.activation(a, adjT[0:r, j, cols(c)], ACT.Square).then_inc(s["r2_log"], 1)
                between[0]()
                at(act, "r2_log", 2 * p + 1)
                nc.scalar.activation(a, a, ACT.Ln, bias=tiny[0:r, 0:1]).then_inc(s["r2_log"], 1)
                between[1]()
                at(act, "r2_log", 2 * p + 2)
                nc.scalar.activation(a, a, ACT.Exp, scale=-0.5).then_inc(s["y0_set"], 1)

            def argument(p):
                if p >= PIECES:
                    return
                c, j = divmod(p, T)
                t = t_ring[0:rows(j), p % RINGS, 0:width(c)]
                at(act, "newton_y", p + 1)
                nc.scalar.activation(t, t, ACT.Square, bias=one[0:rows(j), 0:1]).then_inc(s["sens_arg"], 1)

            def sensitivity(p):
                if p >= PIECES:
                    return
                c, j = divmod(p, T)
                t = t_ring[0:rows(j), p % RINGS, 0:width(c)]
                at(act, "sens_arg", p + 1)
                nc.scalar.activation(t, t, ACT.Exp, scale=-2.0).then_inc(s["sens_exp"], 1)

            def nothing():
                pass

            def h_tokens(c):
                at(act, "htok_ps", c + 1)
                k = len(tiles(c))
                nc.scalar.copy(hTok[:, c * 4:c * 4 + k, :], B_SIDE[:, 0:k * P]).then_inc(s["htok_set"], 1)

            def head_products(t):
                at(act, "hw_ps", t + 1)
                if t == 0:
                    at(act, "W1_split", 2)
                nc.scalar.copy(hW[:, t, :], B_SIDE[:, 0:K * P]).then_inc(s["hw_set"], 1)
                nc.scalar.copy(u[:, t, :], B_SIDE[:, K * P:K * P + 6]).then_inc(s["hw_set"], 1)

            def router_exp(n):
                at(act, "route_d", n + 1)
                k = len(tiles(n % C)) * E
                nc.scalar.activation(rt[:, 1, 0:k], rt[:, 0, 0:k], ACT.Exp).then_inc(s["route_e"], 1)

            def side(task, between=nothing):
                kind = task[0]
                if kind == "sens":
                    first_reciprocal(task[1] + 3, (between, lambda: argument(task[1] + 1)))
                    sensitivity(task[1] + 1)
                elif kind == "center":
                    ln_square(*task[1:])
                elif kind == "var":
                    ln_rsqrt(*task[1:])
                elif kind == "rank":
                    router_exp(task[1])
                elif kind == "table":
                    act.preload_act_table_set("natural_log_exp_and_others")
                elif kind == "htok":
                    h_tokens(task[1])
                elif kind == "hw":
                    head_products(task[1])

            act.preload_act_table_set("natural_log_exp_and_others")
            act.wait_ge(s["const_set"], CONSTS)
            ln_square(0, 0)
            ln_square(0, 1)
            ln_rsqrt(0, 0)
            first_reciprocal(0, (nothing, nothing))
            ln_square(0, 2)
            ln_rsqrt(0, 1)
            first_reciprocal(1, (nothing, nothing))
            ln_rsqrt(0, 2)
            first_reciprocal(2, (nothing, lambda: argument(0)))
            sensitivity(0)
            for c in range(C):
                at(act, "msg_ps", c + 1)
                k = len(tiles(c))
                nc.scalar.copy(msg[:, c * 4:c * 4 + k, :], B_MSG[c][:, 0:k * P]).then_inc(s["msg_set"], 1)
            for p in range(T):
                side(("sens", p))
            side(("center", 1, 0))
            side(("sens", T))
            side(("var", 1, 0))
            side(("sens", T + 1))
            side(("rank", 0))
            side(("sens", T + 2))
            for q in range(TILES0):
                c, e, m = q // (E * M0), q // M0 % E, q % M0
                w = width(c)

                def relu():
                    at(act, "h_ps", q + 1)
                    at(act, "y_mm", q - RING0 + 1)
                    nc.scalar.activation(hr_ring[:, q % RING0, 0:w], B_H[q % 3][:, 0:w], ACT.Relu,
                                         bias=b1c[:, e * M0 + m:e * M0 + m + 1]).then_inc(s["h_relu"], 1)

                tasks = beside(c, q % (E * M0))
                if tasks and tasks[0][0] == "sens":
                    side(tasks[0], relu)
                    tasks = tasks[1:]
                else:
                    relu()
                for task in tasks:
                    side(task)
            side(("center", 2, C - 1))
            side(("var", 2, C - 1))
            side(("htok", C - 1))
            for t in tiles(C - 1):
                side(("hw", t))
            act.preload_act_table_set("exp_and_others")
            for t in range(T):
                r = rows(t)
                at(act, f"adjR_in{t // 4}", 16 * len(tiles(t // 4)))
                at(act, "neg_acc", t)
                nc.scalar.activation(mb[0:r, t, :], adjR[0:r, t, :], ACT.Relu, scale=-1.0,
                                     accum_out=negsum[0:r, t:t + 1]).then_inc(s["neg_acc"], 1)

            at(act, "flag_set", 1)
            any_negative = act.value_load(flag[0:1, 0:1], min_val=0, max_val=1)
            with act.If(any_negative == 1):
                at(act, "ne18_set", C)
            for c in range(C):
                at(act, "e6_ps", c + 1)
                nc.scalar.mul(e6[:, cols(c)], B_E18[c][0:6, 0:width(c)], -0.2).then_inc(s["e6_fifth"], 1)
            for c in range(C):
                at(act, "ns_mm", c + 1)
                at(act, "mask_set", T)
                nc.scalar.copy(nsT[:, cols(c)], B_NS[c][:, 0:width(c)]).then_inc(s["ns_set"], 1)

            def mean_heads(n, c):
                w = width(c)
                at(act, "gat_mm", (K - 1) * C + c + 1)
                at(act, "s_set", K * T if c else (K - 1) * T + 3)
                nc.scalar.mul(GRU_BUF[n][c][3][:, 0:w], B_ACC[c][:, 0:w], 1.0 / K).then_inc(s["es_set"], 1)

            def gates(n, c):
                g, w = n * C + c, width(c)
                (tr, tz, _, _), (b_r, b_z, _, _, _) = GRU_BUF[n][c], GRU_BANK[n][c]
                at(act, "gru_ps", g + 1)
                if n == 0:
                    at(act, "x_edge", c)
                nc.scalar.activation(tr[:, 0:w], b_r[:, 0:w], ACT.Tanh, scale=0.5, bias=gru_c[:, n, 0:1]).then_inc(s["gru_t"], 1)
                nc.scalar.activation(tz[:, 0:w], b_z[:, 0:w], ACT.Tanh, scale=0.5, bias=gru_c[:, n, 1:2]).then_inc(s["gru_t"], 1)

            def new(n, c):
                g, w = n * C + c, width(c)
                a = GRU_BUF[n][c][2][:, 0:w]
                at(act, "gru_a", g + 1)
                nc.scalar.activation(a, a, ACT.Tanh, bias=gru_c[:, n, 2:3]).then_inc(s["gru_n"], 1)

            def gat_side(task):
                if task[0] == "mean_heads":
                    mean_heads(*task[1:])
                elif task[0] == "gates":
                    gates(*task[1:])
                elif task[0] == "new":
                    new(*task[1:])
                else:
                    side(task)

            def score_rows(k):
                for c in range(C):
                    at(act, "eb_ps", C * k + c + 1)
                    if c == 0:
                        at(act, "s_set", T * k)
                        at(act, "mask_used", T)
                    nc.scalar.copy(eplus[:, cols(c)], B_EB[(C * k + c) % 2][:, 0:width(c)]).then_inc(s["eb_set"], 1)
                with act.If(any_negative == 1):
                    for c in range(C):
                        at(act, "nb_ps", C * k + c + 1)
                        nc.scalar.copy(eminus[:, cols(c)], B_EB[0][:, 0:width(c)]).then_inc(s["nb_set"], 1)

            at(act, "gru_bias", 1)
            done = 0
            for g in range(K * T + 2):
                if g < K * T and g % T == 0:
                    score_rows(g // T)
                if g < K * T:
                    r = rows(g % T)
                    at(act, "s_set", g + 1)
                    row = S[g % 3][0:r, 0:N]
                    nc.scalar.activation(row, row, ACT.Exp, bias=lowest[0:r, g:g + 1], scale=-1.0,
                                         accum_out=den[0:r, g:g + 1]).then_inc(s["p_set"], 1)
                if g >= 2:
                    h = g - 2
                    k, t = divmod(h, T)
                    r, c = rows(t), t // 4
                    if h == 4:
                        at(act, "x_edge", C)
                    for v in range(3):
                        at(act, "tr_ps", 3 * h + v + 1)
                        if t % 4 == 0 and v == 0:
                            at(act, "gat_mm", k * C + c - 1)
                        nb = min(4, T - 4 * v)
                        nc.scalar.copy(qT[:, (k * C + c) % 2, 4 * v:4 * v + nb, (t % 4) * P:(t % 4) * P + r],
                                       B_H[v][:, 0:nb * P].rearrange("p (b i) -> p b i", b=nb)[:, :, 0:r]
                                       ).then_inc(s["tr_set"], 1)
                for task in at_step(g):
                    gat_side(task)
                while done < E and g >= (K - 1) * T + mask_tiles(done) + 2:
                    at(act, f"w13_in{done}", 32)
                    at(act, "q_set", (K - 1) * T + hi_tiles(done))
                    nc.scalar.copy(w13hi[:, done, :, :], w13[:, done, :, :]).then_inc(s["w13_hi"], 1)
                    done += 1
            assert done >= E - 2
            for task in AFTER:
                gat_side(task)
                if done < E:
                    at(act, f"w13_in{done}", 32)
                    at(act, "q_set", (K - 1) * T + hi_tiles(done))
                    nc.scalar.copy(w13hi[:, done, :, :], w13[:, done, :, :]).then_inc(s["w13_hi"], 1)
                    done += 1
            at(act, "x3_ready", C)
            for q in range(TILES1):
                c, m = q // (E * M1), q % M1
                r, w = min(P, H1 - m * P), width(c)
                at(act, "h1_ps", q + 1)
                at(act, "m_set", q - 3)
                nc.scalar.activation(s1_ring[0:r, q % 4, 0:w], B_H1[q % 2][0:r, 0:w], ACT.Silu).then_inc(s["s_silu"], 1)
                for task in BESIDE1.get(q, []):
                    side(task)

        @block.tensor
        def _(pe):
            side_free = [("ln_z", 0)]

            def take_side(name, count):
                at(pe, *side_free[0])
                side_free[0] = (name, count)

            def exact(out, w, x, start, stop):
                (whi, wlo), (xhi, xlo) = w, x
                nc.tensor.matmul(out, whi, xhi, start=start, stop=False)
                nc.tensor.matmul(out, whi, xlo, start=False, stop=False)
                return nc.tensor.matmul(out, wlo, xhi, start=False, stop=stop)

            def ln_mean(l, c):
                n, w = LN_AT[l, c], width(c)
                at(pe, ["x_in", "x1_ready", "x2_ready", "x3_ready"][l], c + 1 if l else 16)
                if l:
                    take_side("ln_xc", n + 1)
                nc.tensor.matmul(ln_bank(l, c)[:, 0:w], meanw[:, 0:1].to_broadcast([P, P]), xT[:, cols(c)],
                                 start=True, stop=True).then_inc(s["ln_mean"], 1)

            def ln_var(l, c):
                n, w = LN_AT[l, c], width(c)
                if l:
                    take_side("ln_z", n + 1)
                at(pe, "ln_sq", n + 1)
                nc.tensor.matmul(ln_bank(l, c)[:, 0:w], meanw[:, 0:1].to_broadcast([P, P]), y_ring[:, n % 2, 0:w],
                                 start=True, stop=True).then_inc(s["ln_var"], 1)

            def piece(p):
                c, j = divmod(p, T)
                r, w = rows(j), width(c)
                at(pe, "w_ready", p + 1)
                if j == 0:
                    at(pe, "x1_ready", c)
                    at(pe, "msg_set", C)
                nc.tensor.matmul(B_GNN[:, 0:w], msg[0:r, j, :], w_ring[0:r, p % RINGW, 0:w],
                                 start=(j == 0), stop=(j == T - 1)).then_inc(s["gnn_mm"], 1)

            def logits(n):
                l, c = divmod(n, C)
                at(pe, "ln_z", LN_AT[2 * l + 1, c] + 1)
                take_side("logits_read", n + 1)
                for i, t in enumerate(tiles(c)):
                    o = B_SIDE[:, i * E:(i + 1) * E]
                    mm = nc.tensor.matmul(o, zT[:, t * P:(t + 1) * P], (Wg, rw)[l][:, :], start=True, stop=(l == 1))
                    if l == 0:
                        mm = nc.tensor.matmul(o, one[0:1, 0:1].to_broadcast([1, P]), rowW[0:1, P:P + E], start=False, stop=True)
                mm.then_inc(s["logits_ps"], 1)

            def turn(n):
                l, c = divmod(n, C)
                at(pe, "gates_set", n + 1)
                take_side("gt_set", n + 1)
                for i, t in enumerate(tiles(c)):
                    mm = nc.tensor.transpose(B_SIDE[0:16, i * P:(i + 1) * P], g16[:, i, :].bitcast(F32), ident[:, :])
                mm.then_inc(s["gt_ps"], 1)

            def h_tokens(c):
                at(pe, "ln_z", LN_AT[2, c] + 1)
                take_side("htok_set", c + 1)
                for i, t in enumerate(tiles(c)):
                    mm = nc.tensor.transpose(B_SIDE[:, i * P:(i + 1) * P], zT[:, t * P:(t + 1) * P], ident[:, :])
                mm.then_inc(s["htok_ps"], 1)

            def head_products(t):
                take_side("hw_set", 2 * (t + 1))
                nc.tensor.matmul(B_SIDE[:, 0:K * P + 6], zT[:, t * P:(t + 1) * P], wcat[:, :],
                                 start=True, stop=True).then_inc(s["hw_ps"], 1)

            def side(task):
                kind = task[0]
                if kind == "piece":
                    piece(task[1])
                elif kind == "mean":
                    ln_mean(*task[1:])
                elif kind == "var":
                    ln_var(*task[1:])
                elif kind == "logits":
                    logits(task[1])
                elif kind == "turn":
                    turn(task[1])
                elif kind == "htok":
                    h_tokens(task[1])
                elif kind == "hw":
                    head_products(task[1])

            pe.wait_ge(s["const_set"], CONSTS)
            pe.wait_ge(s["zpad_set"], 1)
            ln_mean(0, 0)
            ln_mean(0, 1)
            ln_var(0, 0)
            ln_mean(0, 2)
            ln_var(0, 1)
            ln_var(0, 2)
            pe.wait_ge(s["wts0_in"], 64)
            for c in range(C):
                at(pe, "ln_z", c + 1)
                for i, t in enumerate(tiles(c)):
                    o = B_MSG[c][:, i * P:(i + 1) * P]
                    nc.tensor.matmul(o, zT[:, t * P:(t + 1) * P], Wl0[:, :], start=True, stop=False)
                    mm = nc.tensor.matmul(o, one[0:1, 0:1].to_broadcast([1, P]), rowW[0:1, 0:P], start=False, stop=True)
                mm.then_inc(s["msg_ps"], 1)
            pe.wait_ge(s["gat_in"], 48)
            for k in range(K):
                mm = nc.tensor.matmul(B_SIDE[:, 2 * k:2 * k + 2], gWT[:, k, :], ga[:, 2 * k:2 * k + 2], start=True, stop=True)
            mm.then_inc(s["v_ps"], 1)
            side_free[0] = ("v_set", 1)
            for p in range(T):
                piece(p)
            side(("mean", 1, 0))
            side(("var", 1, 0))
            pe.wait_ge(s["ffn0_in"], 80)
            pe.wait_ge(s["bgs_set"], 1)
            side(("logits", 0))
            side(("turn", 0))
            at(pe, "W1_split", 2)
            at(pe, "b2_split", 2)
            at(pe, "sel16_set", 1)

            def down(q):
                c, e, m = q // (E * M0), q // M0 % E, q % M0
                w = width(c)
                if e == 0 and m == 0:
                    at(pe, "x2_ready", c)
                    nc.tensor.matmul(B_Y0[:, 0:w], b2hi[:, :], GT0[:, c % 2, 0:w], start=True, stop=False)
                    nc.tensor.matmul(B_Y0[:, 0:w], b2lo[:, :], GT0[:, c % 2, 0:w], start=False, stop=False)
                at(pe, "h_gated", q + 1)
                nc.tensor.matmul(B_Y0[:, 0:w], W2s[:, e, m, :], hr_ring[:, q % RING0, 0:w], start=False,
                                 stop=(e == E - 1 and m == M0 - 1)).then_inc(s["y_mm"], 1)

            for q in range(TILES0):
                c, e, m = q // (E * M0), q // M0 % E, q % M0
                w = width(c)
                if e == 0 and m == 0:
                    at(pe, "gt_set", c + 1)
                    at(pe, "z_split", c + 1)
                    if q == 0:
                        at(pe, "msg_set", C)
                if m == 0:
                    at(pe, "h_gated", (q // M0 - 1) * M0)
                    nc.tensor.matmul(B_GATE[q // M0 % 2][:, 0:w], sel16[:, e:e + 1].to_broadcast([16, P]), GT0[:, c % 2, 0:w],
                                     start=True, stop=True).then_inc(s["gate_ps"], 1)
                at(pe, "h_relu", q - 2)
                exact(B_H[q % 3][:, 0:w], (W1hi[:, e, m * P:(m + 1) * P], W1lo[:, e, m * P:(m + 1) * P]),
                      (zhi[:, c % 2, 0:w], zlo[:, c % 2, 0:w]), True, True).then_inc(s["h_ps"], 1)
                if q % (E * M0) >= LAG0:
                    down(q - LAG0)
                if q % (E * M0) == E * M0 - 1:
                    for late in range(q - LAG0 + 1, q + 1):
                        down(late)
                for task in beside(c, q % (E * M0)):
                    side(task)
            def neighbours(j):
                r = rows(j)
                at(pe, "offdiag_set", j + 1)
                at(pe, "htok_set", j // 4 + 1)
                if j == 0:
                    at(pe, "x2_ready", C)
                for c in range(C):
                    ns = nc.tensor.matmul(B_NS[c][:, 0:width(c)], hTok[0:r, j, :], adjT[0:r, j, cols(c)],
                                          start=(j == 0), stop=(j == T - 1))
                    if j == T - 1:
                        ns.then_inc(s["ns_mm"], 1)
                at(pe, "u18_set", 2 * (j // 4 + 1))
                at(pe, "mask_set", j + 1)
                for c in range(C):
                    mm = nc.tensor.matmul(B_E18[c][0:18, 0:width(c)], u18[0:r, j, 0, :], masks[0:r, j % 2, cols(c)],
                                          start=(j == 0), stop=(j == T - 1))
                mm.then_inc(s["mask_used"], 1)

            side(("mean", 2, C - 1))
            neighbours(0)
            side(("var", 2, C - 1))
            for j in range(1, 4):
                neighbours(j)
            side(("htok", C - 1))
            for i, t in enumerate(tiles(C - 1)):
                side(("hw", t))
                neighbours(4 + i)
            for j in range(4 + len(tiles(C - 1)), T):
                neighbours(j)
            at(pe, "neg_max", 1)
            take_side("flag_set", 1)
            nc.tensor.matmul(B_SIDE[0:1, 0:1], negtot[:, 0:1], one[:, 0:1], start=True, stop=True).then_inc(s["neg_ps"], 1)
            at(pe, "flag_set", 1)
            any_negative = pe.value_load(flag[0:1, 0:1], min_val=0, max_val=1)
            at(pe, "e18_set", C)
            with pe.If(any_negative == 1):
                for j in range(T):
                    r = rows(j)
                    at(pe, "nmask_set", j + 1)
                    for c in range(C):
                        mm = nc.tensor.matmul(B_E18[c][0:18, 0:width(c)], u18[0:r, j, 1, :], masks[0:r, j % 2, cols(c)],
                                              start=(j == 0), stop=(j == T - 1))
                    mm.then_inc(s["nmask_used"], 1)
                at(pe, "ne18_set", C)

            for c in range(C):
                nc.tensor.matmul(B_E18[c][0:6, 0:width(c)], sel6[0:18, :], e18[:, cols(c)], start=True, stop=True
                                 ).then_inc(s["e6_ps"], 1)

            def score_row(n):
                k, c = divmod(n, C)
                at(pe, "eb_set", n - 1)
                if n == 1:
                    at(pe, "ns_set", C)
                if k == 1 and c == 0:
                    at(pe, "x_edge", C)
                if k >= 1 and c == 1:
                    with pe.If(any_negative == 1):
                        at(pe, "nb_set", C * k)
                at(pe, "e6_set", c + 1)
                nc.tensor.matmul(B_EB[n % 2][:, 0:width(c)], ident[0:6, k:k + 1].to_broadcast([6, P]),
                                 e6[:, cols(c)], start=True, stop=True).then_inc(s["eb_ps"], 1)

            def negative_rows(k):
                with pe.If(any_negative == 1):
                    for c in range(C):
                        at(pe, "eb_set", C * (k + 1))
                        at(pe, "nb_set", C * k + c)
                        nc.tensor.matmul(B_EB[0][:, 0:width(c)], ident[0:6, K + k:K + k + 1].to_broadcast([6, P]),
                                         e6[:, cols(c)], start=True, stop=True).then_inc(s["nb_ps"], 1)
                    at(pe, "nb_set", C * (k + 1))

            def new_product(n, c):
                w = width(c)
                nc.tensor.matmul(GRU_BANK[n][c][3][:, 0:w], gruw[:, 1, 2 * P:3 * P], zT[:, cols(c)], start=True, stop=True
                                 ).then_inc(s["gru_nh"], 1)

            def diagonal(n, c):
                for i, t in enumerate(tiles(c)):
                    r = rows(t)
                    mm = nc.tensor.matmul(GRU_BANK[n][c][4][:, i * P:i * P + r], dcol[0:r, t:t + 1].to_broadcast([r, P]),
                                          ident[0:r, 0:r], start=True, stop=True)
                mm.then_inc(s["diag_ps"], 1)

            def gates(n, c):
                w = width(c)
                src = GRU_BUF[1][c][3][:, 0:w] if n else nsT[:, cols(c)]
                b_r, b_z, b_ni, b_nh, b_diag = GRU_BANK[n][c]
                if n == 0:
                    at(pe, "gru_in", 96)
                    at(pe, "eb_set", C)
                    at(pe, "ns_set", C)
                    at(pe, "x_edge", c)
                else:
                    at(pe, "node_in", 32)
                    at(pe, "es_set", c + 1)
                    if c == 0:
                        at(pe, "eb_set", C * K)
                        at(pe, "x_edge", C)
                    if c == 1:
                        at(pe, "tr_set", 3 * K * T)
                    if c == 2:
                        at(pe, "x3_ready", 1)
                        at(pe, "gru_a", C + 2)
                hz = zT[:, cols(c)]
                for b, i in ((b_r, 0), (b_z, 1)):
                    nc.tensor.matmul(b[:, 0:w], gruw[:, 0, i * P:(i + 1) * P], src, start=True, stop=False)
                    nc.tensor.matmul(b[:, 0:w], gruw[:, 1, i * P:(i + 1) * P], hz, start=False, stop=True)
                nc.tensor.matmul(b_ni[:, 0:w], gruw[:, 0, 2 * P:3 * P], src, start=True, stop=True).then_inc(s["gru_ps"], 1)
                if b_nh is not b_r:
                    new_product(n, c)
                if n == 0:
                    diagonal(n, c)

            def mid(n, c):
                at(pe, "gru_t", 2 * (n * C + c + 1))
                if GRU_BANK[n][c][3] is GRU_BANK[n][c][0]:
                    new_product(n, c)
                if n:
                    diagonal(n, c)
                if (n, c) == (1, 0):
                    side_free[0] = ("x3_ready", 1)

            def gat_side(task):
                if task[0] == "gates":
                    gates(*task[1:])
                elif task[0] == "mid":
                    mid(*task[1:])
                else:
                    side(task)

            at(pe, "dcol_set", T)
            for n in range(C):
                score_row(n)
            negative_rows(0)
            pe.wait_ge(s["spad_set"], 3)
            for g in range(K * T + 3):
                k, t = divmod(g, T)
                if 1 <= k < K and t == 0:
                    score_row(C * k + 2)
                    negative_rows(k)
                for kk, c, j in SUMS[g]:
                    r, w = rows(j), width(c)
                    if j == 0:
                        at(pe, "tr_set", 3 * (kk * T + tiles(c)[-1] + 1))
                        at(pe, "x_edge", C)
                    mm = nc.tensor.matmul(B_ACC[c][:, 0:w], hW[0:r, j, kk * P:(kk + 1) * P], qT[0:r, (kk * C + c) % 2, j, 0:w],
                                          start=(kk == 0 and j == 0), stop=(kk == K - 1 and j == T - 1))
                    if j == T - 1:
                        mm.then_inc(s["gat_mm"], 1)
                if 1 <= g <= K * T:
                    h = g - 1
                    r = rows(h % T)
                    at(pe, "q_set", h + 1)
                    for v in range(3):
                        at(pe, "tr_set", 3 * (h - 1) + v + 1)
                        for i in range(min(4, T - 4 * v)):
                            j = 4 * v + i
                            mm = nc.tensor.transpose(B_H[v][:, i * P:i * P + r], S[h % 3][0:r, j * P:(j + 1) * P], ident[0:r, 0:r])
                        mm.then_inc(s["tr_ps"], 1)
                if k < K - 1 and t == T - 2:
                    score_row(C * (k + 1))
                    score_row(C * (k + 1) + 1)
                for task in at_step(g):
                    gat_side(task)
            for task in AFTER:
                if task == ("mean", 3, 0):
                    pe.wait_ge(s["rw_in"], 16)
                gat_side(task)
            pe.wait_ge(s["w2_in"], 16 * M1)

            def down1(q):
                c, e, m = q // (E * M1), q // M1 % E, q % M1
                r, w = min(P, H1 - m * P), width(c)
                first = e == 0 and m == 0
                if first:
                    at(pe, "x4_ready", c)
                at(pe, "m_set", q + 1)
                nc.tensor.matmul(B_Y1[:, 0:w], w2s[0:r, e, m, :], m1_ring[0:r, q % RING1, 0:w], start=first,
                                 stop=(e == E - 1 and m == M1 - 1)).then_inc(s["y1_mm"], 1)

            for q in range(TILES1):
                c, e, m = q // (E * M1), q // M1 % E, q % M1
                r, w = min(P, H1 - m * P), width(c)
                if m == 0:
                    at(pe, "gt_set", C + c + 1)
                    at(pe, "s_gated", (q // M1 - 1) * M1)
                    nc.tensor.matmul(B_GATE[q // M1 % 2][:, 0:w], sel16[:, e:e + 1].to_broadcast([16, P]), GT1[:, c, 0:w],
                                     start=True, stop=True).then_inc(s["gate1_ps"], 1)
                    if c == 0:
                        at(pe, "w13_lo", e + 1)
                    if e == 0:
                        at(pe, "z_split", C + c + 1)
                at(pe, "s_silu", q - 1)
                x = (z3hi[:, cols(c)], z3lo[:, cols(c)])
                f = slice(m * P, m * P + r)
                exact(B_H1[q % 2][0:r, 0:w], (w13hi[:, e, 0, f], w13lo[:, e, 0, f]), x, True, True).then_inc(s["h1_ps"], 1)
                at(pe, "m_set", q - 1)
                exact(B_H3[q % 2][0:r, 0:w], (w13hi[:, e, 1, f], w13lo[:, e, 1, f]), x, True, True).then_inc(s["h3_ps"], 1)
                if q >= LAG1:
                    down1(q - LAG1)
                for task in BESIDE1.get(q, []):
                    side(task)
            for q in range(TILES1 - LAG1, TILES1):
                down1(q)

        @block.vector
        def _(dve):
            def ln_center(l, c):
                n, w = LN_AT[l, c], width(c)
                at(dve, "ln_mean", n + 1)
                at(dve, "ln_z", n - 1)
                nc.vector.tensor_tensor(xc_ring[:, n % 2, 0:w], xT[:, cols(c)], ln_bank(l, c)[:, 0:w], ALU.subtract).then_inc(s["ln_xc"], 1)

            def ln_scale(l, c):
                n, w = LN_AT[l, c], width(c)
                y, t = y_ring[:, n % 2, 0:w], v_ring[:, n % 2, 0:w]
                at(dve, "ln_y0", n + 1)
                nc.vector.tensor_tensor(t, y, y, ALU.mult).then_inc(s["ln_step"], 1)
                at(dve, "ln_step", 4 * n + 1)
                nc.vector.scalar_tensor_tensor(out=t, in0=ln_bank(l, c)[:, 0:w], scalar=1.0e-5, in1=t, op0=ALU.add,
                                               op1=ALU.mult).then_inc(s["ln_step"], 1)
                at(dve, "ln_step", 4 * n + 2)
                nc.vector.tensor_scalar(t, t, -0.5, 1.5, ALU.mult, ALU.add).then_inc(s["ln_step"], 1)
                at(dve, "ln_step", 4 * n + 3)
                nc.vector.tensor_tensor(t, t, y, ALU.mult).then_inc(s["ln_step"], 1)
                at(dve, "ln_step", 4 * n + 4)
                if l == 1:
                    at(dve, "msg_ps", C)
                nc.vector.tensor_tensor(zT[:, cols(c)], xc_ring[:, n % 2, 0:w], t, ALU.mult).then_inc(s["ln_z"], 1)
                if l in (1, 3):
                    hi, lo = (zhi[:, c % 2, 0:w], zlo[:, c % 2, 0:w]) if l == 1 else (z3hi[:, cols(c)], z3lo[:, cols(c)])
                    k = c + (C if l == 3 else 0)
                    if l == 1:
                        at(dve, "h_ps", (c - 1) * E * M0)
                    at(dve, "ln_z", n + 1)
                    nc.vector.tensor_copy(hi, zT[:, cols(c)]).then_inc(s["z_hi"], 1)
                    at(dve, "z_hi", k + 1)
                    nc.vector.tensor_tensor(lo, zT[:, cols(c)], hi.bitcast(F32), ALU.subtract).then_inc(s["z_split"], 1)

            def newton(p, between):
                if p >= PIECES:
                    for step in between:
                        step()
                    return
                c, j = divmod(p, T)
                r, w = rows(j), width(c)
                x, y, t = adjT[0:r, j, cols(c)], a_ring[0:r, p % RINGS, 0:w], t_ring[0:r, p % RINGS, 0:w]
                at(dve, "y0_set", p + 1)
                nc.vector.scalar_tensor_tensor(out=y.bitcast(I32), in0=x.bitcast(I32), scalar=SIGN, in1=y.bitcast(I32),
                                               op0=ALU.bitwise_and, op1=ALU.bitwise_or).then_inc(s["y0_sign"], 1)
                between[0]()
                at(dve, "y0_sign", p + 1)
                at(dve, "w_ready", p - RINGS + 1)
                nc.vector.tensor_tensor(t, x, y, ALU.mult).then_inc(s["newton_t"], 1)
                between[1]()
                at(dve, "newton_t", p + 1)
                nc.vector.scalar_tensor_tensor(out=t, in0=t, scalar=2.0, in1=y, op0=ALU.subtract, op1=ALU.mult
                                               ).then_inc(s["newton_y"], 1)

            def nothing():
                pass

            def cutoff(p):
                c, j = divmod(p, T)
                r, w = rows(j), width(c)
                at(dve, "sens_exp", p + 1)
                at(dve, "gnn_mm", p - RINGW + 1)
                nc.vector.scalar_tensor_tensor(out=w_ring[0:r, p % RINGW, 0:w], in0=adjT[0:r, j, cols(c)], scalar=1.0,
                                               in1=t_ring[0:r, p % RINGS, 0:w], op0=ALU.is_lt, op1=ALU.mult).then_inc(s["w_ready"], 1)

            step = [0]

            def link(ins):
                step[0] += 1
                ins.then_inc(s["route_step"], 1)
                dve.wait_ge(s["route_step"], step[0])

            def x1(c):
                at(dve, "gnn_mm", T * (c + 1))
                nc.vector.tensor_tensor(xT[:, cols(c)], xT[:, cols(c)], B_GNN[:, 0:width(c)], ALU.add).then_inc(s["x1_ready"], 1)

            def route(n):
                l, c = divmod(n, C)
                k = len(tiles(c))
                L, D, X, G = (rt[:, i, 0:k * E].rearrange("p (t e) -> p t e", t=k) for i in (2, 0, 1, 3))
                m1, m2 = rs[:, 0, 0:k], rs[:, 1, 0:k]
                at(dve, "logits_ps", n + 1)
                nc.vector.tensor_copy(L, B_SIDE[:, 0:k * E].rearrange("p (t e) -> p t e", t=k)).then_inc(s["logits_read"], 1)
                at(dve, "logits_read", n + 1)
                link(nc.vector.tensor_reduce(m1, L, AX.X, ALU.max))
                at(dve, "route_e", n)
                nc.vector.tensor_tensor(D, L, m1.unsqueeze(2).to_broadcast([P, k, E]), ALU.subtract).then_inc(s["route_d"], 1)
                if l:
                    at(dve, "route_e", n + 1)
                    link(nc.vector.tensor_reduce(m1, X, AX.X, ALU.add))
                    link(nc.vector.reciprocal(m2, m1))
                    link(nc.vector.tensor_tensor(L, X, m2.unsqueeze(2).to_broadcast([P, k, E]), ALU.mult))
                g4 = [rank[:, i, 0:k * E * E].rearrange("p (t e f) -> p t e f", t=k, e=E) for i in range(2)]
                other = L.unsqueeze(2).to_broadcast([P, k, E, E])
                own = L.unsqueeze(3).to_broadcast([P, k, E, E])
                link(nc.vector.tensor_tensor(g4[0], other, own, ALU.is_gt))
                link(nc.vector.tensor_tensor(g4[1], other, own, ALU.is_ge))
                link(nc.vector.tensor_tensor(g4[1], g4[1], tri[:, :, :].unsqueeze(1).to_broadcast([P, k, E, E]), ALU.mult))
                link(nc.vector.tensor_tensor(g4[0], g4[0], g4[1], ALU.max))
                link(nc.vector.tensor_reduce(G, g4[0], AX.X, ALU.add))
                if l:
                    link(nc.vector.scalar_tensor_tensor(out=G, in0=G, scalar=2.0, in1=L, op0=ALU.is_lt, op1=ALU.mult))
                    link(nc.vector.tensor_reduce(m1, G, AX.X, ALU.add))
                    link(nc.vector.tensor_scalar(m1, m1, 1.0e-9, None, ALU.add))
                else:
                    at(dve, "route_e", n + 1)
                    link(nc.vector.scalar_tensor_tensor(out=G, in0=G, scalar=2.0, in1=X, op0=ALU.is_lt, op1=ALU.mult))
                    link(nc.vector.tensor_reduce(m1, G, AX.X, ALU.add))
                link(nc.vector.reciprocal(m2, m1))
                link(nc.vector.tensor_tensor(G, G, m2.unsqueeze(2).to_broadcast([P, k, E]), ALU.mult))
                at(dve, "gt_ps", n)
                link(nc.vector.tensor_copy(g16[:, 0:k, 0:E], G))
                nc.vector.tensor_tensor(g16[:, 0:k, E:2 * E], G, g16[:, 0:k, 0:E].bitcast(F32), ALU.subtract).then_inc(s["gates_set"], 1)

            def turned(n):
                l, c = divmod(n, C)
                k = len(tiles(c))
                at(dve, "gt_ps", n + 1)
                gt = GT1[:, c, 0:k * P] if l else GT0[:, c % 2, 0:k * P]
                if l == 0:
                    at(dve, "gate_ps", (c - 1) * E)
                nc.vector.tensor_copy(gt, B_SIDE[0:16, 0:k * P]).then_inc(s["gt_set"], 1)

            usw = [u18[:, :, sg, :].rearrange("p t (r j) -> p t r j", r=PARTS) for sg in range(2)]

            def split_u(c):
                a, b = c * 4, c * 4 + len(tiles(c))
                at(dve, "hw_set", 2 * b)
                for part in range(PARTS):
                    src = (u if part == 0 else ur)[:, a:b, :]
                    link(nc.vector.tensor_copy(usw[0][:, a:b, part, :], src))
                    if part + 1 < PARTS:
                        link(nc.vector.tensor_tensor(ur[:, a:b, :], src, usw[0][:, a:b, part, :], ALU.subtract))
                for half in range(2):
                    nc.vector.tensor_copy(usw[1][:, a:b, :, half * K:(half + 1) * K],
                                          usw[0][:, a:b, :, (1 - half) * K:(2 - half) * K]).then_inc(s["u18_set"], 1)

            def positive(j):
                r = rows(j)
                at(dve, "mask_used", j - 1)
                at(dve, "offdiag_set", j + 1)
                if j == 0:
                    at(dve, "gnn_mm", PIECES)
                nc.vector.tensor_scalar(masks[0:r, j % 2, :], adjT[0:r, j, :], 0.0, None, ALU.is_gt).then_inc(s["mask_set"], 1)

            def side(task, between=nothing):
                kind = task[0]
                if kind == "sens":
                    newton(task[1] + 2, (between, lambda: cutoff(task[1])))
                elif kind == "x1":
                    x1(task[1])
                elif kind == "center":
                    ln_center(*task[1:])
                elif kind == "scale":
                    ln_scale(*task[1:])
                elif kind == "rank":
                    route(task[1])
                elif kind == "turn":
                    turned(task[1])
                elif kind == "split":
                    split_u(task[1])
                elif kind == "mask":
                    positive(task[1])

            dve.wait_ge(s["x_in"], 16)
            ln_center(0, 0)
            ln_center(0, 1)
            dve.wait_ge(s["const_set"], CONSTS)
            nc.vector.tensor_copy(sel16[:, :], sel16f[:, :]).then_inc(s["sel16_set"], 1)
            ln_scale(0, 0)
            ln_center(0, 2)
            ln_scale(0, 1)
            newton(0, (nothing, nothing))
            ln_scale(0, 2)
            newton(1, (nothing, nothing))
            dve.wait_ge(s["wts0_in"], 64)
            nc.vector.tensor_tensor(rowW[0:1, P:P + E], rowW[0:1, P:P + E], rowW[0:1, P + E:P + 2 * E],
                                    ALU.add).then_inc(s["bgs_set"], 1)
            for p in range(T):
                side(("sens", p))
                if p == 3:
                    dve.wait_ge(s["W1_in"], 16)
                    nc.vector.tensor_copy(W1hi[:, :, :], W1f[:, :, :]).then_inc(s["W1_split"], 1)
                if p == 5:
                    at(dve, "W1_split", 1)
                    nc.vector.tensor_tensor(W1lo[:, :, :], W1f[:, :, :], W1hi[:, :, :].bitcast(F32), ALU.subtract).then_inc(s["W1_split"], 1)
                if p == 7:
                    dve.wait_ge(s["ffn0_in"], 80)
                    nc.vector.tensor_copy(b2hi[:, :], b2x[:, :]).then_inc(s["b2_split"], 1)
                    at(dve, "b2_split", 1)
                    nc.vector.tensor_tensor(b2lo[:, :], b2x[:, :], b2hi[:, :].bitcast(F32), ALU.subtract).then_inc(s["b2_split"], 1)
                if p == 8:
                    dve.wait_ge(s["v_ps"], 1)
                    nc.vector.tensor_copy(wcat[:, 3 * P:3 * P + 6].rearrange("p (h k) -> p k h", h=2),
                                          B_SIDE[:, 0:6].rearrange("p (k h) -> p k h", h=2)).then_inc(s["v_set"], 1)
            x1(0)
            side(("center", 1, 0))
            side(("sens", T))
            side(("scale", 1, 0))
            side(("sens", T + 1))
            side(("rank", 0))
            side(("sens", T + 2))
            side(("turn", 0))

            def x2(c):
                at(dve, "y_mm", (c + 1) * E * M0)
                nc.vector.tensor_tensor(xT[:, cols(c)], xT[:, cols(c)], B_Y0[:, 0:width(c)], ALU.add).then_inc(s["x2_ready"], 1)

            for q in range(TILES0):
                c, e, m = q // (E * M0), q // M0 % E, q % M0
                w = width(c)

                def gated():
                    at(dve, "gate_ps", q // M0 + 1)
                    at(dve, "h_relu", q + 1)
                    hr = hr_ring[:, q % RING0, 0:w]
                    nc.vector.tensor_tensor(hr, hr, B_GATE[q // M0 % 2][:, 0:w], ALU.mult).then_inc(s["h_gated"], 1)

                tasks = beside(c, q % (E * M0))
                if tasks and tasks[0][0] == "sens":
                    side(tasks[0], gated)
                    tasks = tasks[1:]
                else:
                    gated()
                if c and q % (E * M0) == 0:
                    x2(c - 1)
                for task in tasks:
                    side(task)
            x2(C - 1)

            side(("center", 2, C - 1))
            def row_diagonal(t):
                r = rows(t)
                at(dve, f"adjR_in{t // 4}", 16 * len(tiles(t // 4)))
                at(dve, "dcol_set", t)
                nc.vector.tensor_tensor_reduce(rank[0:r, 0, 0:r], adjR[0:r, t, t * P:t * P + r], ident[0:r, 0:r], 1.0, 0.0,
                                               ALU.mult, ALU.add, dcol[0:r, t:t + 1]).then_inc(s["dcol_set"], 1)

            def edge_mask(t):
                r = rows(t)
                at(dve, "row_diag_set", t + 1)
                at(dve, "neg_acc", t + 1)
                nc.vector.tensor_scalar(mb[0:r, t, :], adjR[0:r, t, :], 0.0, NONE, ALU.is_le, ALU.mult).then_inc(s["mb_set"], 1)

            side(("scale", 2, C - 1))
            for j in range(2, T):
                positive(j)
                if j == 3 + len(tiles(C - 1)):
                    split_u(C - 1)
                for t in (2 * j - 10, 2 * j - 9):
                    if 0 <= t < T:
                        row_diagonal(t)
                for t in (2 * j - 14, 2 * j - 13):
                    if 0 <= t < T:
                        edge_mask(t)
            dve.wait_ge(s["gru_in"], 96)
            for n in range(2):
                link(nc.vector.tensor_tensor(gru_c[:, n, 0:2], gru_b[:, n, 0, 0:2], gru_b[:, n, 1, 0:2], ALU.add))
                link(nc.vector.tensor_scalar(gru_c[:, n, 0:2], gru_c[:, n, 0:2], 0.5, None, ALU.mult))
                link(nc.vector.tensor_copy(gru_c[:, n, 2:3], gru_b[:, n, 0, 2:3]))
                nc.vector.tensor_copy(gru_c[:, n, 3:4], gru_b[:, n, 1, 2:3]).then_inc(s["gru_bias"], 1)
            at(dve, "neg_acc", T)
            link(nc.vector.memset(negtot[:, :], 0.0))
            link(nc.vector.tensor_reduce(negtot[:, :], negsum[:, 0:T - 1], AX.X, ALU.max))
            nc.vector.tensor_tensor(negtot[0:rows(T - 1), :], negtot[0:rows(T - 1), :], negsum[0:rows(T - 1), T - 1:T],
                                    ALU.max).then_inc(s["neg_max"], 1)
            for c in range(C):
                at(dve, "mask_used", T)
                nc.vector.tensor_copy(e18[:, cols(c)], B_E18[c][0:18, 0:width(c)]).then_inc(s["e18_set"], 1)
            at(dve, "neg_ps", 1)
            nc.vector.tensor_scalar(flag[0:1, 0:1], B_SIDE[0:1, 0:1], 0.0, None, ALU.is_gt).then_inc(s["flag_set"], 1)
            at(dve, "flag_set", 1)
            any_negative = dve.value_load(flag[0:1, 0:1], min_val=0, max_val=1)
            with dve.If(any_negative == 1):
                for j in range(T):
                    r = rows(j)
                    at(dve, "nmask_used", j - 1)
                    nc.vector.tensor_scalar(masks[0:r, j % 2, :], adjT[0:r, j, :], 0.0, None, ALU.is_lt).then_inc(s["nmask_set"], 1)
                for c in range(C):
                    at(dve, "nmask_used", T)
                    at(dve, "e18_set", C)
                    nc.vector.tensor_tensor(e18[:, cols(c)], e18[:, cols(c)], B_E18[c][0:18, 0:width(c)], ALU.add).then_inc(s["ne18_set"], 1)

            for c in range(C):
                at(dve, "e6_fifth", c + 1)
                nc.vector.scalar_tensor_tensor(out=e6[:, cols(c)], in0=B_E18[c][0:6, 0:width(c)], scalar=-1.0, in1=e6[:, cols(c)],
                                               op0=ALU.mult, op1=ALU.min).then_inc(s["e6_set"], 1)
            for t in range(2 * (T - 1) - 12, T):
                edge_mask(t)

            def mid(n, c):
                g, w = n * C + c, width(c)
                tr, tz, a, _ = (x[:, 0:w] for x in GRU_BUF[n][c])
                _, _, b_ni, b_nh, _ = GRU_BANK[n][c]
                at(dve, "gru_t", 2 * (g + 1))
                link(nc.vector.tensor_scalar(tr, tr, 0.5, 0.5, ALU.mult, ALU.add))
                at(dve, "gru_nh", g + 1)
                link(nc.vector.scalar_tensor_tensor(out=a, in0=b_nh[:, 0:w], scalar=gru_c[:, n, 3:4], in1=tr, op0=ALU.add, op1=ALU.mult))
                nc.vector.tensor_tensor(a, a, b_ni[:, 0:w], ALU.add).then_inc(s["gru_a"], 1)
                link(nc.vector.tensor_scalar(tz, tz, 0.5, 0.5, ALU.mult, ALU.add))

            def finish(n, c):
                g, w = n * C + c, width(c)
                _, tz, a, d = (x[:, 0:w] for x in GRU_BUF[n][c])
                at(dve, "gru_n", g + 1)
                link(nc.vector.tensor_tensor(d, zT[:, cols(c)], a, ALU.subtract))
                link(nc.vector.tensor_tensor(d, d, tz, ALU.mult))
                link(nc.vector.tensor_tensor(d, d, a, ALU.add))
                at(dve, "diag_ps", g + 1)
                link(nc.vector.tensor_tensor(d, d, GRU_BANK[n][c][4][:, 0:w], ALU.mult))
                nc.vector.tensor_tensor(xT[:, cols(c)], xT[:, cols(c)], d, ALU.add).then_inc(s["x3_ready" if n else "x_edge"], 1)

            def gat_side(task):
                if task[0] == "mid":
                    mid(*task[1:])
                elif task[0] == "finish":
                    finish(*task[1:])
                else:
                    side(task)

            def scores(g):
                t = g % T
                r = rows(t)
                row, low = S[g % 3][0:r, 0:N], lowest[0:r, g:g + 1]
                at(dve, "tr_ps", 3 * (g - 2))
                at(dve, "mb_set", t + 1)
                nc.vector.tensor_tensor_reduce(row, eplus[0:r, :], mb[0:r, t, :], 1.0, 3.0e38,
                                               ALU.add, ALU.min, low).then_inc(s["neg_step"], 1)
                at(dve, "neg_step", g + 1)
                with dve.If(any_negative == 1):
                    n = 8 * g
                    for i in range(2):
                        part = slice(i * HALF, (i + 1) * HALF)
                        for j, ins in enumerate([
                            lambda: nc.vector.tensor_scalar(neg_mask[0:r, 0:HALF], adjR[0:r, t, part], 0.0, NONE, ALU.is_ge, ALU.mult),
                            lambda: nc.vector.tensor_tensor_reduce(neg_row[0:r, :], eminus[0:r, part], neg_mask[0:r, 0:HALF], 1.0, 3.0e38,
                                                                   ALU.add, ALU.min, low2[0:r, i:i + 1]),
                            lambda: nc.vector.tensor_tensor(row[:, part], row[:, part], neg_row[0:r, :], ALU.min),
                            lambda: nc.vector.tensor_tensor(low, low, low2[0:r, i:i + 1], ALU.min),
                        ]):
                            ins().then_inc(s["u_step"], 1)
                            n += 1
                            at(dve, "u_step", n)
                dve.sem_inc(s["s_set"], 1)

            def attend(g):
                t = g % T
                r = rows(t)
                at(dve, "p_set", g + 1)
                nc.vector.reciprocal(rden[0:r, g:g + 1], den[0:r, g:g + 1]).then_inc(s["rden_set"], 1)
                at(dve, "rden_set", g + 1)
                row = S[g % 3][0:r, 0:N]
                nc.vector.scalar_tensor_tensor(out=row, in0=row, scalar=rden[0:r, g:g + 1], in1=adjR[0:r, t, :],
                                               op0=ALU.mult, op1=ALU.mult).then_inc(s["q_set"], 1)

            done = 0

            def split_lo():
                at(dve, "w13_hi", done + 1)
                at(dve, "q_set", (K - 1) * T + lo_tiles(done))
                nc.vector.tensor_tensor(w13lo[:, done, :, :], w13[:, done, :, :], w13hi[:, done, :, :].bitcast(F32),
                                        ALU.subtract).then_inc(s["w13_lo"], 1)

            for g in range(K * T + 2):
                if g < K * T:
                    if g % T == 0:
                        at(dve, "eb_set", C * (g // T + 1))
                        with dve.If(any_negative == 1):
                            at(dve, "nb_set", C * (g // T + 1))
                    scores(g)
                if 1 <= g <= K * T:
                    attend(g - 1)
                for task in at_step(g):
                    gat_side(task)
                while done < E and g >= (K - 1) * T + max(mask_tiles(done) + 3, lo_tiles(done) + 1):
                    split_lo()
                    done += 1
            for task in AFTER:
                gat_side(task)
                if done < E:
                    split_lo()
                    done += 1
            for q in range(TILES1):
                c, e, m = q // (E * M1), q // M1 % E, q % M1
                r, w = min(P, H1 - m * P), width(c)
                sg = s1_ring[0:r, q % 4, 0:w]
                at(dve, "gate1_ps", q // M1 + 1)
                at(dve, "s_silu", q + 1)
                nc.vector.tensor_tensor(sg, sg, B_GATE[q // M1 % 2][0:r, 0:w], ALU.mult).then_inc(s["s_gated"], 1)
                at(dve, "s_gated", q + 1)
                at(dve, "h3_ps", q + 1)
                at(dve, "y1_mm", q - RING1 + 1)
                nc.vector.tensor_tensor(m1_ring[0:r, q % RING1, 0:w], sg, B_H3[q % 2][0:r, 0:w], ALU.mult).then_inc(s["m_set"], 1)
                for task in BESIDE1.get(q, []):
                    side(task)
                if c and q % (E * M1) == LAG1 - 1:
                    at(dve, "y1_mm", c * E * M1)
                    nc.vector.tensor_tensor(xT[:, cols(c - 1)], xT[:, cols(c - 1)], B_Y1[:, 0:width(c - 1)], ALU.add).then_inc(s["x4_ready"], 1)
            at(dve, "y1_mm", TILES1)
            nc.vector.tensor_tensor(xT[:, cols(C - 1)], xT[:, cols(C - 1)], B_Y1[:, 0:width(C - 1)], ALU.add).then_inc(s["x4_ready"], 1)


def kernel(**inputs):
    import numpy as _np
    import concourse.bacc as _bacc
    from concourse import mybir as _mybir
    from concourse.bass_utils import run_bass_kernel_spmd as _run

    g = {k: _np.asarray(v) for k, v in inputs.items()}

    def cols3(b):
        return b.reshape(3, 128).transpose(1, 0)

    laid = {
        "xT": g["x"].transpose(1, 0),
        "adjT": g["adj"].transpose(1, 0),
        "adj": g["adj"],
        "W": g["L0_gnn_W"],
        "B": g["L0_gnn_B"].reshape(1, -1),
        "Wg": g["L0_ffn_Wg"],
        "bg": g["L0_ffn_bg"].reshape(1, -1),
        "bias": g["L0_ffn_bias"].reshape(1, -1),
        "W1": g["L0_ffn_W1"],
        "b1": g["L0_ffn_b1"].reshape(16, 128).transpose(1, 0),
        "W2": g["L0_ffn_W2"],
        "b2": g["L0_ffn_b2"],
        "gW": g["L1_gnn_gat_W"],
        "gWT": g["L1_gnn_gat_W"].transpose(2, 0, 1),
        "ga": g["L1_gnn_gat_a"].reshape(6, 128).transpose(1, 0),
        "eWih": g["L1_gnn_edge_Wih"].transpose(1, 0),
        "eWhh": g["L1_gnn_edge_Whh"].transpose(1, 0),
        "ebih": cols3(g["L1_gnn_edge_bih"]),
        "ebhh": cols3(g["L1_gnn_edge_bhh"]),
        "nWih": g["L1_gnn_node_Wih"].transpose(1, 0),
        "nWhh": g["L1_gnn_node_Whh"].transpose(1, 0),
        "nbih": cols3(g["L1_gnn_node_bih"]),
        "nbhh": cols3(g["L1_gnn_node_bhh"]),
        "rw": g["L1_ffn_router_w"].transpose(1, 0),
        "w1": g["L1_ffn_w1"].transpose(2, 0, 1),
        "w3": g["L1_ffn_w3"].transpose(2, 0, 1),
        "w2": g["L1_ffn_w2"].transpose(2, 0, 1),
    }
    nc = _bacc.Bacc("TRN2", target_bir_lowering=False, num_devices=1)
    arrays, args = {}, []
    for name, a in laid.items():
        a = _np.ascontiguousarray(a)
        arrays[f"in_{name}"] = a
        args.append(nc.dram_tensor(f"in_{name}", a.shape, _mybir.dt.from_np(a.dtype), kind="ExternalInput").ap())
    args.append(nc.dram_tensor("outT", (128, 1354), _mybir.dt.float32, kind="ExternalOutput").ap())
    build(nc, *args)
    r = _run(nc, [arrays], core_ids=[0])
    return _np.ascontiguousarray(r.results[0]["outT"].transpose(1, 0))
```
